# Optimizing a Trainium2 kernel written in Bass

```python
import numpy as np
import jax
import jax.numpy as jnp

def _softmax(x, axis=-1):
    return jax.nn.softmax(x, axis=axis)
def _gelu(x):
    return jax.nn.gelu(x, approximate=True)
def _silu(x):
    return jax.nn.silu(x)
def _sigmoid(x):
    return jax.nn.sigmoid(x)
def _layernorm(x, axis=-1, eps=1e-5):
    m = jnp.mean(x, axis=axis, keepdims=True)
    v = jnp.var(x, axis=axis, keepdims=True)
    return (x - m) / jnp.sqrt(v + eps)
def _scatter_add(tgt, idx, src, axis=0):
    return tgt.at[idx].add(src)
def _segment_sum(src, seg, n):
    return jax.ops.segment_sum(src, seg, n)

kernel_name = 'mk_conv_attn_hybrid_d2_conv_nchw128_1d9f73'

def setup_inputs(seed: int = 0):
    np.random.seed(seed)
    _w = jnp.asarray
    def _rec_inputs():
        import jax
        import jax.numpy as jnp
        _gk = jax.random.key(seed)
        x = -0.0005207 + 1.001 * jax.random.normal(jax.random.fold_in(_gk, 1), (4, 128, 64, 64), jnp.float32)
        return x
    x = _rec_inputs()
    def _L0_conv_setup():
        import jax, jax.numpy as jnp
        import numpy as np
        B, C, H, W = (4, 128, 64, 64)
        D_STATE, D_CONV, EXPAND = (16, 4, 2)
        D_INNER = EXPAND * C
        DT_RANK = (C + 15) // 16
        PS = 4
        L = H * W

        def _gelu(x):
            return jax.nn.gelu(x, approximate=False)

        def _dwconv2d(x, w, b):
            y = jax.lax.conv_general_dilated(x, w, (1, 1), 'SAME', dimension_numbers=('NCHW', 'OIHW', 'NCHW'), feature_group_count=x.shape[1])
            return y + b[None, :, None, None]
        key = jax.random.key(seed)
        k = jax.random.split(key, 16)
        n = lambda i, s, sc=0.02: jax.random.normal(k[i], s, jnp.float32) * sc
        A_log = jnp.log(jnp.broadcast_to(jnp.arange(1, D_STATE + 1, dtype=jnp.float32), (D_INNER, D_STATE)))
        return {'x': jax.random.normal(k[0], (B, C, H, W), jnp.float32), 'pe': n(1, (L, C), 0.02), 'norm_g': jnp.ones(C), 'norm_b': jnp.zeros(C), 'conv1_w': n(2, (C, 1, 3, 3), 0.1), 'conv1_b': jnp.zeros(C), 'ca1_w': n(3, (C // 4, C), 0.1), 'ca2_w': n(4, (C, C // 4), 0.1), 'conv2_w': n(5, (C, 1, 3, 3), 0.1), 'conv2_b': jnp.zeros(C), 'head_w': n(6, (1, C), 0.1), 'head_b': jnp.zeros(1), 'in_proj_w': n(7, (2 * D_INNER, C)), 'conv1d_w': n(8, (D_INNER, D_CONV), 0.2), 'conv1d_b': jnp.zeros(D_INNER), 'x_proj_w': n(9, (DT_RANK + 2 * D_STATE, D_INNER)), 'dt_proj_w': n(10, (D_INNER, DT_RANK), 0.5), 'dt_proj_b': jnp.full((D_INNER,), -4.6), 'A_log': A_log, 'D': jnp.ones(D_INNER), 'out_proj_w': n(11, (C, D_INNER))}
    _L0_conv_all = _L0_conv_setup()
    _L0_conv_in = {k: v for k, v in _L0_conv_all.items() if k in ('pe', 'norm_g', 'norm_b', 'conv1_w', 'conv1_b', 'ca1_w', 'ca2_w', 'conv2_w', 'conv2_b', 'head_w', 'head_b', 'in_proj_w', 'conv1d_w', 'conv1d_b', 'x_proj_w', 'dt_proj_w', 'dt_proj_b', 'A_log', 'D', 'out_proj_w', )}
    del _L0_conv_all

    def _L1_attn_setup():
        import jax, jax.numpy as jnp
        import numpy as np
        HEADS = 4
        DIM_HEAD = 32
        SCALE = 10.0
        EPS = 1e-12

        def l2norm_axis1(t):
            denom = jnp.clip(jnp.linalg.norm(t, ord=2, axis=1, keepdims=True), EPS)
            return t / denom
        key = jax.random.key(seed)
        k1, k2, k3 = jax.random.split(key, 3)
        B, N, C = (4, 4096, 128)
        dim = HEADS * DIM_HEAD
        x = jax.random.normal(k1, (B, N, C), dtype=jnp.float32)
        W_qkv = jax.random.normal(k2, (C, 3 * dim), dtype=jnp.float32) * (1.0 / np.sqrt(C))
        W_out = jax.random.normal(k3, (dim, C), dtype=jnp.float32) * (1.0 / np.sqrt(dim))
        b_out = jnp.zeros((C,), dtype=jnp.float32)
        return {'x': x, 'W_qkv': W_qkv, 'W_out': W_out, 'b_out': b_out}
    _L1_attn_all = _L1_attn_setup()
    _L1_attn_in = {k: v for k, v in _L1_attn_all.items() if k in ('W_qkv', 'W_out', 'b_out', )}
    del _L1_attn_all

    def _L1_ffn_setup():
        import jax, jax.numpy as jnp
        import numpy as np
        B, N, D, C, E, K = (8, 8192, 128, 128, 8, 2)
        key = jax.random.key(seed)
        k0, k1, k2 = jax.random.split(key, 3)
        x = jax.random.normal(k0, (B, N, D), dtype=jnp.float32)
        router_w = jax.random.normal(k1, (D, E), dtype=jnp.float32) * 0.05
        router_b = jnp.zeros((E,), dtype=jnp.float32)
        expert_w = jax.random.normal(k2, (E, D, C), dtype=jnp.float32) * (1.0 / np.sqrt(D))
        expert_b = jnp.zeros((E, C), dtype=jnp.float32)
        return {'x': x, 'router_w': router_w, 'router_b': router_b, 'expert_w': expert_w, 'expert_b': expert_b}
    _L1_ffn_all = _L1_ffn_setup()
    _L1_ffn_in = {k: v for k, v in _L1_ffn_all.items() if k in ('router_w', 'router_b', 'expert_w', 'expert_b', )}
    del _L1_ffn_all

    return {
        "x": x,
        "L0_conv_pe": _L0_conv_in["pe"],
        "L0_conv_norm_g": _L0_conv_in["norm_g"],
        "L0_conv_norm_b": _L0_conv_in["norm_b"],
        "L0_conv_conv1_w": _L0_conv_in["conv1_w"],
        "L0_conv_conv1_b": _L0_conv_in["conv1_b"],
        "L0_conv_ca1_w": _L0_conv_in["ca1_w"],
        "L0_conv_ca2_w": _L0_conv_in["ca2_w"],
        "L0_conv_conv2_w": _L0_conv_in["conv2_w"],
        "L0_conv_conv2_b": _L0_conv_in["conv2_b"],
        "L0_conv_head_w": _L0_conv_in["head_w"],
        "L0_conv_head_b": _L0_conv_in["head_b"],
        "L0_conv_in_proj_w": _L0_conv_in["in_proj_w"],
        "L0_conv_conv1d_w": _L0_conv_in["conv1d_w"],
        "L0_conv_conv1d_b": _L0_conv_in["conv1d_b"],
        "L0_conv_x_proj_w": _L0_conv_in["x_proj_w"],
        "L0_conv_dt_proj_w": _L0_conv_in["dt_proj_w"],
        "L0_conv_dt_proj_b": _L0_conv_in["dt_proj_b"],
        "L0_conv_A_log": _L0_conv_in["A_log"],
        "L0_conv_D": _L0_conv_in["D"],
        "L0_conv_out_proj_w": _L0_conv_in["out_proj_w"],
        "L1_attn_W_qkv": _L1_attn_in["W_qkv"],
        "L1_attn_W_out": _L1_attn_in["W_out"],
        "L1_attn_b_out": _L1_attn_in["b_out"],
        "L1_ffn_router_w": _L1_ffn_in["router_w"],
        "L1_ffn_router_b": _L1_ffn_in["router_b"],
        "L1_ffn_expert_w": _L1_ffn_in["expert_w"],
        "L1_ffn_expert_b": _L1_ffn_in["expert_b"],
    }

def reference(x, L0_conv_pe, L0_conv_norm_g, L0_conv_norm_b, L0_conv_conv1_w, L0_conv_conv1_b, L0_conv_ca1_w, L0_conv_ca2_w, L0_conv_conv2_w, L0_conv_conv2_b, L0_conv_head_w, L0_conv_head_b, L0_conv_in_proj_w, L0_conv_conv1d_w, L0_conv_conv1d_b, L0_conv_x_proj_w, L0_conv_dt_proj_w, L0_conv_dt_proj_b, L0_conv_A_log, L0_conv_D, L0_conv_out_proj_w, L1_attn_W_qkv, L1_attn_W_out, L1_attn_b_out, L1_ffn_router_w, L1_ffn_router_b, L1_ffn_expert_w, L1_ffn_expert_b):
    import jax
    import jax.numpy as jnp
    def _L0_conv_ref(x, pe, norm_g, norm_b, conv1_w, conv1_b, ca1_w, ca2_w, conv2_w, conv2_b, head_w, head_b, in_proj_w, conv1d_w, conv1d_b, x_proj_w, dt_proj_w, dt_proj_b, A_log, D, out_proj_w):
        import jax, jax.numpy as jnp
        import numpy as np
        B, C, H, W = (4, 128, 64, 64)
        D_STATE, D_CONV, EXPAND = (16, 4, 2)
        D_INNER = EXPAND * C
        DT_RANK = (C + 15) // 16
        PS = 4
        L = H * W

        def _gelu(x):
            return jax.nn.gelu(x, approximate=False)

        def _dwconv2d(x, w, b):
            y = jax.lax.conv_general_dilated(x, w, (1, 1), 'SAME', dimension_numbers=('NCHW', 'OIHW', 'NCHW'), feature_group_count=x.shape[1])
            return y + b[None, :, None, None]
        x_adapted = x
        feat = _gelu(_dwconv2d(x_adapted, conv1_w, conv1_b))
        ca = feat.mean((2, 3))
        ca = jax.nn.sigmoid(jnp.maximum(ca @ ca1_w.T, 0.0) @ ca2_w.T)
        feat = feat * ca[:, :, None, None]
        feat = _gelu(_dwconv2d(feat, conv2_w, conv2_b))
        scores = jax.nn.sigmoid(jnp.einsum('bchw,oc->bohw', feat, head_w)[:, 0] + head_b[0])
        pv = jnp.var(x_adapted, axis=1, ddof=1)
        final_scores = 0.7 * scores + 0.3 * jax.nn.sigmoid(pv * 10.0)
        Hp, Wp = (H // PS, W // PS)
        sm = final_scores.reshape(B, Hp, PS, Wp, PS).mean((2, 4)).reshape(B, Hp * Wp)
        idx = jnp.argsort(-sm, axis=1)
        p_y, p_x = (idx // Wp, idx % Wp)
        offs_y = jnp.repeat(jnp.arange(PS), PS)
        offs_x = jnp.tile(jnp.arange(PS), PS)
        pix_y = p_y[:, :, None] * PS + offs_y[None, None, :]
        pix_x = p_x[:, :, None] * PS + offs_x[None, None, :]
        order = (pix_y * W + pix_x).reshape(B, L)
        pe_re = pe[order]
        x_re = jnp.take_along_axis(x_adapted.reshape(B, C, L), jnp.broadcast_to(order[:, None, :], (B, C, L)), axis=2)
        x1 = x_re.transpose(0, 2, 1) + pe_re
        mu = x1.mean(-1, keepdims=True)
        var = ((x1 - mu) ** 2).mean(-1, keepdims=True)
        x1n = (x1 - mu) * jax.lax.rsqrt(var + 1e-05) * norm_g + norm_b
        xz = x1n @ in_proj_w.T
        xm, z = (xz[..., :D_INNER], xz[..., D_INNER:])
        xp = jnp.pad(xm.transpose(0, 2, 1), ((0, 0), (0, 0), (D_CONV - 1, 0)))
        xc = jax.lax.conv_general_dilated(xp, conv1d_w[:, None, :], (1,), 'VALID', dimension_numbers=('NCH', 'OIH', 'NCH'), feature_group_count=D_INNER)
        xc = jax.nn.silu(xc + conv1d_b[None, :, None]).transpose(0, 2, 1)
        dbc = xc @ x_proj_w.T
        dt_low = dbc[..., :DT_RANK]
        Bc = dbc[..., DT_RANK:DT_RANK + D_STATE]
        Cc = dbc[..., DT_RANK + D_STATE:]
        dt = jax.nn.softplus(dt_low @ dt_proj_w.T + dt_proj_b)
        A = -jnp.exp(A_log)
        dA = jnp.exp(dt[..., None] * A)
        dBx = dt[..., None] * Bc[:, :, None, :] * xc[..., None]

        def step(h, inp):
            dA_t, dBx_t, C_t = inp
            h = dA_t * h + dBx_t
            return (h, jnp.einsum('bds,bs->bd', h, C_t))
        h0 = jnp.zeros((B, D_INNER, D_STATE), xc.dtype)
        _, ys = jax.lax.scan(step, h0, (dA.transpose(1, 0, 2, 3), dBx.transpose(1, 0, 2, 3), Cc.transpose(1, 0, 2)))
        y = ys.transpose(1, 0, 2) + D * xc
        y = y * jax.nn.silu(z)
        out_m = y @ out_proj_w.T
        inv = jnp.argsort(order, axis=1)
        out_flat = jnp.take_along_axis(out_m.transpose(0, 2, 1), jnp.broadcast_to(inv[:, None, :], (B, C, L)), axis=2)
        return out_flat.reshape(B, C, H, W)

    def _L1_attn_ref(x, W_qkv, W_out, b_out):
        import jax, jax.numpy as jnp
        import numpy as np
        HEADS = 4
        DIM_HEAD = 32
        SCALE = 10.0
        EPS = 1e-12

        def l2norm_axis1(t):
            denom = jnp.clip(jnp.linalg.norm(t, ord=2, axis=1, keepdims=True), EPS)
            return t / denom
        B, N, C = x.shape
        qkv = jnp.einsum('bnc,ce->bne', x, W_qkv)
        q, k, v = jnp.split(qkv, 3, axis=-1)
        q = q.reshape(B, N, HEADS, DIM_HEAD)
        k = k.reshape(B, N, HEADS, DIM_HEAD)
        v = v.reshape(B, N, HEADS, DIM_HEAD)
        q = l2norm_axis1(q)
        k = l2norm_axis1(k)
        sim = jnp.einsum('bihd,bjhd->bhij', q, k) * SCALE
        attn = jax.nn.softmax(sim, axis=-1)
        out = jnp.einsum('bhij,bjhd->bhid', attn, v)
        out = out.transpose(0, 2, 1, 3).reshape(B, N, HEADS * DIM_HEAD)
        return jnp.einsum('bne,ec->bnc', out, W_out) + b_out

    def _L1_ffn_ref(x, router_w, router_b, expert_w, expert_b):
        import jax, jax.numpy as jnp
        import numpy as np
        B, N, D, C, E, K = (8, 8192, 128, 128, 8, 2)
        router_probs = jax.nn.softmax(x @ router_w + router_b, axis=-1)
        top_p, top_i = jax.lax.top_k(router_probs, K)
        top_p = top_p / jnp.sum(top_p, axis=-1, keepdims=True)
        expert_out = jnp.einsum('bnd,edc->bnec', x, expert_w) + expert_b
        gathered = jnp.take_along_axis(expert_out, top_i[..., None], axis=2)
        return jnp.einsum('bnk,bnkc->bnc', top_p, gathered)

    def _gn(v, G=32, eps=1e-5):
        B_, C_, H_, W_ = v.shape
        g = v.reshape(B_, G, C_ // G, H_, W_)
        m = jnp.mean(g, axis=(2, 3, 4), keepdims=True)
        s = jnp.var(g, axis=(2, 3, 4), keepdims=True)
        return ((g - m) / jnp.sqrt(s + eps)).reshape(v.shape)

    def _ln_c(v, eps=1e-6):
        m = jnp.mean(v, axis=1, keepdims=True)
        s = jnp.var(v, axis=1, keepdims=True)
        return (v - m) / jnp.sqrt(s + eps)

    def _ln_t(v, eps=1e-5):
        m = jnp.mean(v, axis=-1, keepdims=True)
        s = jnp.var(v, axis=-1, keepdims=True)
        return (v - m) / jnp.sqrt(s + eps)

    def _to_tokens(v):
        B_, C_, H_, W_ = v.shape
        return v.reshape(B_, C_, H_ * W_).transpose(0, 2, 1)
    def _from_tokens(t, like):
        B_, C_, H_, W_ = like.shape
        return t.transpose(0, 2, 1).reshape(B_, C_, H_, W_)

    x = x + _L0_conv_ref(_gn(x), L0_conv_pe, L0_conv_norm_g, L0_conv_norm_b, L0_conv_conv1_w, L0_conv_conv1_b, L0_conv_ca1_w, L0_conv_ca2_w, L0_conv_conv2_w, L0_conv_conv2_b, L0_conv_head_w, L0_conv_head_b, L0_conv_in_proj_w, L0_conv_conv1d_w, L0_conv_conv1d_b, L0_conv_x_proj_w, L0_conv_dt_proj_w, L0_conv_dt_proj_b, L0_conv_A_log, L0_conv_D, L0_conv_out_proj_w)
    t = _to_tokens(x)
    t = t + _L1_attn_ref(_ln_t(t), L1_attn_W_qkv, L1_attn_W_out, L1_attn_b_out)
    t = t + _L1_ffn_ref(_ln_t(t), L1_ffn_router_w, L1_ffn_router_b, L1_ffn_expert_w, L1_ffn_expert_b)
    x = _from_tokens(t, x)
    return x


_drawn_inputs = setup_inputs


def setup_inputs(seed=0):
    import zlib

    import numpy as np

    out = dict(_drawn_inputs(seed))
    spreads = {'L0_conv_norm_g': (1.0, 0.6),
     'L0_conv_norm_b': (0.0, 0.767),
     'L0_conv_conv1_b': (0.0, 0.8),
     'L0_conv_conv2_b': (0.0, 0.705),
     'L0_conv_conv1d_b': (0.0, 0.344),
     'L0_conv_dt_proj_b': (-4.599999904632568, 0.6),
     'L0_conv_D': (1.0, 0.6),
     'L1_attn_b_out': (0.0, 2.0),
     'L1_ffn_router_b': (0.0, 0.8),
     'L1_ffn_expert_b': (0.0, 2.0)}
    factors = {'L0_conv_pe': 8.0,
     'L0_conv_conv1_w': 7.561,
     'L0_conv_ca1_w': 8.0,
     'L0_conv_ca2_w': 8.0,
     'L0_conv_conv2_w': 8.0,
     'L0_conv_head_w': 6.744,
     'L0_conv_in_proj_w': 2.687,
     'L0_conv_conv1d_w': 2.942,
     'L0_conv_x_proj_w': 8.0,
     'L0_conv_dt_proj_w': 8.0,
     'L0_conv_A_log': 8.0,
     'L1_attn_W_qkv': 8.0,
     'L1_attn_W_out': 8.0,
     'L1_ffn_router_w': 3.178,
     'L1_ffn_expert_w': 2.786}
    for name, (base, spread) in spreads.items():
        noise = np.random.default_rng([zlib.crc32(name.encode()), seed]).standard_normal(out[name].shape)
        drawn = base * np.exp(spread * noise) if base else spread * noise
        out[name] = jnp.asarray(drawn.astype(out[name].dtype))
    for name, factor in factors.items():
        out[name] = (out[name] * factor).astype(out[name].dtype)
    return out
```

```python
import numpy as np
import concourse.bass as bass
from concourse import mybir
from contextlib import ExitStack

F32, BF16, F16, I32 = mybir.dt.float32, mybir.dt.bfloat16, mybir.dt.float16, mybir.dt.int32
ALU, ACT, AX = mybir.AluOpType, mybir.ActivationFunctionType, mybir.AxisListType

B, C, H, W = 4, 128, 64, 64
L = H * W
PS = 4
NP_ = (H // PS) * (W // PS)
TT = NP_ // 128
OFF = PS * PS
NT = TT * OFF
DI, DS, DR, DC = 2 * C, 16, C // 16, 4
HD = DI // 128
CH = 512
NCH = L // CH
PW = W + 2
HEADS, DH = 4, 32
SCALE = 10.0
NE = 8
SPLIT = 4096.0
SAFE = 60.0


class Chain:

    def __init__(self, eng, sem):
        self.eng, self.sem, self.n = eng, sem, 0

    def __call__(self, ins):
        self.n += 1
        ins.then_inc(self.sem, 1)
        self.eng.wait_ge(self.sem, self.n)


class Kernel:

    def __init__(self, nc, ctx, ins, out, batches=B):
        self.nc, self.ctx, self.ins, self.out, self.batches = nc, ctx, ins, out, batches
        self.sems = {}

        def sb(name, shape, dt=F32):
            return ctx.enter_context(nc.sbuf_tensor(name, shape, dt))

        self.ident = sb("ident", [128, 128])
        self.group = sb("group", [128, 32, 4])
        self.diag = sb("diag", [128, 2, 9, 128])
        self.wz = sb("wz", [128, DI])
        self.tapw = sb("tapw", [128, DC, DI])
        self.xpw = sb("xpw", [128, HD, 128])
        self.dtw = sb("dtw", [128, DI])
        self.sel = sb("sel", [128, 32, 128], BF16)
        self.outw = sb("outw", [128, HD, C])
        self.wqkv = sb("wqkv", [128, 3 * C])
        self.wout = sb("wout", [128, C])
        self.expw = sb("expw", [128, NE, C])
        self.expb = sb("expb", [128, 4, C])
        self.routw = sb("routw", [128, NE])
        self.iota = sb("iota", [128, NP_])
        self.lower = sb("lower", [128, TT, NP_], BF16)
        self.mask8 = sb("mask8", [NCH, NCH, 32], BF16)
        self.hwin = sb("hwin", [128, 2 * NCH - 1])
        self.owin = sb("owin", [128, 2 * NCH - 1])
        self.ca1 = sb("ca1", [128, C // 4])
        self.ca2 = sb("ca2", [C // 4, C])
        self.brow = sb("brow", [1, 4, C])
        self.ones = sb("ones", [128, 128])
        self.cols = sb("cols", [128, 64])
        self.convw = sb("convw", [128, 2, 9])
        self.amat = sb("amat", [128, HD, DS])
        self.rtb = sb("rtb", [128, NE])
        self.rank8 = sb("rank8", [128, NE])
        self.perm = sb("perm", [128, TT, NP_])
        self.permt = sb("permt", [128, TT, NP_])
        self.hlast = sb("hlast", [128, DS, HD, 1])
        self.small = sb("small", [128, 160])
        self.flag = sb("flag", [1, 1], I32)
        self.R = sb("arena", [128, 40960])
        self.ps = ctx.enter_context(nc.psum_tensor("ps", [128, 8 * CH], F32))

    def sem(self, name):
        if name not in self.sems:
            self.sems[name] = self.ctx.enter_context(self.nc.semaphore(name))
        return self.sems[name]

    def clear(self):
        nums = [s.num for s in self.sems.values()]
        self.nc.all_engine_barrier(sems_to_clear=range(min(nums), max(nums) + 1))

    def bank(self, n, cols=CH, at=0):
        return self.ps[:, n * CH + at:n * CH + at + cols]

    def at(self, off, n):
        return self.R[:, off:off + n]


C_B1, C_B2, C_G, C_NB, C_HB, C_CB, C_DTB, C_D, C_ONE = 0, 1, 2, 3, 4, 5, 7, 9, 11


def patch_order(image, t, y):
    rows = H // TT
    v = image[:, t * rows * W:(t + 1) * rows * W].rearrange("p (h y w x) -> p y x h w", y=PS, w=W // PS, x=PS)
    return v[:, y]


def patch_tiles(tiles, t, y):
    n = PS * 128
    at = (t * PS + y) * n
    return tiles[:, at:at + n].rearrange("p (x h w) -> p x h w", x=PS, w=W // PS)


def setup(k):
    nc, w = k.nc, k.ins
    loaded, zeroed, built, made = k.sem("weights_loaded"), k.sem("zeroed"), k.sem("masks_built"), k.sem("made")
    taps = k.at(0, DI * DC)
    pieces = []

    def col(name, at):
        return (k.cols[:, at:at + 1], w[name].rearrange("(p a) -> p a", a=1))

    pieces += [col("L0_conv_conv1_b", C_B1), col("L0_conv_conv2_b", C_B2), col("L0_conv_norm_g", C_G), col("L0_conv_norm_b", C_NB)]
    for n, at in (("L0_conv_conv1d_b", C_CB), ("L0_conv_dt_proj_b", C_DTB), ("L0_conv_D", C_D)):
        for h in range(HD):
            pieces.append((k.cols[:, at + h:at + h + 1], w[n][h * 128:(h + 1) * 128].rearrange("(p a) -> p a", a=1)))
    pieces.append((k.cols[:, C_HB:C_HB + 1], w["L0_conv_head_b"].partition_broadcast(128)))
    pieces.append((k.convw[:, 0, :], w["L0_conv_conv1_w"].rearrange("c a y x -> c (a y x)")))
    pieces.append((k.convw[:, 1, :], w["L0_conv_conv2_w"].rearrange("c a y x -> c (a y x)")))
    pieces.append((k.tapw[:, 0, :], w["in_projT"][:, 0:DI]))
    pieces.append((k.wz[:, :], w["in_projT"][:, DI:2 * DI]))
    pieces.append((taps, w["L0_conv_conv1d_w"].rearrange("d k -> (d k)").partition_broadcast(128)))
    pieces.append((k.outw[:, :, :], w["out_projT"].rearrange("(h p) c -> p h c", h=HD)))
    pieces.append((k.wqkv[:, :], w["L1_attn_W_qkv"]))
    pieces.append((k.wout[:, :], w["L1_attn_W_out"]))
    pieces.append((k.routw[:, :], w["L1_ffn_router_w"]))
    pieces.append((k.rtb[:, :], w["L1_ffn_router_b"].partition_broadcast(128)))
    pieces.append((k.expw[:, :, :], w["L1_ffn_expert_w"].rearrange("e d c -> d e c")))
    pieces.append((k.ca1[:, :], w["ca1T"]))
    pieces.append((k.ca2[:, :], w["ca2T"]))
    pieces.append((k.amat[:, :, :], w["L0_conv_A_log"].rearrange("(h p) s -> p h s", h=HD)))
    for q in range(4):
        pieces.append((k.brow[0:1, q, :], w["L1_attn_b_out"].rearrange("(a c) -> a c", a=1)))
    late = [(k.hwin[:, NCH - 1:NCH], w["L0_conv_head_w"].rearrange("a c -> c a"))]
    for g in range(3):
        for h in range(HD):
            late.append((k.xpw[:, h, 32 * g:32 * g + 32], w["x_projT"][h * 128:(h + 1) * 128, DR:DR + 2 * DS]))
    for h in range(HD):
        late.append((k.xpw[:, h, 96:96 + DR], w["x_projT"][h * 128:(h + 1) * 128, 0:DR]))
    late.append((k.dtw[96:96 + DR, :], w["dt_projT"]))
    for q in range(4):
        late.append((k.expb[32 * q:32 * q + NE, q, :], w["L1_ffn_expert_b"]))
    total = 16 * (len(pieces) + len(late))

    with nc.Block() as block:
        @block.sync
        def _(sp):
            for dst, src in pieces:
                sp.dma_start(dst, src, allow_slow_non_contiguous=True).then_inc(loaded, 16)
            sp.wait_ge(zeroed, 5)
            for dst, src in late:
                sp.dma_start(dst, src, allow_slow_non_contiguous=True).then_inc(loaded, 16)

        @block.gpsimd
        def _(pool):
            step = Chain(pool, built)
            step(pool.memset(k.ident[:, :], 0.0))
            step(pool.affine_select(out=k.ident[:, :], in_=k.ident[:, :], compare_op=ALU.not_equal, fill=1.0,
                                    base=0, pattern=[[-1, 128]], channel_multiplier=1))
            step(pool.memset(k.group[:, :, :], 0.25))
            step(pool.affine_select(out=k.group[:, :, :], in_=k.group[:, :, :], compare_op=ALU.is_ge, fill=0.0,
                                    base=0, pattern=[[-4, 32], [0, 4]], channel_multiplier=1))
            step(pool.affine_select(out=k.group[:, :, :], in_=k.group[:, :, :], compare_op=ALU.is_ge, fill=0.0,
                                    base=3, pattern=[[4, 32], [0, 4]], channel_multiplier=-1))
            step(pool.memset(k.sel[:, :, :], 0.0))
            for g in range(3):
                v = k.sel[32 * g:32 * g + 32, :, :]
                step(pool.affine_select(out=v, in_=v, compare_op=ALU.not_equal, fill=1.0,
                                        base=0, pattern=[[-1, 32], [0, 128]], channel_multiplier=1))
            step(pool.iota(k.iota[:, :], [[1, NP_]], base=0, channel_multiplier=0, allow_small_or_imprecise_dtypes=True))
            step(pool.iota(k.rank8[:, :], [[-1, NE]], base=NE, channel_multiplier=0, allow_small_or_imprecise_dtypes=True))
            step(pool.memset(k.lower[:, :, :], 1.0))
            step(pool.affine_select(out=k.lower[:, :, :], in_=k.lower[:, :, :], compare_op=ALU.is_gt, fill=0.0,
                                    base=0, pattern=[[128, TT], [-1, NP_]], channel_multiplier=1))
            step(pool.memset(k.mask8[:, :, :], 0.0))
            step(pool.affine_select(out=k.mask8[:, :, :], in_=k.mask8[:, :, :], compare_op=ALU.not_equal, fill=1.0,
                                    base=0, pattern=[[-1, NCH], [0, 32]], channel_multiplier=1))
            step(pool.memset(k.owin[:, :], 0.0))
            step(pool.memset(k.owin[:, NCH - 1:NCH], 1.0))
            step(pool.memset(k.ones[:, :], 1.0))
            step(pool.memset(k.cols[:, C_ONE:C_ONE + 1], 1.0))

        @block.vector
        def _(dve):
            for t in (k.hwin[:, :], k.xpw[:, :, :], k.dtw[:, :], k.expb[:, :, :], k.small[:, :]):
                dve.memset(t, 0.0).then_inc(zeroed, 1)
            dve.wait_ge(loaded, total)
            dve.wait_ge(built, 2)
            for n in range(2):
                for t in range(9):
                    dve.tensor_scalar(k.diag[:, n, t, :], k.ident[:, :], k.convw[:, n, t:t + 1], None, ALU.mult)\
                       .then_inc(made, 1)
            tv = taps.rearrange("p (d k) -> p k d", k=DC)
            for t in range(DC - 1, -1, -1):
                if t == 0:
                    dve.wait_ge(made, 18 + DC - 1)
                dve.tensor_tensor(k.tapw[:, t, :], k.tapw[:, 0, :], tv[:, t, :], ALU.mult).then_inc(made, 1)

        @block.scalar
        def _(act):
            step = Chain(act, k.sem("a_made"))
            act.wait_ge(loaded, total)
            step(act.activation(k.amat[:, :, :], k.amat[:, :, :], ACT.Exp))
            step(act.mul(k.amat[:, :, :], k.amat[:, :, :], -1.0))
    k.clear()


X_AT, PAD1_AT, PAD2_AT, FEAT_AT, SQ_AT, XT_AT, PE_AT, X1_AT, XP_AT = 0, 4096, 8704, 13312, 17408, 21504, 25600, 29696, 33800
X1_PAD = 8


def score(k, b):
    nc = k.nc
    x = k.at(X_AT, L)
    pad = [k.at(o, PW * PW).rearrange("p (h w) -> p h w", w=PW) for o in (PAD1_AT, PAD2_AT)]
    inner = [p[:, 1:H + 1, 1:W + 1] for p in pad]
    feat, sq, xp = k.at(FEAT_AT, L), k.at(SQ_AT, L), k.at(XP_AT, L)
    RC = CH // W
    S = k.small
    stats = S[:, 0:48].rearrange("p (n s) -> p n s", s=6)
    mv, g2, gm, rstd, t0, t1 = S[:, 48:50], S[:, 50:52], S[:, 52:53], S[:, 53:54], S[:, 54:55], S[:, 55:56]
    csum, ctot, hid, ca = S[:, 56:64], S[:, 64:65], S[0:C // 4, 65:66], S[:, 66:67]
    colv, rank = S[:, 68:70], S[:, 70:72]
    work = k.at(X1_AT, 4096)
    rows = [work[0:NCH, i * CH:(i + 1) * CH] for i in range(6)]
    bd = work[0:NCH, 3072:3072 + NP_].rearrange("p (n q) -> p n q", q=32)
    smb, junk = work[:, 3328:3328 + NP_], work[:, 3584:3584 + NP_]
    x_in, pe_in = k.sem("x_in"), k.sem("pe_in")
    border, gn_in, gn_sum, gn_var, gn_std, xn = (k.sem(n) for n in ("borders_zero", "gn_in", "gn_sum", "gn_var", "gn_std", "xn_ready"))
    conv = [k.sem("conv1_done"), k.sem("conv2_done")]
    gelu = [k.sem("gelu1_done"), k.sem("gelu2_done")]
    csm, hmm, hre, amm, ca_s, scaled, sq_s = (k.sem(n) for n in ("csum_ready", "hid_mm", "hid_relu", "att_mm", "att_ready", "feat_scaled", "squares"))
    head, sigs, pv, bd_s, bc, pm, pt = (k.sem(n) for n in ("head_mm", "sigmoids", "pv_ready", "scores_spread", "scores_bcast", "perm_ready", "permt_mm"))
    vch = k.sem("v_chain")

    with nc.Block() as block:
        @block.sync
        def _(sp):
            for i in range(4):
                sp.dma_start(x[:, i * 1024:(i + 1) * 1024], k.ins["x"][b, :, i * 1024:(i + 1) * 1024]).then_inc(x_in, 16)
            pe_v = k.ins["pe"].rearrange("(t h y w x) c -> t y h w (x c)", t=TT, y=PS, w=W // PS, x=PS)
            dst = k.at(PE_AT, L).rearrange("p (t y n) -> p t y n", t=TT, y=PS)
            for t in range(TT):
                for y in range(PS):
                    for h in range(8):
                        sp.dma_start(dst[16 * h:16 * h + 16, t, y, :], pe_v[t, y, h]).then_inc(pe_in, 16)
            sp.wait_ge(pe_in, 16 * TT * PS * 8)

        @block.gpsimd
        def _(pool):
            for p in pad:
                pool.memset(p[:, 0:PW:PW - 1, :], 0.0).then_inc(border, 1)
                pool.memset(p[:, 1:H + 1, 0:PW:PW - 1], 0.0).then_inc(border, 1)
            pool.wait_ge(xn, 1)
            for t in range(TT):
                for y in range(PS):
                    pool.tensor_scalar(patch_tiles(xp, t, y), patch_order(x, t, y), gm, rstd, ALU.subtract, ALU.mult)\
                        .then_inc(k.sem("patches_ready"), 1)

        @block.vector
        def _(dve):
            step = Chain(dve, vch)
            for n in range(NCH):
                dve.wait_ge(x_in, 64)
                step(dve.bn_stats(stats[:, n, :], x[:, n * CH:(n + 1) * CH]))
            step(dve.bn_aggr(mv, stats))
            step(dve.tensor_copy(g2[:, 0:1], mv[:, 0:1]))
            dve.scalar_tensor_tensor(g2[:, 1:2], mv[:, 0:1], mv[:, 0:1], mv[:, 1:2], ALU.mult, ALU.add).then_inc(gn_in, 1)
            dve.wait_ge(gn_sum, 1)
            step(dve.tensor_copy(gm, k.bank(0, 1)))
            step(dve.tensor_tensor(t0, gm, gm, ALU.mult))
            step(dve.tensor_tensor(t0, k.bank(0, 1, 1), t0, ALU.subtract))
            dve.tensor_scalar(t0, t0, 1e-5, None, ALU.add).then_inc(gn_var, 1)
            dve.wait_ge(gn_std, 1)
            step(dve.reciprocal(rstd, rstd))
            step(dve.tensor_tensor(t1, rstd, rstd, ALU.mult))
            step(dve.tensor_tensor(t1, t1, t0, ALU.mult))
            step(dve.tensor_scalar(t1, t1, -0.5, 1.5, ALU.mult, ALU.add))
            step(dve.tensor_tensor(rstd, rstd, t1, ALU.mult))
            dve.wait_ge(border, 4)
            dve.tensor_scalar(inner[0], x.rearrange("p (h w) -> p h w", w=W), gm, rstd, ALU.subtract, ALU.mult).then_inc(xn, 1)
            dve.wait_ge(gelu[0], NCH)
            step(dve.reduce_sum(ctot, csum, axis=AX.X))
            dve.tensor_scalar(ctot, ctot, 1.0 / L, None, ALU.mult).then_inc(csm, 1)
            dve.wait_ge(hmm, 1)
            dve.tensor_scalar(hid, k.ps[0:C // 4, 0:1], 0.0, None, ALU.max).then_inc(hre, 1)
            dve.wait_ge(ca_s, 1)
            dve.tensor_scalar(inner[1], inner[1], ca, None, ALU.mult).then_inc(scaled, 1)
            dve.wait_ge(head, 3)
            step(dve.tensor_copy(rows[0], k.ps[0:NCH, CH:2 * CH]))
            step(dve.scalar_tensor_tensor(rows[1], rows[0], -1.0 / C, rows[0], ALU.mult, ALU.mult))
            dve.tensor_tensor(rows[1], k.ps[0:NCH, 2 * CH:3 * CH], rows[1], ALU.add).then_inc(pv, 1)
            dve.wait_ge(sigs, 2)
            step(dve.tensor_scalar(rows[3], rows[3], 0.3, None, ALU.mult))
            step(dve.scalar_tensor_tensor(rows[4], rows[2], 0.7, rows[3], ALU.mult, ALU.add))
            step(dve.reduce_sum(rows[5][:, 0:128], rows[4].rearrange("p (n x) -> p n x", x=PS), axis=AX.X))
            step(dve.reduce_sum(rows[0][:, 0:32].rearrange("p (h w) -> p h w", h=2),
                                rows[5][:, 0:128].rearrange("p (h y w) -> p h w y", h=2, y=PS), axis=AX.X))
            dve.scalar_tensor_tensor(bd, rows[0][:, 0:32].unsqueeze(1).broadcast_to([NCH, NCH, 32]), 1.0 / OFF,
                                     k.mask8[:, :, :], ALU.mult, ALU.mult).then_inc(bd_s, 1)
            dve.wait_ge(bc, 1)
            step(dve.tensor_copy(smb, k.bank(3, NP_)))
            for t in range(TT):
                step(dve.scalar_tensor_tensor(junk[:, 0:128], smb[:, 128 * t:128 * t + 128], 1.0, k.ident[:, :],
                                              ALU.mult, ALU.mult, accum_out=colv[:, t:t + 1]))
                step(dve.scalar_tensor_tensor(junk, smb, colv[:, t:t + 1], k.lower[:, t, :], ALU.is_equal, ALU.mult))
                step(dve.scalar_tensor_tensor(junk, smb, colv[:, t:t + 1], junk, ALU.is_gt, ALU.add,
                                              accum_out=rank[:, t:t + 1]))
                dve.tensor_scalar(k.perm[:, t, :], k.iota[:, :], rank[:, t:t + 1], None, ALU.is_equal).then_inc(pm, 1)
            dve.wait_ge(pt, 1)
            dve.tensor_copy(k.permt[:, :, :].rearrange("p a b -> p (a b)"), k.bank(4)).then_inc(vch, 1)

        @block.scalar
        def _(act):
            act.wait_ge(gn_var, 1)
            act.activation(rstd, t0, ACT.Sqrt).then_inc(gn_std, 1)
            act.wait_ge(xn, 1)
            for i in range(2):
                if i == 1:
                    act.wait_ge(amm, 1)
                    act.activation(ca, k.bank(1, 1), ACT.Sigmoid).then_inc(ca_s, 1)
                for n in range(NCH):
                    act.wait_ge(conv[i], n + 1)
                    if i == 0:
                        act.wait_ge(border, 4)
                        act.activation(pad[1][:, 1 + RC * n:1 + RC * n + RC, 1:W + 1],
                                       k.bank(n).rearrange("p (h w) -> p h w", w=W), ACT.Gelu,
                                       bias=k.cols[:, C_B1:C_B1 + 1], accum_out=csum[:, n:n + 1]).then_inc(gelu[0], 1)
                    else:
                        act.activation(feat[:, n * CH:(n + 1) * CH], k.bank(n), ACT.Gelu,
                                       bias=k.cols[:, C_B2:C_B2 + 1]).then_inc(gelu[1], 1)
                if i == 0:
                    act.activation(sq.rearrange("p (h w) -> p h w", w=W), inner[0], ACT.Square).then_inc(sq_s, 1)
            act.wait_ge(head, 1)
            act.activation(rows[2], k.ps[0:NCH, 0:CH], ACT.Sigmoid, bias=k.cols[0:NCH, C_HB:C_HB + 1]).then_inc(sigs, 1)
            act.wait_ge(pv, 1)
            act.activation(rows[3], rows[1], ACT.Sigmoid, scale=10.0 / (C - 1)).then_inc(sigs, 1)

        @block.tensor
        def _(pe):
            pe.wait_ge(gn_in, 1)
            pe.matmul(k.bank(0, 2), k.group[:, :, :].rearrange("p a b -> p (a b)"), g2, start=True, stop=True).then_inc(gn_sum, 1)
            pe.wait_ge(xn, 1)
            for i in range(2):
                if i == 1:
                    pe.wait_ge(csm, 1)
                    pe.matmul(k.ps[0:C // 4, 0:1], k.ca1[:, :], ctot, start=True, stop=True).then_inc(hmm, 1)
                    pe.wait_ge(hre, 1)
                    pe.matmul(k.bank(1, 1), k.ca2[:, :], hid, start=True, stop=True).then_inc(amm, 1)
                    pe.wait_ge(scaled, 1)
                for n in range(NCH):
                    for t in range(9):
                        y, xx = t // 3, t % 3
                        last = pe.matmul(k.bank(n).rearrange("p (h w) -> p h w", w=W), k.diag[:, i, t, :],
                                         pad[i][:, RC * n + y:RC * n + y + RC, xx:xx + W], start=t == 0, stop=t == 8)
                    last.then_inc(conv[i], 1)
            pe.wait_ge(gelu[1], NCH)
            for n in range(NCH):
                last = pe.matmul(k.ps[0:NCH, 0:CH], k.hwin[:, NCH - 1 - n:2 * NCH - 1 - n], feat[:, n * CH:(n + 1) * CH],
                                 start=n == 0, stop=n == NCH - 1)
            last.then_inc(head, 1)
            for n in range(NCH):
                last = pe.matmul(k.ps[0:NCH, CH:2 * CH].rearrange("p (h w) -> p h w", w=W), k.owin[:, NCH - 1 - n:2 * NCH - 1 - n],
                                 pad[0][:, 1 + RC * n:1 + RC * n + RC, 1:W + 1], start=n == 0, stop=n == NCH - 1)
            last.then_inc(head, 1)
            pe.wait_ge(sq_s, 1)
            for n in range(NCH):
                last = pe.matmul(k.ps[0:NCH, 2 * CH:3 * CH], k.owin[:, NCH - 1 - n:2 * NCH - 1 - n], sq[:, n * CH:(n + 1) * CH],
                                 start=n == 0, stop=n == NCH - 1)
            last.then_inc(head, 1)
            pe.wait_ge(bd_s, 1)
            pe.matmul(k.bank(3, NP_), k.ones[0:NCH, :], bd.rearrange("p n q -> p (n q)"), start=True, stop=True).then_inc(bc, 1)
            for t in range(TT):
                pe.wait_ge(pm, t + 1)
                for u in range(TT):
                    last = pe.transpose(k.bank(4, 128, NP_ * u + 128 * t), k.perm[:, t, 128 * u:128 * u + 128], k.ident[:, :])
            last.then_inc(pt, 1)
    k.clear()


def sort_tokens(k):
    nc = k.nc
    xp, xt, pe_t = k.at(XP_AT, L), k.at(XT_AT, L), k.at(PE_AT, L)
    x1 = k.at(X1_AT, X1_PAD + L)
    x1v = x1[:, X1_PAD:].rearrange("p (s o) -> p o s", o=OFF)
    tr, xtr, std, nrm, pmm, vch = (k.sem(n) for n in ("tr_done", "var_ready", "std_ready", "norm_done", "perm_mm", "v_chain"))
    st = k.at(FEAT_AT, NT * 6).rearrange("p (n s) -> p n s", s=6)
    mv = k.at(FEAT_AT + 192, NT * 2).rearrange("p (n s) -> p n s", s=2)
    rs = k.at(FEAT_AT + 256, NT)

    with nc.Block() as block:
        @block.tensor
        def _(pe):
            for i in range(NT):
                last = pe.transpose(k.ps[:, i * 128:(i + 1) * 128], xp[:, i * 128:(i + 1) * 128], k.ident[:, :])
                if i % 4 == 3:
                    last.then_inc(tr, 1)
            for o in range(0, OFF, 2):
                pe.wait_ge(nrm, NT)
                for oo in (o, o + 1):
                    for t in range(TT):
                        last = pe.matmul(k.bank(o // 2, NP_, (oo % 2) * NP_), xt[:, (t * OFF + oo) * 128:(t * OFF + oo + 1) * 128],
                                         k.perm[:, t, :], start=t == 0, stop=t == TT - 1)
                last.then_inc(pmm, 1)

        @block.gpsimd
        def _(pool):
            pool.memset(x1[:, 0:X1_PAD], 0.0).then_inc(k.sem("x1_pad"), 1)

        @block.vector
        def _(dve):
            step = Chain(dve, vch)
            for g in range(NT // 4):
                dve.wait_ge(tr, g + 1)
                step(dve.tensor_tensor(xt[:, g * CH:(g + 1) * CH], k.bank(g), pe_t[:, g * CH:(g + 1) * CH], ALU.add))
                for i in range(4 * g, 4 * g + 4):
                    dve.bn_stats(st[:, i, :], xt[:, i * 128:(i + 1) * 128]).then_inc(vch, 1)
                    step.n += 1
            dve.wait_ge(vch, step.n)
            for i in range(NT):
                dve.bn_aggr(mv[:, i, :], st[:, i, :]).then_inc(vch, 1)
                step.n += 1
            dve.wait_ge(vch, step.n)
            dve.tensor_scalar(rs, mv[:, :, 1], 1e-5, None, ALU.add).then_inc(xtr, 1)
            dve.wait_ge(std, 1)
            step(dve.reciprocal(rs, rs))
            for i in range(NT):
                dve.tensor_scalar(xt[:, i * 128:(i + 1) * 128], xt[:, i * 128:(i + 1) * 128], mv[:, i, 0:1], rs[:, i:i + 1],
                                  ALU.subtract, ALU.mult).then_inc(nrm, 1)

        @block.scalar
        def _(act):
            act.wait_ge(xtr, 1)
            act.activation(rs, rs, ACT.Sqrt).then_inc(std, 1)
            for g in range(OFF // 2):
                act.wait_ge(pmm, g + 1)
                act.activation(x1v[:, 2 * g:2 * g + 2, :], k.bank(g).rearrange("p (o s) -> p o s", o=2), ACT.Identity,
                               bias=k.cols[:, C_NB:C_NB + 1], scale=k.cols[:, C_G:C_G + 1]).then_inc(k.sem("x1_ready"), 1)
    k.clear()


XC_AT, SZ_AT, DBC_AT = 0, 8192, 16384


def project(k):
    nc = k.nc
    x1 = k.at(X1_AT, X1_PAD + L)
    xc = k.at(XC_AT, HD * L).rearrange("p (h n) -> p h n", h=HD)
    sz = k.at(SZ_AT, HD * L).rearrange("p (h n) -> p h n", h=HD)
    dbc = k.at(DBC_AT, L)
    mm, xp, ev = k.sem("proj_mm"), k.sem("xproj_mm"), k.sem("silu_done")

    with nc.Block() as block:
        @block.tensor
        def _(pe):
            with pe.Fori(0, NCH) as c:
                for h in range(HD):
                    pe.wait_ge(ev, c * 5 + h + 1)
                    for t in range(DC):
                        last = pe.matmul(k.bank(h), k.tapw[:, t, h * 128:(h + 1) * 128],
                                         x1[:, bass.ds(c * CH + (X1_PAD - DC + 1 + t), CH)], start=t == 0, stop=t == DC - 1)
                    last.then_inc(mm, 1)
                for h in range(HD):
                    pe.wait_ge(ev, c * 5 + 2 + h + 1)
                    pe.matmul(k.bank(2 + h), k.wz[:, h * 128:(h + 1) * 128], x1[:, bass.ds(c * CH + X1_PAD, CH)],
                              start=True, stop=True).then_inc(mm, 1)
                pe.wait_ge(ev, c * 5 + 7)
                for h in range(HD):
                    last = pe.matmul(k.bank(4), k.xpw[:, h, :], xc[:, h, bass.ds(c * CH, CH)], start=h == 0, stop=h == HD - 1)
                last.then_inc(xp, 1)

        @block.scalar
        def _(act):
            act.sem_inc(ev, 5)
            with act.Fori(0, NCH) as c:
                for h in range(HD):
                    act.wait_ge(mm, c * 4 + h + 1)
                    act.activation(xc[:, h, bass.ds(c * CH, CH)], k.bank(h), ACT.Silu,
                                   bias=k.cols[:, C_CB + h:C_CB + h + 1]).then_inc(ev, 1)
                for h in range(HD):
                    act.wait_ge(mm, c * 4 + 2 + h + 1)
                    act.activation(sz[:, h, bass.ds(c * CH, CH)], k.bank(2 + h), ACT.Silu).then_inc(ev, 1)
                act.wait_ge(xp, c + 1)
                act.activation(dbc[:, bass.ds(c * CH, CH)], k.bank(4), ACT.Copy).then_inc(ev, 1)
    k.clear()


def cols_of(c, n=CH):
    return slice(c * n, (c + 1) * n) if isinstance(c, int) else bass.ds(c * n, n)


def scan(k):
    nc = k.nc
    xc = k.at(XC_AT, HD * L).rearrange("p (h n) -> p h n", h=HD)
    sz = k.at(SZ_AT, HD * L).rearrange("p (h n) -> p h n", h=HD)
    dbc = k.at(DBC_AT, L)
    at = [DBC_AT + L]

    def ring(n, cols=HD * CH):
        out = [k.at(at[0] + i * cols, cols) for i in range(n)]
        at[0] += n * cols
        return out

    def halves(t):
        return t.rearrange("p (h n) -> p h n", h=HD)

    dt, u = ring(2), ring(2)
    (ab,), (onep,), (ln,), (rx,) = ring(1), ring(1), ring(1), ring(1)
    pieces = [t.bitcast(BF16) for t in ring(2, CH // 2)]
    (rest,) = ring(1, CH)
    da, dbx, hb, g, (tmp,) = ring(4), ring(2), ring(2), ring(2), ring(1)
    assert at[0] <= 40960
    dt_mm, ab_s, e_s, w_s, ln_s, rx_s, dt_s, pc_s = (k.sem(n) for n in (
        "dt_mm", "dt_abs", "dt_exp", "dt_onep", "dt_ln", "dt_relu", "dt_ready", "pieces_ready"))
    b_mm, c_mm, y_mm, da_s, dbx_s, sc_s, hl_s, hc_s, fin_s = (k.sem(n) for n in (
        "b_mm", "c_mm", "y_mm", "da_ready", "dbx_ready", "scan_done", "hlast_saved", "hc_ready", "chunk_done"))
    va, vp = k.sem("v_chain"), k.sem("p_chain")
    STEPS = NCH * DS

    def chunks(eng, prepare, body):
        prepare(0, 0)
        with eng.Fori(0, NCH // 2 - 1) as cc:
            for q in range(2):
                body(cc * 2 + q, q, True)
        body(NCH - 2, 0, True)
        body(NCH - 1, 1, False)

    with nc.Block() as block:
        @block.tensor
        def _(pe):
            def prepare(c, q):
                if q or not isinstance(c, int) or c:
                    pe.wait_ge(rx_s, c * 2)
                for h in range(HD):
                    last = pe.matmul(k.bank(h), k.dtw[:, h * 128:(h + 1) * 128], dbc[:, cols_of(c)], start=True, stop=True)
                last.then_inc(dt_mm, 1)

            def total(c, s):
                pe.wait_ge(hc_s, c * DS + (s + 1 + 2))
                if s == 0:
                    pe.wait_ge(fin_s, c * 1 + 1)
                for h in range(HD):
                    last = pe.matmul(k.bank(6 + h), k.ident[:, :], halves(g[s % 2])[:, h, :], start=s == 0, stop=s == DS - 1)
                last.then_inc(y_mm, 1)

            def body(c, q, more):
                pe.wait_ge(pc_s, c * 1 + 1)
                for s in range(DS):
                    n = c * DS + s
                    pe.wait_ge(dbx_s, n + 1)
                    pe.matmul(k.bank(2 + s % 2), k.sel[:, s, :], pieces[q], start=True, stop=True).then_inc(b_mm, 1)
                    pe.wait_ge(hc_s, n + 1)
                    pe.matmul(k.bank(4 + s % 2), k.sel[:, DS + s, :], pieces[q], start=True, stop=True).then_inc(c_mm, 1)
                    if s >= 1:
                        total(c, s - 1)
                    if more and s == 1:
                        prepare(c + 1, 1 - q)
                total(c, DS - 1)
            chunks(pe, prepare, body)

        @block.scalar
        def _(act):
            def abs_exp(c):
                act.wait_ge(dt_mm, c * 1 + 1)
                for h in range(HD):
                    act.activation(halves(ab)[:, h, :], k.bank(h), ACT.Abs, bias=k.cols[:, C_DTB + h:C_DTB + h + 1]).then_inc(ab_s, 1)
                for h in range(HD):
                    act.activation(halves(rx)[:, h, :], k.bank(h), ACT.Relu, bias=k.cols[:, C_DTB + h:C_DTB + h + 1]).then_inc(rx_s, 1)
                act.wait_ge(ab_s, c * 2 + 2)
                act.activation(ab, ab, ACT.Exp, scale=-1.0).then_inc(e_s, 1)

            def log(c):
                act.wait_ge(w_s, c * 1 + 1)
                act.activation(ln, onep, ACT.Ln).then_inc(ln_s, 1)

            def body(c, q, more):
                act.wait_ge(dt_s, c * 2 + 1)
                for s in range(DS):
                    act.wait_ge(sc_s, c * (2 * DS) + (2 * s + 2))
                    for h in range(HD):
                        act.activation(halves(da[s % 4])[:, h, :], halves(dt[q])[:, h, :], ACT.Exp,
                                       scale=k.amat[:, h, s:s + 1]).then_inc(da_s, 1)
                    if more and s == 3:
                        abs_exp(c + 1)
                    if more and s == 8:
                        log(c + 1)
            chunks(act, lambda c, q: (abs_exp(c), log(c)), body)

        @block.gpsimd
        def _(pool):
            started = k.sem("h_zero")

            def wait(sem, value):
                pool.wait_ge(sem, value)
                pool.sem_inc(k.sem("pool_waits_met"), 1)

            def onep_(c):
                wait(e_s, c * 1 + 1)
                pool.tensor_scalar(onep, ab, 1.0, None, ALU.add).then_inc(w_s, 1)

            def split(c, q):
                p, b0 = pieces[q], c * 5
                src = dbc[0:96, cols_of(c)]
                pool.tensor_copy(p[0:96, :], src).then_inc(vp, 1)
                wait(vp, b0 + 1)
                pool.tensor_tensor(rest[0:64, :], dbc[0:64, cols_of(c)], p[0:64, :], ALU.subtract).then_inc(vp, 1)
                wait(vp, b0 + 2)
                pool.tensor_copy(p[0:64, :], rest[0:64, :]).then_inc(vp, 1)
                wait(vp, b0 + 3)
                pool.tensor_tensor(p[0:32, :], rest[0:32, :], p[0:32, :], ALU.subtract).then_inc(vp, 1)
                wait(vp, b0 + 4)
                pool.sem_inc(vp, 1)
                pool.sem_inc(pc_s, 1)

            def softplus(c, q):
                step_s = k.sem("softplus_chain")
                n = c * 4
                wait(ln_s, c * 1 + 1)
                pool.tensor_scalar(onep, onep, 1.0, None, ALU.subtract).then_inc(step_s, 1)
                wait(step_s, n + 1)
                pool.tensor_tensor(onep, ab, onep, ALU.subtract).then_inc(step_s, 1)
                wait(step_s, n + 2)
                pool.tensor_tensor(onep, onep, ln, ALU.add).then_inc(step_s, 1)
                wait(step_s, n + 3)
                wait(rx_s, c * 2 + 2)
                pool.tensor_tensor(dt[q], onep, rx, ALU.add).then_inc(dt_s, 1)
                wait(dt_s, c * 2 + 1)
                pool.tensor_tensor(halves(u[q]), halves(dt[q]), xc[:, :, cols_of(c)], ALU.mult).then_inc(dt_s, 1)
                pool.sem_inc(step_s, 1)

            def body(c, q, more):
                for s in range(DS):
                    wait(sc_s, c * (2 * DS) + (2 * s + 2 + 8))
                    pool.tensor_copy(k.hlast[:, s, :, :], halves(hb[s % 2])[:, :, CH - 1:CH]).then_inc(hl_s, 1)
                    if more and s == 2:
                        split(c + 1, 1 - q)
                    if more and s == 6:
                        onep_(c + 1)
                    if more and s == 10:
                        softplus(c + 1, 1 - q)

            def prepare(c, q):
                for p in pieces:
                    pool.memset(p[96:128, :], 0.0).then_inc(k.sem("p_zero"), 1)
                pool.wait_ge(k.sem("p_zero"), 2)
                pool.memset(k.hlast[:, :, :, :], 0.0).then_inc(k.sem("h_zero"), 1)
                pool.wait_ge(started, 1)
                pool.sem_inc(hl_s, DS)
                split(c, q)
                onep_(c)
                softplus(c, q)
            chunks(pool, prepare, body)

        @block.vector
        def _(dve):
            def inject(c, q, s):
                if s == 0:
                    dve.wait_ge(dt_s, c * 2 + 2)
                dve.wait_ge(b_mm, c * DS + (s + 1))
                dve.tensor_tensor(halves(dbx[s % 2]), halves(u[q]), k.bank(2 + s % 2).unsqueeze(1).broadcast_to([128, HD, CH]),
                                  ALU.mult).then_inc(dbx_s, 1)

            def body(c, q, more):
                inject(c, q, 0)
                for s in range(DS):
                    dve.wait_ge(hl_s, c * DS + (s - 1 + DS))
                    dve.wait_ge(dbx_s, c * DS + (s + 1 + 2))
                    for h in range(HD):
                        dve.wait_ge(da_s, c * (2 * DS) + (2 * s + h + 1))
                        dve.tensor_tensor_scan(halves(hb[s % 2])[:, h, :], halves(da[s % 4])[:, h, :], halves(dbx[s % 2])[:, h, :],
                                               k.hlast[:, s, h, :], ALU.mult, ALU.add).then_inc(sc_s, 1)
                    if s < DS - 1:
                        inject(c, q, s + 1)
                    dve.wait_ge(c_mm, c * DS + (s + 1))
                    dve.wait_ge(y_mm, c * DS + (s + 1))
                    dve.wait_ge(sc_s, c * (2 * DS) + (2 * s + 2 + 8))
                    dve.tensor_tensor(halves(g[s % 2]), halves(hb[s % 2]), k.bank(4 + s % 2).unsqueeze(1).broadcast_to([128, HD, CH]),
                                      ALU.mult).then_inc(hc_s, 1)
                dve.wait_ge(y_mm, c * DS + (DS + 2))
                for h in range(HD):
                    dve.scalar_tensor_tensor(halves(tmp)[:, h, :], xc[:, h, cols_of(c)], k.cols[:, C_D + h:C_D + h + 1], k.bank(6 + h),
                                             ALU.mult, ALU.add).then_inc(va, 1)
                dve.wait_ge(va, c * 2 + 2)
                dve.sem_inc(fin_s, 1)
                dve.tensor_tensor(sz[:, :, cols_of(c)], halves(tmp), sz[:, :, cols_of(c)], ALU.mult).then_inc(k.sem("y_ready"), 1)

            dve.sem_inc(dbx_s, 2)
            dve.sem_inc(hc_s, 2)
            dve.sem_inc(sc_s, 8)
            dve.sem_inc(fin_s, 1)
            dve.sem_inc(y_mm, 2)
            chunks(dve, lambda c, q: None, body)
    k.clear()


T_AT = 20480


def unsort(k, b):
    nc = k.nc
    y = k.at(SZ_AT, HD * L).rearrange("p (h n) -> p h n", h=HD)
    om, x, xp, t1 = k.at(DBC_AT, L), k.at(0, L), k.at(4096, L), k.at(T_AT, L)
    x_in, xp_s, o_mm, o_ev, t_mm = (k.sem(n) for n in ("x_in", "patches_ready", "outproj_mm", "outproj_read", "unsort_mm"))
    t_ev = k.sem("tokens_ready")
    with nc.Block() as block:
        @block.sync
        def _(sp):
            for i in range(4):
                sp.dma_start(x[:, i * 1024:(i + 1) * 1024], k.ins["x"][b, :, i * 1024:(i + 1) * 1024]).then_inc(x_in, 16)

        @block.gpsimd
        def _(pool):
            pool.wait_ge(x_in, 64)
            for t in range(TT):
                for r in range(PS):
                    pool.tensor_copy(patch_tiles(xp, t, r), patch_order(x, t, r)).then_inc(xp_s, 1)

        @block.tensor
        def _(pe):
            for i in range(NT):
                u, o = i // OFF, i % OFF
                for h in range(HD):
                    first = u * 128 * OFF + o
                    last = pe.matmul(k.ps[:, i * 128:(i + 1) * 128], y[:, h, first:first + 127 * OFF + 1:OFF], k.outw[:, h, :],
                                     start=h == 0, stop=h == HD - 1)
                if i % 4 == 3:
                    last.then_inc(o_mm, 1)
            pe.wait_ge(o_ev, NT // 4)
            for g in range(NT // 4):
                t, o4 = g // 4, g % 4
                for u in range(TT):
                    pe.matmul(k.bank(g), k.permt[:, u, t * 128:(t + 1) * 128], om[:, u * OFF * 128 + o4 * CH:u * OFF * 128 + (o4 + 1) * CH],
                              start=u == 0, stop=False)
                pe.wait_ge(xp_s, g + 1)
                for j in range(4):
                    last = pe.matmul(k.bank(g, 128, 128 * j), xp[:, g * CH + 128 * j:g * CH + 128 * j + 128], k.ident[:, :],
                                     start=False, stop=j == 3)
                last.then_inc(t_mm, 1)

        @block.scalar
        def _(act):
            for g in range(0, NT // 4):
                act.wait_ge(o_mm, g + 1)
                act.activation(om[:, g * CH:(g + 1) * CH], k.bank(g), ACT.Copy).then_inc(o_ev, 1)

        @block.vector
        def _(dve):
            for g in range(NT // 4):
                dve.wait_ge(t_mm, g + 1)
                dve.tensor_copy(t1[:, g * CH:(g + 1) * CH], k.bank(g)).then_inc(t_ev, 1)
    k.clear()


def normalize(k, dve, act, tn_at, x_at, eps):
    x, tn = k.at(x_at, L), k.at(tn_at, L)
    S = k.small
    st = k.at(tn_at, NT * 6).rearrange("p (n s) -> p n s", s=6)
    mv = S[:, 0:NT * 2].rearrange("p (n s) -> p n s", s=2)
    rs = S[:, 64:64 + NT]
    var_s, std_s, st_s, tn_s = k.sem("ln_var"), k.sem("ln_std"), k.sem("ln_stats"), k.sem("ln_done")
    if act is not None:
        act.wait_ge(var_s, 1)
        act.activation(rs, rs, ACT.Sqrt).then_inc(std_s, 1)
        return
    for i in range(NT):
        dve.bn_stats(st[:, i, :], x[:, i * 128:(i + 1) * 128]).then_inc(st_s, 1)
    dve.wait_ge(st_s, NT)
    for i in range(NT):
        dve.bn_aggr(mv[:, i, :], st[:, i, :]).then_inc(st_s, 1)
    dve.wait_ge(st_s, 2 * NT)
    dve.tensor_scalar(rs, mv[:, :, 1], eps, None, ALU.add).then_inc(var_s, 1)
    dve.wait_ge(std_s, 1)
    dve.reciprocal(rs, rs).then_inc(st_s, 1)
    dve.wait_ge(st_s, 2 * NT + 1)
    for i in range(NT):
        dve.tensor_scalar(tn[:, i * 128:(i + 1) * 128], x[:, i * 128:(i + 1) * 128], mv[:, i, 0:1], rs[:, i:i + 1],
                          ALU.subtract, ALU.mult).then_inc(tn_s, 1)


TN_AT, TNT_AT = 24576, 28672
QF_AT, KF_AT, QH_AT, QL_AT, KH_AT, KL_AT = 0, 4096, 8192, 10240, 12288, 14336
KS_AT, QS_AT, V_AT = 0, 32768, 16384
S_MV, S_SSQ, S_MAX, S_SC, S_U = 0, 100, 102, 104, 106


def qkv(k):
    nc = k.nc
    tn, tnt = k.at(TN_AT, L), k.at(TNT_AT, L)
    full = [k.at(QF_AT, L), k.at(KF_AT, L)]
    hi = [k.at(a, L // 2).bitcast(F16) for a in (QH_AT, KH_AT)]
    lo = [k.at(a, L // 2).bitcast(F16) for a in (QL_AT, KL_AT)]
    stack = [k.at(a, 2 * L).bitcast(F16).rearrange("p (h n) -> p h n", h=HEADS) for a in (QS_AT, KS_AT)]
    v = k.at(V_AT, L)
    S = k.small
    ssq, mx, sc, u = S[:, S_SSQ:S_SSQ + 2], S[:, S_MAX:S_MAX + 2], S[:, S_SC:S_SC + 2], S[:, S_U:S_U + 1]
    tn_s, tr, tr_ev, mm, ev, vmm, vev = (k.sem(n) for n in ("ln_done", "tr_done", "tnt_ready", "qk_mm", "qk_ready", "v_mm", "v_ready"))
    ss_s, sq_s, split_s, stacked, umm = (k.sem(n) for n in ("squares", "norm_roots", "split_done", "stacked", "bound_mm"))
    NG = NT // 4
    with nc.Block() as block:
        @block.tensor
        def _(pe):
            for i in range(NT):
                pe.wait_ge(tn_s, i + 1)
                last = pe.transpose(k.ps[:, i * 128:(i + 1) * 128], tn[:, i * 128:(i + 1) * 128], k.ident[:, :])
                if i % 4 == 3:
                    last.then_inc(tr, 1)
            for m in range(2):
                for c in range(NCH):
                    if m == 0:
                        pe.wait_ge(tr_ev, max(c + 1, NG if c == 0 else 1))
                    else:
                        pe.wait_ge(ev, c + 1)
                    pe.matmul(k.bank(c), k.wqkv[:, m * C:(m + 1) * C], tnt[:, c * CH:(c + 1) * CH], start=True, stop=True).then_inc(mm, 1)
            for g in range(NG):
                pe.wait_ge(ev, NCH + g + 1)
                for i in range(4 * g, 4 * g + 4):
                    last = pe.matmul(k.ps[:, i * 128:(i + 1) * 128], tnt[:, i * 128:(i + 1) * 128], k.wqkv[:, 2 * C:3 * C], start=True, stop=True)
                last.then_inc(vmm, 1)
            pe.wait_ge(sq_s, 2)
            pe.wait_ge(vev, 1)
            pe.matmul(k.ps[0:1, 0:1], u, k.ones[:, 0:1], start=True, stop=True).then_inc(umm, 1)

        @block.scalar
        def _(act):
            normalize(k, None, act, TN_AT, T_AT, 1e-5)
            for g in range(NG):
                act.wait_ge(tr, g + 1)
                act.activation(tnt[:, g * CH:(g + 1) * CH], k.bank(g), ACT.Copy).then_inc(tr_ev, 1)
            for m in range(2):
                for c in range(NCH):
                    act.wait_ge(mm, m * NCH + c + 1)
                    act.activation(full[m][:, c * CH:(c + 1) * CH], k.bank(c), ACT.Copy).then_inc(ev, 1)
            act.wait_ge(ss_s, 2)
            act.activation(sc, ssq, ACT.Sqrt).then_inc(sq_s, 1)
            for g in range(NG):
                act.wait_ge(vmm, g + 1)
                act.activation(v[:, g * CH:(g + 1) * CH], k.bank(g), ACT.Copy).then_inc(vev, 1)

        @block.vector
        def _(dve):
            normalize(k, dve, None, TN_AT, T_AT, 1e-5)
            step = Chain(dve, k.sem("v_chain"))
            dve.wait_ge(tr, NG)
            for m in range(2):
                dve.wait_ge(ev, (m + 1) * NCH)
                dve.scalar_tensor_tensor(tn, full[m], 1.0, full[m], ALU.mult, ALU.mult, accum_out=ssq[:, m:m + 1]).then_inc(ss_s, 1)
                dve.wait_ge(ss_s, m + 1)
                step(dve.reduce_max(mx[:, m:m + 1], tn, axis=AX.X))
            dve.wait_ge(sq_s, 1)
            step(dve.tensor_scalar(sc, sc, 1e-12, None, ALU.max))
            step(dve.reciprocal(sc, sc))
            step(dve.tensor_tensor(mx, mx, sc, ALU.mult))
            step(dve.tensor_tensor(mx, mx, sc, ALU.mult))
            step(dve.tensor_tensor(u, mx[:, 0:1], mx[:, 1:2], ALU.mult))
            step(dve.tensor_scalar(sc, sc, SPLIT, None, ALU.mult))
            dve.sem_inc(sq_s, 1)
            for m in range(2):
                step(dve.tensor_scalar(hi[m], full[m], sc[:, m:m + 1], None, ALU.mult))
                dve.scalar_tensor_tensor(lo[m], full[m], sc[:, m:m + 1], hi[m], ALU.mult, ALU.subtract).then_inc(split_s, 1)
            dve.wait_ge(umm, 1)
            dve.tensor_scalar(k.flag[0:1, 0:1], k.ps[0:1, 0:1], (SAFE / SCALE) ** 2 / C, None, ALU.is_gt).then_inc(k.sem("flag"), 1)

        @block.sync
        def _(sp):
            n = 0
            for m in range(2):
                sp.wait_ge(split_s, 2 if m else 1)
                for g in range(4):
                    high = (g < 2) if m == 0 else (g % 2 == 0)
                    for h in range(HEADS):
                        sp.dma_start(stack[m][32 * g:32 * g + 32, h, :], (hi if high else lo)[m][32 * h:32 * h + 32, :]).then_inc(stacked, 16)
                        n += 16
            sp.wait_ge(stacked, n)
    k.clear()


def attend(k):
    qs, ks = (k.at(a, 2 * L).bitcast(F16).rearrange("p (h n) -> p h n", h=HEADS) for a in (QS_AT, KS_AT))
    v, ao = k.at(V_AT, L), k.at(TNT_AT, L)
    probs = [k.at(8192 + i * 2 * CH, 2 * CH) for i in range(8)]
    acc = [k.at(TN_AT + i * 2 * CH, 2 * CH) for i in range(2)]
    rl = k.at(TN_AT + 4 * CH, CH)
    NJ, NPAIR = L // 128, 2 * (L // 128)
    s_mm, exp_s, pv_s, acc_s, l_mm, l_s, norm_s = (k.sem(n) for n in (
        "scores_mm", "probs_ready", "pv_mm", "probs_summed", "sums_mm", "sums_inverse", "chunk_normed"))
    O, LS = 6, 7
    def tensor(pe):
        def weigh(c, j):
            pe.wait_ge(exp_s, c * NPAIR + (2 * j + 2 + 3))
            if j == 0:
                pe.wait_ge(norm_s, c + 1)
            for h in range(HEADS):
                last = pe.matmul(k.ps[32 * h:32 * h + 32, O * CH:(O + 1) * CH], v[:, j * 128 + 32 * h:j * 128 + 32 * h + 32],
                                 probs[(2 * j + h // 2) % 8][:, (h % 2) * CH:(h % 2 + 1) * CH],
                                 start=j == 0, stop=j == NJ - 1, tile_position=(0, 32 * h))
            last.then_inc(pv_s, 1)

        with pe.Fori(0, NCH) as c:
            for j in range(NJ):
                for a in range(2):
                    p = 2 * j + a
                    pe.wait_ge(exp_s, c * NPAIR + (p + 1 if p >= 3 else 3))
                    for e in range(2):
                        h = 2 * a + e
                        last = pe.matmul(k.bank(2 * (p % 3) + e), ks[:, h, j * 128:(j + 1) * 128], qs[:, h, bass.ds(c * CH, CH)],
                                         start=True, stop=True)
                    last.then_inc(s_mm, 1)
                if j >= 1:
                    weigh(c, j - 1)
            weigh(c, NJ - 1)
            pe.wait_ge(acc_s, c * NPAIR + (NPAIR + 8))
            for h in range(HEADS):
                last = pe.matmul(k.ps[32 * h:32 * h + 32, LS * CH:(LS + 1) * CH], k.ones[:, 0:32],
                                 acc[h // 2][:, (h % 2) * CH:(h % 2 + 1) * CH], start=True, stop=True, tile_position=(0, 32 * h))
            last.then_inc(l_mm, 1)

    def scalar(act):
        act.sem_inc(exp_s, 3)
        with act.Fori(0, NCH) as c:
            for p in range(NPAIR):
                act.wait_ge(s_mm, c * NPAIR + (p + 1))
                act.wait_ge(pv_s, c * NJ + (p // 2 + 1))
                act.wait_ge(acc_s, c * NPAIR + (p + 1))
                act.activation(probs[p % 8], k.bank(2 * (p % 3), 2 * CH), ACT.Exp, scale=SCALE / SPLIT ** 2).then_inc(exp_s, 1)

    def vector(dve):
        dve.sem_inc(pv_s, 4)
        dve.sem_inc(acc_s, 8)
        dve.sem_inc(norm_s, 1)
        dve.sem_inc(l_mm, 1)
        with dve.Fori(0, NCH) as c:
            dve.wait_ge(l_mm, c + 1)
            for p in range(NPAIR):
                dve.wait_ge(exp_s, c * NPAIR + (p + 1 + 3))
                if p < 2:
                    dve.tensor_copy(acc[p], probs[p % 8]).then_inc(acc_s, 1)
                else:
                    dve.wait_ge(acc_s, c * NPAIR + (p - 1 + 8))
                    dve.tensor_tensor(acc[p % 2], acc[p % 2], probs[p % 8], ALU.add).then_inc(acc_s, 1)
            dve.wait_ge(l_mm, c + 2)
            dve.reciprocal(rl, k.bank(LS)).then_inc(l_s, 1)
            dve.wait_ge(l_s, c + 1)
            dve.wait_ge(pv_s, c * NJ + (NJ + 4))
            dve.tensor_tensor(ao[:, bass.ds(c * CH, CH)], k.bank(O), rl, ALU.mult).then_inc(norm_s, 1)

    return tensor, scalar, vector


def attend_guarded(k):
    qs, ks = (k.at(a, 2 * L).bitcast(F16).rearrange("p (h n) -> p h n", h=HEADS) for a in (QS_AT, KS_AT))
    v, ao = k.at(V_AT, L), k.at(TNT_AT, L)
    probs = [k.at(8192 + i * 2 * CH, 2 * CH) for i in range(4)]
    mb = k.at(12288, HEADS * CH).rearrange("p (h n) -> p h n", h=HEADS)
    diag, mcol = k.at(14336, 128), k.small[:, 150:151]
    acc = [k.at(TN_AT + i * 2 * CH, 2 * CH) for i in range(2)]
    rl = k.at(TN_AT + 4 * CH, CH)
    NJ, NPAIR, NR = L // 128, 2 * (L // 128), HEADS * CH // 128
    row_mm, max_s, diag_s, spread_mm, mb_s, s_mm, shift_s, exp_s, pv_s, acc_s, l_mm, l_s, norm_s = (k.sem(n) for n in (
        "rows_mm", "max_ready", "diag_ready", "max_spread", "max_saved", "scores_mm", "shifted", "probs_ready", "pv_mm",
        "probs_summed", "sums_mm", "sums_inverse", "chunk_normed"))
    O, LS = 6, 7
    def tensor(pe):
        def weigh(c, j):
            pe.wait_ge(exp_s, c * NPAIR + (2 * j + 2))
            for h in range(HEADS):
                last = pe.matmul(k.ps[32 * h:32 * h + 32, O * CH:(O + 1) * CH], v[:, j * 128 + 32 * h:j * 128 + 32 * h + 32],
                                 probs[(2 * j + h // 2) % 4][:, (h % 2) * CH:(h % 2 + 1) * CH],
                                 start=j == 0, stop=j == NJ - 1, tile_position=(0, 32 * h))
            last.then_inc(pv_s, 1)

        with pe.Fori(0, NCH) as c:
            pe.wait_ge(norm_s, c + 1)
            for r in range(NR):
                h, i = r // 4, r % 4
                pe.wait_ge(mb_s, c * NR + (r + 1))
                for g in range(NCH):
                    last = pe.matmul(k.bank(g), qs[:, h, bass.ds(c * CH + 128 * i, 128)], ks[:, h, g * CH:(g + 1) * CH],
                                     start=True, stop=True)
                last.then_inc(row_mm, 1)
                pe.wait_ge(diag_s, c * NR + (r + 1))
                pe.matmul(k.bank(0, 128), k.ones[:, :], diag, start=True, stop=True).then_inc(spread_mm, 1)
            pe.wait_ge(mb_s, c * NR + (NR + 1))
            for j in range(NJ):
                for a in range(2):
                    p = 2 * j + a
                    pe.wait_ge(shift_s, c * NPAIR + (p + 1 if p >= 3 else 3))
                    for e in range(2):
                        h = 2 * a + e
                        last = pe.matmul(k.bank(2 * (p % 3) + e), ks[:, h, j * 128:(j + 1) * 128], qs[:, h, bass.ds(c * CH, CH)],
                                         start=True, stop=True)
                    last.then_inc(s_mm, 1)
                if j >= 1:
                    weigh(c, j - 1)
            weigh(c, NJ - 1)
            pe.wait_ge(acc_s, c * NPAIR + NPAIR)
            for h in range(HEADS):
                last = pe.matmul(k.ps[32 * h:32 * h + 32, LS * CH:(LS + 1) * CH], k.ones[:, 0:32],
                                 acc[h // 2][:, (h % 2) * CH:(h % 2 + 1) * CH], start=True, stop=True, tile_position=(0, 32 * h))
            last.then_inc(l_mm, 1)

    def scalar(act):
        with act.Fori(0, NCH) as c:
            for p in range(NPAIR):
                act.wait_ge(shift_s, c * NPAIR + (p + 1 + 3))
                act.activation(probs[p % 4], probs[p % 4], ACT.Exp, scale=SCALE / SPLIT ** 2).then_inc(exp_s, 1)

    def vector(dve):
        dve.sem_inc(mb_s, 1)
        dve.sem_inc(shift_s, 3)
        dve.sem_inc(pv_s, 2)
        dve.sem_inc(norm_s, 1)
        with dve.Fori(0, NCH) as c:
            for r in range(NR):
                h, i = r // 4, r % 4
                dve.wait_ge(row_mm, c * NR + (r + 1))
                dve.reduce_max(mcol, k.ps[:, :], axis=AX.X).then_inc(max_s, 1)
                dve.wait_ge(max_s, c * NR + (r + 1))
                dve.tensor_scalar(diag, k.ident[:, :], mcol, None, ALU.mult).then_inc(diag_s, 1)
                dve.wait_ge(spread_mm, c * NR + (r + 1))
                dve.tensor_copy(mb[:, h, 128 * i:128 * i + 128], k.bank(0, 128)).then_inc(mb_s, 1)
            dve.wait_ge(mb_s, c * NR + (NR + 1))

            def add(p):
                dve.wait_ge(exp_s, c * NPAIR + (p + 1))
                if p < 2:
                    dve.tensor_copy(acc[p], probs[p % 4]).then_inc(acc_s, 1)
                else:
                    dve.wait_ge(acc_s, c * NPAIR + (p - 1))
                    dve.tensor_tensor(acc[p % 2], acc[p % 2], probs[p % 4], ALU.add).then_inc(acc_s, 1)

            for p in range(NPAIR):
                a = p % 2
                dve.wait_ge(s_mm, c * NPAIR + (p + 1))
                dve.wait_ge(pv_s, c * NJ + (p // 2 + 1))
                if p >= 4:
                    dve.wait_ge(acc_s, c * NPAIR + (p - 3))
                dve.tensor_tensor(probs[p % 4].rearrange("p (e n) -> p e n", e=2),
                                  k.bank(2 * (p % 3), 2 * CH).rearrange("p (e n) -> p e n", e=2),
                                  mb[:, 2 * a:2 * a + 2, :], ALU.subtract).then_inc(shift_s, 1)
                if p >= 1:
                    add(p - 1)
            add(NPAIR - 1)
            dve.wait_ge(l_mm, c + 1)
            dve.reciprocal(rl, k.bank(LS)).then_inc(l_s, 1)
            dve.wait_ge(l_s, c + 1)
            dve.wait_ge(pv_s, c * NJ + (NJ + 2))
            dve.tensor_tensor(ao[:, bass.ds(c * CH, CH)], k.bank(O), rl, ALU.mult).then_inc(norm_s, 1)
            dve.wait_ge(norm_s, c + 2)

    return tensor, scalar, vector


def attention_out(k):
    nc = k.nc
    t1, ao = k.at(T_AT, L), k.at(TNT_AT, L)
    o_mm, t_s = k.sem("outproj_mm"), k.sem("tokens_ready")
    with nc.Block() as block:
        @block.tensor
        def _(pe):
            for g in range(NT // 4):
                pe.matmul(k.bank(g), k.ones[0:1, :], k.brow[0:1, :, :].rearrange("a q c -> a (q c)"), start=True, stop=False)
                for i in range(4):
                    at = g * CH + 128 * i
                    last = pe.matmul(k.bank(g, 128, 128 * i), ao[:, at:at + 128], k.wout[:, :], start=False, stop=i == 3)
                last.then_inc(o_mm, 1)

        @block.vector
        def _(dve):
            for g in range(NT // 4):
                dve.wait_ge(o_mm, g + 1)
                dve.tensor_tensor(t1[:, g * CH:(g + 1) * CH], t1[:, g * CH:(g + 1) * CH], k.bank(g), ALU.add).then_inc(t_s, 1)
    k.clear()


def attention(k):
    guarded, bounded = attend_guarded(k), attend(k)
    with k.nc.Block() as block:
        @block.tensor
        def _(pe):
            need = pe.value_load(k.flag[0:1, 0:1], min_val=0, max_val=1)
            with pe.If(need == 1):
                guarded[0](pe)
            with pe.Else():
                bounded[0](pe)
            pe.drain()

        @block.scalar
        def _(act):
            need = act.value_load(k.flag[0:1, 0:1], min_val=0, max_val=1)
            with act.If(need == 1):
                guarded[1](act)
            with act.Else():
                bounded[1](act)
            act.drain()

        @block.vector
        def _(dve):
            need = dve.value_load(k.flag[0:1, 0:1], min_val=0, max_val=1)
            with dve.If(need == 1):
                guarded[2](dve)
            with dve.Else():
                bounded[2](dve)
            dve.drain()
    k.clear()
    attention_out(k)


def ffn(k, b):
    nc = k.nc
    t1, tn, tnt, img = k.at(T_AT, L), k.at(TN_AT, L), k.at(0, L), k.at(4096, L)
    E0 = 8192
    names = ("ex", "c1", "oh1", "e2", "oh2", "gate", "tmp")
    small = {n: k.at(E0 + i * 256, NT * NE).rearrange("p (i e) -> p i e", e=NE) for i, n in enumerate(names)}
    gpad = k.at(E0 + 2048, NT * 32).rearrange("p (i e) -> p i e", e=32)
    gt = k.at(E0 + 3072, 1024)
    cols = k.at(E0 + 4096, 256)
    m1, m2, den = (cols[:, i * NT:(i + 1) * NT] for i in range(3))
    prod = [k.at(E0 + 4352 + i * 1024, NE * C).rearrange("p (e c) -> p e c", e=NE) for i in range(4)]
    tn_s, tr, tr_ev, lg, lc, ex_s = (k.sem(n) for n in ("ln_done", "tr_done", "tnt_ready", "logits_mm", "logits_ready", "exp_done"))
    gp, gz, gtm, gte, bmm, bad = (k.sem(n) for n in ("gates_ready", "gates_zero", "gates_tr", "gates_out", "bias_mm", "bias_added"))
    emm, ml, hs, ts, fm, fe, out_s = (k.sem(n) for n in (
        "experts_mm", "weighted", "halved", "tile_added", "final_tr", "final_out", "stored"))
    NG = NT // 4

    def spread(col):
        return col.unsqueeze(2).broadcast_to([128, NT, NE])

    with nc.Block() as block:
        @block.tensor
        def _(pe):
            for i in range(NT):
                pe.wait_ge(tn_s, i + 1)
                last = pe.transpose(k.ps[:, i * 128:(i + 1) * 128], tn[:, i * 128:(i + 1) * 128], k.ident[:, :])
                if i % 4 == 3:
                    last.then_inc(tr, 1)
            pe.wait_ge(tr_ev, NG)
            for i in range(NT):
                last = pe.matmul(k.bank(0, NE, NE * i), tnt[:, i * 128:(i + 1) * 128], k.routw[:, :], start=True, stop=True)
            last.then_inc(lg, 1)
            pe.wait_ge(gp, 1)
            for q in range(NT // 4):
                last = pe.transpose(k.bank(1 + q // 4, 128, 128 * (q % 4)), gpad[:, 4 * q:4 * q + 4, :].rearrange("p i e -> p (i e)"), k.ident[:, :])
            last.then_inc(gtm, 1)
            pe.wait_ge(gte, 1)
            for g in range(NG):
                for i in range(4):
                    last = pe.matmul(k.bank(g, 128, 128 * i), gt[:, g * 128:(g + 1) * 128], k.expb[:, i, :], start=True, stop=True)
                last.then_inc(bmm, 1)
            for i in range(NT):
                if i < 4:
                    pe.wait_ge(bad, NG)
                else:
                    pe.wait_ge(ml, i - 3)
                for hb in range(2):
                    last = pe.matmul(k.bank(2 * (i % 4) + hb), tnt[:, i * 128:(i + 1) * 128],
                                     k.expw[:, hb * 4:hb * 4 + 4, :].rearrange("p e c -> p (e c)"), start=True, stop=True)
                last.then_inc(emm, 1)
            for g in range(NG):
                pe.wait_ge(ml, NT)
                pe.wait_ge(ts, 2 * (4 * g + 4))
                for i in range(4 * g, 4 * g + 4):
                    last = pe.transpose(k.ps[:, i * 128:(i + 1) * 128], t1[:, i * 128:(i + 1) * 128], k.ident[:, :])
                last.then_inc(fm, 1)

        @block.scalar
        def _(act):
            normalize(k, None, act, TN_AT, T_AT, 1e-5)
            for g in range(NG):
                act.wait_ge(tr, g + 1)
                act.activation(tnt[:, g * CH:(g + 1) * CH], k.bank(g), ACT.Copy).then_inc(tr_ev, 1)
            act.wait_ge(lc, 1)
            act.activation(small["ex"], small["tmp"], ACT.Exp).then_inc(ex_s, 1)
            act.wait_ge(gtm, 1)
            act.activation(gt, k.ps[:, CH:3 * CH], ACT.Copy).then_inc(gte, 1)
            for g in range(NG):
                act.wait_ge(fm, g + 1)
                act.activation(patch_order(img, g // PS, g % PS), k.bank(g).rearrange("p (x h w) -> p x h w", x=PS, w=W // PS), ACT.Copy).then_inc(fe, 1)

        @block.gpsimd
        def _(pool):
            pool.memset(gpad, 0.0).then_inc(gz, 1)
            for i in range(NT):
                pool.wait_ge(ml, i + 1)
                t = prod[i % 4]
                pool.tensor_tensor(t[:, 0:4, :], t[:, 0:4, :], t[:, 4:8, :], ALU.add).then_inc(hs, 1)
                pool.wait_ge(hs, 2 * i + 1)
                pool.tensor_tensor(t[:, 0:2, :], t[:, 0:2, :], t[:, 2:4, :], ALU.add).then_inc(hs, 1)

        @block.vector
        def _(dve):
            normalize(k, dve, None, TN_AT, T_AT, 1e-5)
            step = Chain(dve, k.sem("v_chain"))
            ex, c1, oh1, e2, oh2, gate, tmp = (small[n] for n in names)
            dve.wait_ge(lg, 1)
            step(dve.tensor_tensor(tmp, k.bank(0, NT * NE).rearrange("p (i e) -> p i e", e=NE), k.rtb[:, :].unsqueeze(1).broadcast_to([128, NT, NE]), ALU.add))
            step(dve.reduce_max(m1, tmp, axis=AX.X))
            dve.tensor_tensor(tmp, tmp, spread(m1), ALU.subtract).then_inc(lc, 1)
            dve.wait_ge(ex_s, 1)
            order = k.rank8[:, :].unsqueeze(1).broadcast_to([128, NT, NE])

            def first_max(src, top, onehot):
                step(dve.reduce_max(top, src, axis=AX.X))
                step(dve.tensor_tensor(c1, src, spread(top), ALU.is_equal))
                step(dve.tensor_tensor(c1, c1, order, ALU.mult))
                step(dve.reduce_max(den, c1, axis=AX.X))
                step(dve.tensor_tensor(onehot, c1, spread(den), ALU.is_equal))

            first_max(ex, m1, oh1)
            step(dve.scalar_tensor_tensor(e2, oh1, -4.0, ex, ALU.mult, ALU.add))
            first_max(e2, m2, oh2)
            step(dve.tensor_tensor(den, m1, m2, ALU.add))
            step(dve.reciprocal(den, den))
            step(dve.tensor_tensor(gate, oh1, oh2, ALU.add))
            step(dve.tensor_tensor(gate, gate, ex, ALU.mult))
            step(dve.tensor_tensor(gate, gate, spread(den), ALU.mult))
            dve.wait_ge(gz, 1)
            dve.tensor_copy(gpad[:, :, 0:NE], gate).then_inc(gp, 1)
            for g in range(NG):
                dve.wait_ge(bmm, g + 1)
                dve.tensor_tensor(t1[:, g * CH:(g + 1) * CH], t1[:, g * CH:(g + 1) * CH], k.bank(g), ALU.add).then_inc(bad, 1)

            def finish(i):
                dve.wait_ge(hs, 2 * i + 2)
                t = prod[i % 4]
                tile = t1[:, i * 128:(i + 1) * 128]
                dve.tensor_tensor(tile, tile, t[:, 0, :], ALU.add).then_inc(ts, 1)
                dve.wait_ge(ts, 2 * i + 1)
                dve.tensor_tensor(tile, tile, t[:, 1, :], ALU.add).then_inc(ts, 1)

            dve.wait_ge(bad, NG)
            for i in range(NT):
                dve.wait_ge(emm, i + 1)
                if i >= 4:
                    dve.wait_ge(ts, 2 * (i - 3))
                dve.tensor_tensor(prod[i % 4], k.bank(2 * (i % 4), 2 * CH).rearrange("p (e c) -> p e c", e=NE),
                                  gate[:, i, :].unsqueeze(2).broadcast_to([128, NE, C]), ALU.mult).then_inc(ml, 1)
                if i >= 3:
                    finish(i - 3)
            for i in range(NT - 3, NT):
                finish(i)

        @block.sync
        def _(sp):
            sp.wait_ge(fe, NG // 2)
            sp.dma_start(k.out[b, :, 0:L // 2], img[:, 0:L // 2]).then_inc(out_s, 16)
            sp.wait_ge(fe, NG)
            sp.dma_start(k.out[b, :, L // 2:L], img[:, L // 2:L]).then_inc(out_s, 16)
            sp.wait_ge(out_s, 32)
    k.clear()


def program(nc, ins, out):
    with ExitStack() as ctx:
        k = Kernel(nc, ctx, ins, out)
        setup(k)
        with nc.Fori(0, B) as b:
            score(k, b)
            sort_tokens(k)
            project(k)
            scan(k)
            unsort(k, b)
            qkv(k)
            attention(k)
            ffn(k, b)


TRANSPOSED = {
    "in_projT": "L0_conv_in_proj_w", "out_projT": "L0_conv_out_proj_w", "x_projT": "L0_conv_x_proj_w",
    "dt_projT": "L0_conv_dt_proj_w", "ca1T": "L0_conv_ca1_w", "ca2T": "L0_conv_ca2_w",
}


def kernel(**inputs):
    import concourse.bacc as bacc
    from concourse.bass_utils import run_bass_kernel_spmd

    arrays = {n: np.ascontiguousarray(a) for n, a in inputs.items() if n not in TRANSPOSED.values()}
    arrays["x"] = arrays["x"].reshape(B, C, L)
    arrays["pe"] = arrays.pop("L0_conv_pe")
    for name, source in TRANSPOSED.items():
        arrays[name] = np.ascontiguousarray(np.asarray(inputs[source]).T)
    nc = bacc.Bacc("TRN2", target_bir_lowering=False, num_devices=1)
    ins = {n: nc.dram_tensor(n, a.shape, mybir.dt.from_np(a.dtype), kind="ExternalInput").ap() for n, a in arrays.items()}
    out = nc.dram_tensor("out", (B, C, L), F32, kind="ExternalOutput").ap()
    program(nc, ins, out)
    r = run_bass_kernel_spmd(nc, [arrays], core_ids=[0])
    return r.results[0]["out"].reshape(B, C, H, W)
```

```python
import numpy as np
import concourse.bass as bass
from concourse import mybir
from contextlib import ExitStack

F32, BF16, F16, I32 = mybir.dt.float32, mybir.dt.bfloat16, mybir.dt.float16, mybir.dt.int32
ALU, ACT, AX = mybir.AluOpType, mybir.ActivationFunctionType, mybir.AxisListType

B, C, H, W = 4, 128, 64, 64
L = H * W
PS = 4
NP_ = (H // PS) * (W // PS)
TT = NP_ // 128
OFF = PS * PS
NT = TT * OFF
DI, DS, DR, DC = 2 * C, 16, C // 16, 4
HD = DI // 128
CH = 512
NCH = L // CH
PW = W + 2
HEADS, DH = 4, 32
SCALE = 10.0
NE = 8
SPLIT = 4096.0
SAFE = 60.0


ARENA = 44032


class Chain:

    def __init__(self, eng, sem):
        self.eng, self.sem, self.n = eng, sem, 0

    def __call__(self, ins):
        self.n += 1
        ins.then_inc(self.sem, 1)
        self.eng.wait_ge(self.sem, self.n)


class Kernel:

    def __init__(self, nc, ctx, ins, out, batches=B):
        self.nc, self.ctx, self.ins, self.out, self.batches = nc, ctx, ins, out, batches
        self.sems = {}

        def sb(name, shape, dt=F32):
            return ctx.enter_context(nc.sbuf_tensor(name, shape, dt))

        self.ident = sb("ident", [128, 128])
        self.group = sb("group", [128, 32, 4])
        self.wz = sb("wz", [128, DI])
        self.tapw = sb("tapw", [128, DC, DI])
        self.xpw = sb("xpw", [128, HD, 128])
        self.dtw = sb("dtw", [128, DI])
        self.sel = sb("sel", [128, 32, 128], BF16)
        self.outw = sb("outw", [128, HD, C])
        self.wqkv = sb("wqkv", [128, 3 * C])
        self.wout = sb("wout", [128, C])
        self.expw = sb("expw", [128, NE, C])
        self.expb = sb("expb", [128, 4, C])
        self.routw = sb("routw", [128, NE])
        self.iota = sb("iota", [128, NP_], BF16)
        self.lower = sb("lower", [128, TT, NP_], BF16)
        self.mask8 = sb("mask8", [NCH, NCH, 32], BF16)
        self.hwin = sb("hwin", [128, 2 * NCH - 1])
        self.owin = sb("owin", [128, 2 * NCH - 1])
        self.ca1 = sb("ca1", [128, C // 4])
        self.ca2 = sb("ca2", [C // 4, C])
        self.brow = sb("brow", [1, 4, C])
        self.ones = sb("ones", [128, 128])
        self.cols = sb("cols", [128, 64])
        self.convw = sb("convw", [128, 2, 9])
        self.amat = sb("amat", [128, HD, DS])
        self.rtb = sb("rtb", [128, NE])
        self.rank8 = sb("rank8", [128, NE])
        self.perm = sb("perm", [128, TT, NP_])
        self.permt = sb("permt", [128, TT, NP_])
        self.hlast = sb("hlast", [128, DS, HD, 1])
        self.small = sb("small", [128, 160])
        self.flag = sb("flag", [1, 1], I32)
        self.R = sb("arena", [128, ARENA])
        self.ps = ctx.enter_context(nc.psum_tensor("ps", [128, 8 * CH], F32))

    def sem(self, name):
        if name not in self.sems:
            self.sems[name] = self.ctx.enter_context(self.nc.semaphore(name))
        return self.sems[name]

    def clear(self):
        nums = [s.num for s in self.sems.values()]
        self.nc.all_engine_barrier(sems_to_clear=range(min(nums), max(nums) + 1))

    def bank(self, n, cols=CH, at=0):
        return self.ps[:, n * CH + at:n * CH + at + cols]

    def at(self, off, n):
        return self.R[:, off:off + n]


C_B1, C_B2, C_G, C_NB, C_HB, C_CB, C_DTB, C_D, C_ONE = 0, 1, 2, 3, 4, 5, 7, 9, 11


def patch_order(image, t, y):
    rows = H // TT
    v = image[:, t * rows * W:(t + 1) * rows * W].rearrange("p (h y w x) -> p y x h w", y=PS, w=W // PS, x=PS)
    return v[:, y]


def patch_tiles(tiles, t, y):
    n = PS * 128
    at = (t * PS + y) * n
    return tiles[:, at:at + n].rearrange("p (x h w) -> p x h w", x=PS, w=W // PS)


def setup(k):
    nc, w = k.nc, k.ins
    loaded, zeroed, built, made = k.sem("weights_loaded"), k.sem("zeroed"), k.sem("masks_built"), k.sem("made")
    taps = k.at(0, DI * DC)
    pieces = []

    def col(name, at):
        return (k.cols[:, at:at + 1], w[name].rearrange("(p a) -> p a", a=1))

    pieces += [col("L0_conv_conv1_b", C_B1), col("L0_conv_conv2_b", C_B2), col("L0_conv_norm_g", C_G), col("L0_conv_norm_b", C_NB)]
    for n, at in (("L0_conv_conv1d_b", C_CB), ("L0_conv_dt_proj_b", C_DTB), ("L0_conv_D", C_D)):
        for h in range(HD):
            pieces.append((k.cols[:, at + h:at + h + 1], w[n][h * 128:(h + 1) * 128].rearrange("(p a) -> p a", a=1)))
    pieces.append((k.cols[:, C_HB:C_HB + 1], w["L0_conv_head_b"].partition_broadcast(128)))
    pieces.append((k.convw[:, 0, :], w["L0_conv_conv1_w"].rearrange("c a y x -> c (a y x)")))
    pieces.append((k.convw[:, 1, :], w["L0_conv_conv2_w"].rearrange("c a y x -> c (a y x)")))
    pieces.append((k.tapw[:, 0, :], w["in_projT"][:, 0:DI]))
    pieces.append((k.wz[:, :], w["in_projT"][:, DI:2 * DI]))
    pieces.append((taps, w["L0_conv_conv1d_w"].rearrange("d k -> (d k)").partition_broadcast(128)))
    pieces.append((k.outw[:, :, :], w["out_projT"].rearrange("(h p) c -> p h c", h=HD)))
    pieces.append((k.wqkv[:, :], w["L1_attn_W_qkv"]))
    pieces.append((k.wout[:, :], w["L1_attn_W_out"]))
    pieces.append((k.routw[:, :], w["L1_ffn_router_w"]))
    pieces.append((k.rtb[:, :], w["L1_ffn_router_b"].partition_broadcast(128)))
    pieces.append((k.expw[:, :, :], w["L1_ffn_expert_w"].rearrange("e d c -> d e c")))
    pieces.append((k.ca1[:, :], w["ca1T"]))
    pieces.append((k.ca2[:, :], w["ca2T"]))
    pieces.append((k.amat[:, :, :], w["L0_conv_A_log"].rearrange("(h p) s -> p h s", h=HD)))
    for q in range(4):
        pieces.append((k.brow[0:1, q, :], w["L1_attn_b_out"].rearrange("(a c) -> a c", a=1)))
    late = [(k.hwin[:, NCH - 1:NCH], w["L0_conv_head_w"].rearrange("a c -> c a"))]
    for g in range(3):
        for h in range(HD):
            late.append((k.xpw[:, h, 32 * g:32 * g + 32], w["x_projT"][h * 128:(h + 1) * 128, DR:DR + 2 * DS]))
    for h in range(HD):
        late.append((k.xpw[:, h, 96:96 + DR], w["x_projT"][h * 128:(h + 1) * 128, 0:DR]))
    late.append((k.dtw[96:96 + DR, :], w["dt_projT"]))
    for q in range(4):
        late.append((k.expb[32 * q:32 * q + NE, q, :], w["L1_ffn_expert_b"]))
    total = 16 * (len(pieces) + len(late))

    with nc.Block() as block:
        @block.sync
        def _(sp):
            for dst, src in pieces:
                sp.dma_start(dst, src, allow_slow_non_contiguous=True).then_inc(loaded, 16)
            sp.wait_ge(zeroed, 5)
            for dst, src in late:
                sp.dma_start(dst, src, allow_slow_non_contiguous=True).then_inc(loaded, 16)

        @block.gpsimd
        def _(pool):
            step = Chain(pool, built)
            step(pool.memset(k.ident[:, :], 0.0))
            step(pool.affine_select(out=k.ident[:, :], in_=k.ident[:, :], compare_op=ALU.not_equal, fill=1.0,
                                    base=0, pattern=[[-1, 128]], channel_multiplier=1))
            step(pool.memset(k.group[:, :, :], 0.25))
            step(pool.affine_select(out=k.group[:, :, :], in_=k.group[:, :, :], compare_op=ALU.is_ge, fill=0.0,
                                    base=0, pattern=[[-4, 32], [0, 4]], channel_multiplier=1))
            step(pool.affine_select(out=k.group[:, :, :], in_=k.group[:, :, :], compare_op=ALU.is_ge, fill=0.0,
                                    base=3, pattern=[[4, 32], [0, 4]], channel_multiplier=-1))
            step(pool.memset(k.sel[:, :, :], 0.0))
            for g in range(3):
                v = k.sel[32 * g:32 * g + 32, :, :]
                step(pool.affine_select(out=v, in_=v, compare_op=ALU.not_equal, fill=1.0,
                                        base=0, pattern=[[-1, 32], [0, 128]], channel_multiplier=1))
            step(pool.iota(k.iota[:, :], [[1, NP_]], base=0, channel_multiplier=0, allow_small_or_imprecise_dtypes=True))
            step(pool.iota(k.rank8[:, :], [[-1, NE]], base=NE, channel_multiplier=0, allow_small_or_imprecise_dtypes=True))
            step(pool.memset(k.lower[:, :, :], 1.0))
            step(pool.affine_select(out=k.lower[:, :, :], in_=k.lower[:, :, :], compare_op=ALU.is_gt, fill=0.0,
                                    base=0, pattern=[[128, TT], [-1, NP_]], channel_multiplier=1))
            step(pool.memset(k.mask8[:, :, :], 0.0))
            step(pool.affine_select(out=k.mask8[:, :, :], in_=k.mask8[:, :, :], compare_op=ALU.not_equal, fill=1.0,
                                    base=0, pattern=[[-1, NCH], [0, 32]], channel_multiplier=1))
            step(pool.memset(k.owin[:, :], 0.0))
            step(pool.memset(k.owin[:, NCH - 1:NCH], 1.0))
            step(pool.memset(k.ones[:, :], 1.0))
            step(pool.memset(k.cols[:, C_ONE:C_ONE + 1], 1.0))

        @block.vector
        def _(dve):
            for t in (k.hwin[:, :], k.xpw[:, :, :], k.dtw[:, :], k.expb[:, :, :], k.small[:, :]):
                dve.memset(t, 0.0).then_inc(zeroed, 1)
            dve.wait_ge(loaded, total)
            tv = taps.rearrange("p (d k) -> p k d", k=DC)
            for t in range(DC - 1, -1, -1):
                if t == 0:
                    dve.wait_ge(made, DC - 1)
                dve.tensor_tensor(k.tapw[:, t, :], k.tapw[:, 0, :], tv[:, t, :], ALU.mult).then_inc(made, 1)

        @block.scalar
        def _(act):
            step = Chain(act, k.sem("a_made"))
            act.wait_ge(loaded, total)
            step(act.activation(k.amat[:, :, :], k.amat[:, :, :], ACT.Exp))
            step(act.mul(k.amat[:, :, :], k.amat[:, :, :], -1.0))
    k.clear()


X_AT, PAD1_AT, PAD2_AT, FEAT_AT, SQ_AT, XT_AT, PE_AT, X1_AT, XP_AT, DIAG_AT = 0, 4096, 8704, 13312, 17408, 21504, 25600, 29696, 33800, 37896
X1_PAD = 8


def score(k, b):
    nc = k.nc
    x = k.at(X_AT, L)
    pad = [k.at(o, PW * PW).rearrange("p (h w) -> p h w", w=PW) for o in (PAD1_AT, PAD2_AT)]
    inner = [p[:, 1:H + 1, 1:W + 1] for p in pad]
    feat, sq, xp = k.at(FEAT_AT, L), k.at(SQ_AT, L), k.at(XP_AT, L)
    RC = CH // W
    S = k.small
    stats = S[:, 0:48].rearrange("p (n s) -> p n s", s=6)
    mv, g2, gm, rstd, t0, t1 = S[:, 48:50], S[:, 50:52], S[:, 52:53], S[:, 53:54], S[:, 54:55], S[:, 55:56]
    csum, ctot, hid, ca = S[:, 56:64], S[:, 64:65], S[0:C // 4, 65:66], S[:, 66:67]
    colv, rank = S[:, 68:70], S[:, 70:72]
    diag = k.at(DIAG_AT, 2 * 9 * 128).rearrange("p (i t n) -> p i t n", i=2, t=9)
    work = k.at(X1_AT, 4096)
    rows = [work[0:NCH, i * CH:(i + 1) * CH] for i in range(6)]
    bd = work[0:NCH, 3072:3072 + NP_].rearrange("p (n q) -> p n q", q=32)
    smb, junk = work[:, 3328:3328 + NP_], work[:, 3584:3584 + NP_]
    x_in, pe_in = k.sem("x_in"), k.sem("pe_in")
    border, gn_in, gn_sum, gn_var, gn_std, xn = (k.sem(n) for n in ("borders_zero", "gn_in", "gn_sum", "gn_var", "gn_std", "xn_ready"))
    conv = [k.sem("conv1_done"), k.sem("conv2_done")]
    gelu = [k.sem("gelu1_done"), k.sem("gelu2_done")]
    csm, hmm, hre, amm, ca_s, scaled, sq_s = (k.sem(n) for n in ("csum_ready", "hid_mm", "hid_relu", "att_mm", "att_ready", "feat_scaled", "squares"))
    head, sigs, pv, bd_s, bc, pm, pt = (k.sem(n) for n in ("head_mm", "sigmoids", "pv_ready", "scores_spread", "scores_bcast", "perm_ready", "permt_mm"))
    vch, diag_s = k.sem("v_chain"), k.sem("diag_ready")

    with nc.Block() as block:
        @block.sync
        def _(sp):
            for i in range(4):
                sp.dma_start(x[:, i * 1024:(i + 1) * 1024], k.ins["x"][b, :, i * 1024:(i + 1) * 1024]).then_inc(x_in, 16)
            pe_v = k.ins["pe"].rearrange("(t h y w x) c -> t y h w (x c)", t=TT, y=PS, w=W // PS, x=PS)
            dst = k.at(PE_AT, L).rearrange("p (t y n) -> p t y n", t=TT, y=PS)
            for t in range(TT):
                for y in range(PS):
                    for h in range(8):
                        sp.dma_start(dst[16 * h:16 * h + 16, t, y, :], pe_v[t, y, h]).then_inc(pe_in, 16)
            sp.wait_ge(pe_in, 16 * TT * PS * 8)

        @block.gpsimd
        def _(pool):
            for p in pad:
                pool.memset(p[:, 0:PW:PW - 1, :], 0.0).then_inc(border, 1)
                pool.memset(p[:, 1:H + 1, 0:PW:PW - 1], 0.0).then_inc(border, 1)
            pool.wait_ge(xn, 1)
            for t in range(TT):
                for y in range(PS):
                    pool.tensor_scalar(patch_tiles(xp, t, y), patch_order(x, t, y), gm, rstd, ALU.subtract, ALU.mult)\
                        .then_inc(k.sem("patches_ready"), 1)

        @block.vector
        def _(dve):
            step = Chain(dve, vch)
            for n in range(2):
                for t in range(9):
                    dve.tensor_scalar(diag[:, n, t, :], k.ident[:, :], k.convw[:, n, t:t + 1], None, ALU.mult).then_inc(diag_s, 1)
            for n in range(NCH):
                dve.wait_ge(x_in, 64)
                step(dve.bn_stats(stats[:, n, :], x[:, n * CH:(n + 1) * CH]))
            step(dve.bn_aggr(mv, stats))
            step(dve.tensor_copy(g2[:, 0:1], mv[:, 0:1]))
            dve.scalar_tensor_tensor(g2[:, 1:2], mv[:, 0:1], mv[:, 0:1], mv[:, 1:2], ALU.mult, ALU.add).then_inc(gn_in, 1)
            dve.wait_ge(gn_sum, 1)
            step(dve.tensor_copy(gm, k.bank(0, 1)))
            step(dve.tensor_tensor(t0, gm, gm, ALU.mult))
            step(dve.tensor_tensor(t0, k.bank(0, 1, 1), t0, ALU.subtract))
            dve.tensor_scalar(t0, t0, 1e-5, None, ALU.add).then_inc(gn_var, 1)
            dve.wait_ge(gn_std, 1)
            step(dve.reciprocal(rstd, rstd))
            step(dve.tensor_tensor(t1, rstd, rstd, ALU.mult))
            step(dve.tensor_tensor(t1, t1, t0, ALU.mult))
            step(dve.tensor_scalar(t1, t1, -0.5, 1.5, ALU.mult, ALU.add))
            step(dve.tensor_tensor(rstd, rstd, t1, ALU.mult))
            dve.wait_ge(border, 4)
            dve.tensor_scalar(inner[0], x.rearrange("p (h w) -> p h w", w=W), gm, rstd, ALU.subtract, ALU.mult).then_inc(xn, 1)
            dve.wait_ge(gelu[0], NCH)
            step(dve.reduce_sum(ctot, csum, axis=AX.X))
            dve.tensor_scalar(ctot, ctot, 1.0 / L, None, ALU.mult).then_inc(csm, 1)
            dve.wait_ge(hmm, 1)
            dve.tensor_scalar(hid, k.ps[0:C // 4, 0:1], 0.0, None, ALU.max).then_inc(hre, 1)
            dve.wait_ge(ca_s, 1)
            dve.tensor_scalar(inner[1], inner[1], ca, None, ALU.mult).then_inc(scaled, 1)
            dve.wait_ge(head, 3)
            step(dve.tensor_copy(rows[0], k.ps[0:NCH, CH:2 * CH]))
            step(dve.scalar_tensor_tensor(rows[1], rows[0], -1.0 / C, rows[0], ALU.mult, ALU.mult))
            dve.tensor_tensor(rows[1], k.ps[0:NCH, 2 * CH:3 * CH], rows[1], ALU.add).then_inc(pv, 1)
            dve.wait_ge(sigs, 2)
            step(dve.tensor_scalar(rows[3], rows[3], 0.3, None, ALU.mult))
            step(dve.scalar_tensor_tensor(rows[4], rows[2], 0.7, rows[3], ALU.mult, ALU.add))
            step(dve.reduce_sum(rows[5][:, 0:128], rows[4].rearrange("p (n x) -> p n x", x=PS), axis=AX.X))
            step(dve.reduce_sum(rows[0][:, 0:32].rearrange("p (h w) -> p h w", h=2),
                                rows[5][:, 0:128].rearrange("p (h y w) -> p h w y", h=2, y=PS), axis=AX.X))
            dve.scalar_tensor_tensor(bd, rows[0][:, 0:32].unsqueeze(1).broadcast_to([NCH, NCH, 32]), 1.0 / OFF,
                                     k.mask8[:, :, :], ALU.mult, ALU.mult).then_inc(bd_s, 1)
            dve.wait_ge(bc, 1)
            step(dve.tensor_copy(smb, k.bank(3, NP_)))
            for t in range(TT):
                step(dve.scalar_tensor_tensor(junk[:, 0:128], smb[:, 128 * t:128 * t + 128], 1.0, k.ident[:, :],
                                              ALU.mult, ALU.mult, accum_out=colv[:, t:t + 1]))
                step(dve.scalar_tensor_tensor(junk, smb, colv[:, t:t + 1], k.lower[:, t, :], ALU.is_equal, ALU.mult))
                step(dve.scalar_tensor_tensor(junk, smb, colv[:, t:t + 1], junk, ALU.is_gt, ALU.add,
                                              accum_out=rank[:, t:t + 1]))
                dve.tensor_scalar(k.perm[:, t, :], k.iota[:, :], rank[:, t:t + 1], None, ALU.is_equal).then_inc(pm, 1)
            dve.wait_ge(pt, 1)
            dve.tensor_copy(k.permt[:, :, :].rearrange("p a b -> p (a b)"), k.bank(4)).then_inc(vch, 1)

        @block.scalar
        def _(act):
            act.wait_ge(gn_var, 1)
            act.activation(rstd, t0, ACT.Sqrt).then_inc(gn_std, 1)
            act.wait_ge(xn, 1)
            for i in range(2):
                if i == 1:
                    act.wait_ge(amm, 1)
                    act.activation(ca, k.bank(1, 1), ACT.Sigmoid).then_inc(ca_s, 1)
                for n in range(NCH):
                    act.wait_ge(conv[i], n + 1)
                    if i == 0:
                        act.wait_ge(border, 4)
                        act.activation(pad[1][:, 1 + RC * n:1 + RC * n + RC, 1:W + 1],
                                       k.bank(n).rearrange("p (h w) -> p h w", w=W), ACT.Gelu,
                                       bias=k.cols[:, C_B1:C_B1 + 1], accum_out=csum[:, n:n + 1]).then_inc(gelu[0], 1)
                    else:
                        act.activation(feat[:, n * CH:(n + 1) * CH], k.bank(n), ACT.Gelu,
                                       bias=k.cols[:, C_B2:C_B2 + 1]).then_inc(gelu[1], 1)
                if i == 0:
                    act.activation(sq.rearrange("p (h w) -> p h w", w=W), inner[0], ACT.Square).then_inc(sq_s, 1)
            act.wait_ge(head, 1)
            act.activation(rows[2], k.ps[0:NCH, 0:CH], ACT.Sigmoid, bias=k.cols[0:NCH, C_HB:C_HB + 1]).then_inc(sigs, 1)
            act.wait_ge(pv, 1)
            act.activation(rows[3], rows[1], ACT.Sigmoid, scale=10.0 / (C - 1)).then_inc(sigs, 1)

        @block.tensor
        def _(pe):
            pe.wait_ge(gn_in, 1)
            pe.matmul(k.bank(0, 2), k.group[:, :, :].rearrange("p a b -> p (a b)"), g2, start=True, stop=True).then_inc(gn_sum, 1)
            pe.wait_ge(diag_s, 2 * 9)
            pe.wait_ge(xn, 1)
            for i in range(2):
                if i == 1:
                    pe.wait_ge(csm, 1)
                    pe.matmul(k.ps[0:C // 4, 0:1], k.ca1[:, :], ctot, start=True, stop=True).then_inc(hmm, 1)
                    pe.wait_ge(hre, 1)
                    pe.matmul(k.bank(1, 1), k.ca2[:, :], hid, start=True, stop=True).then_inc(amm, 1)
                    pe.wait_ge(scaled, 1)
                for n in range(NCH):
                    for t in range(9):
                        y, xx = t // 3, t % 3
                        last = pe.matmul(k.bank(n).rearrange("p (h w) -> p h w", w=W), diag[:, i, t, :],
                                         pad[i][:, RC * n + y:RC * n + y + RC, xx:xx + W], start=t == 0, stop=t == 8)
                    last.then_inc(conv[i], 1)
            pe.wait_ge(gelu[1], NCH)
            for n in range(NCH):
                last = pe.matmul(k.ps[0:NCH, 0:CH], k.hwin[:, NCH - 1 - n:2 * NCH - 1 - n], feat[:, n * CH:(n + 1) * CH],
                                 start=n == 0, stop=n == NCH - 1)
            last.then_inc(head, 1)
            for n in range(NCH):
                last = pe.matmul(k.ps[0:NCH, CH:2 * CH].rearrange("p (h w) -> p h w", w=W), k.owin[:, NCH - 1 - n:2 * NCH - 1 - n],
                                 pad[0][:, 1 + RC * n:1 + RC * n + RC, 1:W + 1], start=n == 0, stop=n == NCH - 1)
            last.then_inc(head, 1)
            pe.wait_ge(sq_s, 1)
            for n in range(NCH):
                last = pe.matmul(k.ps[0:NCH, 2 * CH:3 * CH], k.owin[:, NCH - 1 - n:2 * NCH - 1 - n], sq[:, n * CH:(n + 1) * CH],
                                 start=n == 0, stop=n == NCH - 1)
            last.then_inc(head, 1)
            pe.wait_ge(bd_s, 1)
            pe.matmul(k.bank(3, NP_), k.ones[0:NCH, :], bd.rearrange("p n q -> p (n q)"), start=True, stop=True).then_inc(bc, 1)
            for t in range(TT):
                pe.wait_ge(pm, t + 1)
                for u in range(TT):
                    last = pe.transpose(k.bank(4, 128, NP_ * u + 128 * t), k.perm[:, t, 128 * u:128 * u + 128], k.ident[:, :])
            last.then_inc(pt, 1)
    k.clear()


def sort_tokens(k):
    nc = k.nc
    xp, xt, pe_t = k.at(XP_AT, L), k.at(XT_AT, L), k.at(PE_AT, L)
    x1 = k.at(X1_AT, X1_PAD + L)
    x1v = x1[:, X1_PAD:].rearrange("p (s o) -> p o s", o=OFF)
    tr, xtr, std, nrm, pmm, vch = (k.sem(n) for n in ("tr_done", "var_ready", "std_ready", "norm_done", "perm_mm", "v_chain"))
    st = k.at(FEAT_AT, NT * 6).rearrange("p (n s) -> p n s", s=6)
    mv = k.at(FEAT_AT + 192, NT * 2).rearrange("p (n s) -> p n s", s=2)
    rs = k.at(FEAT_AT + 256, NT)

    with nc.Block() as block:
        @block.tensor
        def _(pe):
            for i in range(NT):
                last = pe.transpose(k.ps[:, i * 128:(i + 1) * 128], xp[:, i * 128:(i + 1) * 128], k.ident[:, :])
                if i % 4 == 3:
                    last.then_inc(tr, 1)
            for o in range(0, OFF, 2):
                pe.wait_ge(nrm, NT)
                for oo in (o, o + 1):
                    for t in range(TT):
                        last = pe.matmul(k.bank(o // 2, NP_, (oo % 2) * NP_), xt[:, (t * OFF + oo) * 128:(t * OFF + oo + 1) * 128],
                                         k.perm[:, t, :], start=t == 0, stop=t == TT - 1)
                last.then_inc(pmm, 1)

        @block.gpsimd
        def _(pool):
            pool.memset(x1[:, 0:X1_PAD], 0.0).then_inc(k.sem("x1_pad"), 1)

        @block.vector
        def _(dve):
            step = Chain(dve, vch)
            for g in range(NT // 4):
                dve.wait_ge(tr, g + 1)
                step(dve.tensor_tensor(xt[:, g * CH:(g + 1) * CH], k.bank(g), pe_t[:, g * CH:(g + 1) * CH], ALU.add))
                for i in range(4 * g, 4 * g + 4):
                    dve.bn_stats(st[:, i, :], xt[:, i * 128:(i + 1) * 128]).then_inc(vch, 1)
                    step.n += 1
            dve.wait_ge(vch, step.n)
            for i in range(NT):
                dve.bn_aggr(mv[:, i, :], st[:, i, :]).then_inc(vch, 1)
                step.n += 1
            dve.wait_ge(vch, step.n)
            dve.tensor_scalar(rs, mv[:, :, 1], 1e-5, None, ALU.add).then_inc(xtr, 1)
            dve.wait_ge(std, 1)
            step(dve.reciprocal(rs, rs))
            for i in range(NT):
                dve.tensor_scalar(xt[:, i * 128:(i + 1) * 128], xt[:, i * 128:(i + 1) * 128], mv[:, i, 0:1], rs[:, i:i + 1],
                                  ALU.subtract, ALU.mult).then_inc(nrm, 1)

        @block.scalar
        def _(act):
            act.wait_ge(xtr, 1)
            act.activation(rs, rs, ACT.Sqrt).then_inc(std, 1)
            for g in range(OFF // 2):
                act.wait_ge(pmm, g + 1)
                act.activation(x1v[:, 2 * g:2 * g + 2, :], k.bank(g).rearrange("p (o s) -> p o s", o=2), ACT.Identity,
                               bias=k.cols[:, C_NB:C_NB + 1], scale=k.cols[:, C_G:C_G + 1]).then_inc(k.sem("x1_ready"), 1)
    k.clear()


XC_AT, SZ_AT, DBC_AT = 0, 8192, 16384


def project(k):
    nc = k.nc
    x1 = k.at(X1_AT, X1_PAD + L)
    xc = k.at(XC_AT, HD * L).rearrange("p (h n) -> p h n", h=HD)
    sz = k.at(SZ_AT, HD * L).rearrange("p (h n) -> p h n", h=HD)
    dbc = k.at(DBC_AT, L)
    mm, xp, ev = k.sem("proj_mm"), k.sem("xproj_mm"), k.sem("silu_done")

    with nc.Block() as block:
        @block.tensor
        def _(pe):
            with pe.Fori(0, NCH) as c:
                for h in range(HD):
                    pe.wait_ge(ev, c * 5 + h + 1)
                    for t in range(DC):
                        last = pe.matmul(k.bank(h), k.tapw[:, t, h * 128:(h + 1) * 128],
                                         x1[:, bass.ds(c * CH + (X1_PAD - DC + 1 + t), CH)], start=t == 0, stop=t == DC - 1)
                    last.then_inc(mm, 1)
                for h in range(HD):
                    pe.wait_ge(ev, c * 5 + 2 + h + 1)
                    pe.matmul(k.bank(2 + h), k.wz[:, h * 128:(h + 1) * 128], x1[:, bass.ds(c * CH + X1_PAD, CH)],
                              start=True, stop=True).then_inc(mm, 1)
                pe.wait_ge(ev, c * 5 + 7)
                for h in range(HD):
                    last = pe.matmul(k.bank(4), k.xpw[:, h, :], xc[:, h, bass.ds(c * CH, CH)], start=h == 0, stop=h == HD - 1)
                last.then_inc(xp, 1)

        @block.scalar
        def _(act):
            act.sem_inc(ev, 5)
            with act.Fori(0, NCH) as c:
                for h in range(HD):
                    act.wait_ge(mm, c * 4 + h + 1)
                    act.activation(xc[:, h, bass.ds(c * CH, CH)], k.bank(h), ACT.Silu,
                                   bias=k.cols[:, C_CB + h:C_CB + h + 1]).then_inc(ev, 1)
                for h in range(HD):
                    act.wait_ge(mm, c * 4 + 2 + h + 1)
                    act.activation(sz[:, h, bass.ds(c * CH, CH)], k.bank(2 + h), ACT.Silu).then_inc(ev, 1)
                act.wait_ge(xp, c + 1)
                act.activation(dbc[:, bass.ds(c * CH, CH)], k.bank(4), ACT.Copy).then_inc(ev, 1)
    k.clear()


def cols_of(c, n=CH):
    return slice(c * n, (c + 1) * n) if isinstance(c, int) else bass.ds(c * n, n)


def scan(k):
    nc = k.nc
    xc = k.at(XC_AT, HD * L).rearrange("p (h n) -> p h n", h=HD)
    sz = k.at(SZ_AT, HD * L).rearrange("p (h n) -> p h n", h=HD)
    dbc = k.at(DBC_AT, L)
    at = [DBC_AT + L]

    def ring(n, cols=HD * CH):
        out = [k.at(at[0] + i * cols, cols) for i in range(n)]
        at[0] += n * cols
        return out

    def halves(t):
        return t.rearrange("p (h n) -> p h n", h=HD)

    dt, u = ring(2), ring(2)
    (ab,), (onep,), (rx,) = ring(1), ring(1), ring(1)
    rest = onep[:, 0:CH]
    pieces = [t.bitcast(BF16) for t in ring(2, CH // 2)]
    da, dbx, hb, g, cs = ring(4), ring(2), ring(4), ring(4), ring(3, CH)
    assert at[0] <= ARENA
    dt_mm, ab_s, e_s, w_s, q_s, ln_s, rx_s, dt_s, hi_s, mid_s, r_s, pc_s = (k.sem(n) for n in (
        "dt_mm", "dt_abs", "dt_exp", "dt_onep", "dt_rest", "dt_ln", "dt_relu", "dt_ready", "high_ready", "middle_ready",
        "remainder", "pieces_ready"))
    b_mm, c_mm, y_mm, da_s, dbx_s, sc_s, hl_s, hp_s, hv_s, cs_s, fin_s = (k.sem(n) for n in (
        "b_mm", "c_mm", "y_mm", "da_ready", "dbx_ready", "scan_done", "hlast_saved", "hc_gpsimd", "hc_vector", "c_copied",
        "chunk_done"))
    va = k.sem("v_chain")

    def pooled(s):
        return s % 4 != 3

    NP = sum(pooled(s) for s in range(DS))
    NV = DS - NP

    def count(kind, c, s):
        n = NP if kind else NV
        if s < 0:
            return c * n + sum(pooled(i) == kind for i in range(s + DS + 1))
        return c * n + (n + sum(pooled(i) == kind for i in range(s + 1)))

    def chunks(prepare, body, eng):
        prepare(0, 0)
        for q in range(2):
            body(q, q, True)
        with eng.Fori(1, NCH // 2 - 1) as cc:
            for q in range(2):
                body(cc * 2 + q, q, True)
        body(NCH - 2, 0, True)
        body(NCH - 1, 1, False)

    def first(c):
        return isinstance(c, int) and c == 0

    with nc.Block() as block:
        @block.tensor
        def _(pe):
            def prepare(c, q):
                if not first(c):
                    pe.wait_ge(rx_s, c * 2)
                for h in range(HD):
                    last = pe.matmul(k.bank(h), k.dtw[:, h * 128:(h + 1) * 128], dbc[:, cols_of(c)], start=True, stop=True)
                last.then_inc(dt_mm, 1)

            def total(c, s):
                pe.wait_ge(hp_s if pooled(s) else hv_s, count(pooled(s), c, s))
                if s == 0:
                    pe.wait_ge(fin_s, c * 1 + 1)
                for h in range(HD):
                    last = pe.matmul(k.bank(6 + h), k.ident[:, :], halves(g[s % 4])[:, h, :], start=s == 0, stop=s == DS - 1)
                last.then_inc(y_mm, 1)

            def body(c, q, more):
                pe.wait_ge(pc_s, c * 1 + 1)
                for s in range(DS):
                    n = c * DS + s
                    pe.wait_ge(dbx_s, n + 1)
                    pe.matmul(k.bank(2 + s % 2), k.sel[:, s, :], pieces[q], start=True, stop=True).then_inc(b_mm, 1)
                    kind = pooled((s - 2) % DS)
                    pe.wait_ge(cs_s if kind else hv_s, count(kind, c, s - 2))
                    pe.matmul(k.bank(4 + s % 2), k.sel[:, DS + s, :], pieces[q], start=True, stop=True).then_inc(c_mm, 1)
                    if s >= 4:
                        total(c, s - 4)
                    elif not first(c):
                        total(c - 1, s - 4 + DS)
                    if more and s == 0:
                        prepare(c + 1, 1 - q)
            chunks(prepare, body, pe)
            for s in range(DS - 4, DS):
                total(NCH - 1, s)

        @block.scalar
        def _(act):
            def abs_exp(c):
                act.wait_ge(dt_mm, c * 1 + 1)
                for h in range(HD):
                    act.activation(halves(ab)[:, h, :], k.bank(h), ACT.Abs, bias=k.cols[:, C_DTB + h:C_DTB + h + 1]).then_inc(ab_s, 1)
                for h in range(HD):
                    act.activation(halves(rx)[:, h, :], k.bank(h), ACT.Relu, bias=k.cols[:, C_DTB + h:C_DTB + h + 1]).then_inc(rx_s, 1)
                act.wait_ge(ab_s, c * 2 + 2)
                act.activation(ab, ab, ACT.Exp, scale=-1.0).then_inc(e_s, 1)

            def log(c):
                act.wait_ge(q_s, c * 1 + 1)
                act.activation(onep, onep, ACT.Ln).then_inc(ln_s, 1)

            def high(c, q):
                act.activation(pieces[q][0:96, :], dbc[0:96, cols_of(c)], ACT.Copy).then_inc(hi_s, 1)

            def middle(c, q):
                act.wait_ge(r_s, c * 1 + 1)
                act.activation(pieces[q][0:64, :], rest[0:64, :], ACT.Copy).then_inc(mid_s, 1)

            def body(c, q, more):
                act.wait_ge(dt_s, c * 2 + 1)
                for s in range(DS):
                    act.wait_ge(sc_s, c * (2 * DS) + (2 * s + 2))
                    for h in range(HD):
                        act.activation(halves(da[s % 4])[:, h, :], halves(dt[q])[:, h, :], ACT.Exp,
                                       scale=k.amat[:, h, s:s + 1]).then_inc(da_s, 1)
                    if pooled(s):
                        act.wait_ge(c_mm, c * DS + (s + 1))
                        act.wait_ge(hp_s, count(True, c, s - 4))
                        act.activation(cs[s % 4], k.bank(4 + s % 2), ACT.Copy).then_inc(cs_s, 1)
                    if more and s == 0:
                        high(c + 1, 1 - q)
                    if more and s == 2:
                        abs_exp(c + 1)
                    if more and s == 3:
                        middle(c + 1, 1 - q)
                    if more and s == 9:
                        log(c + 1)
            chunks(lambda c, q: (abs_exp(c), high(c, q), middle(c, q), log(c)), body, act)

        @block.gpsimd
        def _(pool):
            def wait(sem, value):
                pool.wait_ge(sem, value)
                pool.sem_inc(k.sem("pool_waits_met"), 1)

            def remainder(c, q):
                wait(hi_s, c * 1 + 1)
                pool.tensor_tensor(rest[0:64, :], dbc[0:64, cols_of(c)], pieces[q][0:64, :], ALU.subtract).then_inc(r_s, 1)

            def low(c, q):
                wait(mid_s, c * 1 + 1)
                pool.tensor_tensor(pieces[q][0:32, :], rest[0:32, :], pieces[q][0:32, :], ALU.subtract).then_inc(pc_s, 1)

            def softplus(c, q, part):
                if part == 0:
                    wait(ln_s, c * 1 + 1)
                    pool.tensor_tensor(onep, onep, ab, ALU.subtract).then_inc(k.sem("log1p"), 1)
                if part == 1:
                    wait(k.sem("log1p"), c * 1 + 1)
                    wait(rx_s, c * 2 + 2)
                    pool.tensor_tensor(dt[q], onep, rx, ALU.add).then_inc(dt_s, 1)
                if part == 2:
                    wait(dt_s, c * 2 + 1)
                    pool.tensor_tensor(halves(u[q]), halves(dt[q]), xc[:, :, cols_of(c)], ALU.mult).then_inc(dt_s, 1)

            def body(c, q, more):
                for s in range(DS):
                    wait(sc_s, c * (2 * DS) + (2 * s + 2 + 8))
                    pool.tensor_copy(k.hlast[:, s, :, :], halves(hb[s % 4])[:, :, CH - 1:CH]).then_inc(hl_s, 1)
                    if pooled(s):
                        wait(cs_s, count(True, c, s))
                        wait(y_mm, c * DS + (s + 1))
                        pool.tensor_tensor(halves(g[s % 4]), halves(hb[s % 4]), cs[s % 4].unsqueeze(1).broadcast_to([128, HD, CH]),
                                           ALU.mult).then_inc(hp_s, 1)
                    if more and s == 0:
                        remainder(c + 1, 1 - q)
                    if more and s == 5:
                        low(c + 1, 1 - q)
                    if more and s in (10, 11, 13):
                        softplus(c + 1, 1 - q, (10, 11, 13).index(s))

            def prepare(c, q):
                for p in pieces:
                    pool.memset(p[96:128, :], 0.0).then_inc(k.sem("p_zero"), 1)
                pool.wait_ge(k.sem("p_zero"), 2)
                pool.memset(k.hlast[:, :, :, :], 0.0).then_inc(k.sem("h_zero"), 1)
                pool.wait_ge(k.sem("h_zero"), 1)
                pool.sem_inc(hl_s, DS)
                pool.sem_inc(hp_s, NP)
                remainder(c, q)
                low(c, q)
                for part in range(3):
                    softplus(c, q, part)
            chunks(prepare, body, pool)

        @block.vector
        def _(dve):
            def onep_(c):
                dve.wait_ge(e_s, c * 1 + 1)
                dve.wait_ge(mid_s, c * 1 + 1)
                dve.wait_ge(pc_s, c * 1 + 1)
                dve.tensor_scalar(onep, ab, 1.0, None, ALU.add).then_inc(w_s, 1)

            def rounding(c):
                dve.wait_ge(w_s, c * 1 + 1)
                dve.scalar_tensor_tensor(ab, onep, 1.0, ab, ALU.subtract, ALU.subtract).then_inc(q_s, 1)

            def inject(c, q, s):
                if s == 0:
                    dve.wait_ge(dt_s, c * 2 + 2)
                dve.wait_ge(b_mm, c * DS + (s + 1))
                dve.tensor_tensor(halves(dbx[s % 2]), halves(u[q]), k.bank(2 + s % 2).unsqueeze(1).broadcast_to([128, HD, CH]),
                                  ALU.mult).then_inc(dbx_s, 1)

            def finish(c):
                dve.wait_ge(y_mm, c * DS + (DS + 4))
                for h in range(HD):
                    dve.scalar_tensor_tensor(k.bank(6 + h), xc[:, h, cols_of(c)], k.cols[:, C_D + h:C_D + h + 1], k.bank(6 + h),
                                             ALU.mult, ALU.add).then_inc(va, 1)
                dve.wait_ge(va, c * 2 + 2)
                dve.tensor_tensor(sz[:, :, cols_of(c)], k.bank(6, 2 * CH).rearrange("p (h n) -> p h n", h=HD), sz[:, :, cols_of(c)],
                                  ALU.mult).then_inc(fin_s, 1)

            def body(c, q, more):
                inject(c, q, 0)
                for s in range(DS):
                    dve.wait_ge(hl_s, c * DS + (s - 3 + DS))
                    kind = pooled((s - 4) % DS)
                    dve.wait_ge(hp_s if kind else hv_s, count(kind, c, s - 4))
                    dve.wait_ge(dbx_s, c * DS + (s + 1 + 2))
                    for h in range(HD):
                        dve.wait_ge(da_s, c * (2 * DS) + (2 * s + h + 1))
                        dve.tensor_tensor_scan(halves(hb[s % 4])[:, h, :], halves(da[s % 4])[:, h, :], halves(dbx[s % 2])[:, h, :],
                                               k.hlast[:, s, h, :], ALU.mult, ALU.add).then_inc(sc_s, 1)
                        if h == 0 and s < DS - 1:
                            if s >= 1:
                                dve.wait_ge(sc_s, c * (2 * DS) + (2 * s + 8))
                            inject(c, q, s + 1)
                    if not pooled(s):
                        dve.wait_ge(c_mm, c * DS + (s + 1))
                        dve.wait_ge(y_mm, c * DS + (s + 1))
                        dve.wait_ge(sc_s, c * (2 * DS) + (2 * s + 2 + 8))
                        dve.tensor_tensor(halves(g[s % 4]), halves(hb[s % 4]), k.bank(4 + s % 2).unsqueeze(1).broadcast_to([128, HD, CH]),
                                          ALU.mult).then_inc(hv_s, 1)
                    if more and s == 7:
                        onep_(c + 1)
                        rounding(c + 1)
                    if s == 2 and not first(c):
                        finish(c - 1)

            dve.sem_inc(dbx_s, 2)
            dve.sem_inc(hv_s, NV)
            dve.sem_inc(cs_s, NP)
            dve.sem_inc(sc_s, 8)
            dve.sem_inc(fin_s, 1)
            dve.sem_inc(y_mm, 4)
            chunks(lambda c, q: (onep_(c), rounding(c)), body, dve)
            finish(NCH - 1)
    k.clear()


T_AT = 20480


def unsort(k, b):
    nc = k.nc
    y = k.at(SZ_AT, HD * L).rearrange("p (h n) -> p h n", h=HD)
    om, x, xp, t1 = k.at(DBC_AT, L), k.at(0, L), k.at(4096, L), k.at(T_AT, L)
    x_in, xp_s, o_mm, o_ev, t_mm = (k.sem(n) for n in ("x_in", "patches_ready", "outproj_mm", "outproj_read", "unsort_mm"))
    t_ev = k.sem("tokens_ready")
    with nc.Block() as block:
        @block.sync
        def _(sp):
            for i in range(4):
                sp.dma_start(x[:, i * 1024:(i + 1) * 1024], k.ins["x"][b, :, i * 1024:(i + 1) * 1024]).then_inc(x_in, 16)

        @block.gpsimd
        def _(pool):
            pool.wait_ge(x_in, 64)
            for t in range(TT):
                for r in range(PS):
                    pool.tensor_copy(patch_tiles(xp, t, r), patch_order(x, t, r)).then_inc(xp_s, 1)

        @block.tensor
        def _(pe):
            for i in range(NT):
                u, o = i // OFF, i % OFF
                for h in range(HD):
                    first = u * 128 * OFF + o
                    last = pe.matmul(k.ps[:, i * 128:(i + 1) * 128], y[:, h, first:first + 127 * OFF + 1:OFF], k.outw[:, h, :],
                                     start=h == 0, stop=h == HD - 1)
                if i % 4 == 3:
                    last.then_inc(o_mm, 1)
            pe.wait_ge(o_ev, NT // 4)
            for g in range(NT // 4):
                t, o4 = g // 4, g % 4
                for u in range(TT):
                    pe.matmul(k.bank(g), k.permt[:, u, t * 128:(t + 1) * 128], om[:, u * OFF * 128 + o4 * CH:u * OFF * 128 + (o4 + 1) * CH],
                              start=u == 0, stop=False)
                pe.wait_ge(xp_s, g + 1)
                for j in range(4):
                    last = pe.matmul(k.bank(g, 128, 128 * j), xp[:, g * CH + 128 * j:g * CH + 128 * j + 128], k.ident[:, :],
                                     start=False, stop=j == 3)
                last.then_inc(t_mm, 1)

        @block.scalar
        def _(act):
            for g in range(0, NT // 4):
                act.wait_ge(o_mm, g + 1)
                act.activation(om[:, g * CH:(g + 1) * CH], k.bank(g), ACT.Copy).then_inc(o_ev, 1)

        @block.vector
        def _(dve):
            for g in range(NT // 4):
                dve.wait_ge(t_mm, g + 1)
                dve.tensor_copy(t1[:, g * CH:(g + 1) * CH], k.bank(g)).then_inc(t_ev, 1)
    k.clear()


def normalize(k, dve, act, tn_at, x_at, eps):
    x, tn = k.at(x_at, L), k.at(tn_at, L)
    S = k.small
    st = k.at(tn_at, NT * 6).rearrange("p (n s) -> p n s", s=6)
    mv = S[:, 0:NT * 2].rearrange("p (n s) -> p n s", s=2)
    rs = S[:, 64:64 + NT]
    var_s, std_s, st_s, tn_s = k.sem("ln_var"), k.sem("ln_std"), k.sem("ln_stats"), k.sem("ln_done")
    if act is not None:
        act.wait_ge(var_s, 1)
        act.activation(rs, rs, ACT.Sqrt).then_inc(std_s, 1)
        return
    for i in range(NT):
        dve.bn_stats(st[:, i, :], x[:, i * 128:(i + 1) * 128]).then_inc(st_s, 1)
    dve.wait_ge(st_s, NT)
    for i in range(NT):
        dve.bn_aggr(mv[:, i, :], st[:, i, :]).then_inc(st_s, 1)
    dve.wait_ge(st_s, 2 * NT)
    dve.tensor_scalar(rs, mv[:, :, 1], eps, None, ALU.add).then_inc(var_s, 1)
    dve.wait_ge(std_s, 1)
    dve.reciprocal(rs, rs).then_inc(st_s, 1)
    dve.wait_ge(st_s, 2 * NT + 1)
    for i in range(NT):
        dve.tensor_scalar(tn[:, i * 128:(i + 1) * 128], x[:, i * 128:(i + 1) * 128], mv[:, i, 0:1], rs[:, i:i + 1],
                          ALU.subtract, ALU.mult).then_inc(tn_s, 1)


TN_AT, TNT_AT = 24576, 28672
QF_AT, KF_AT, QH_AT, QL_AT, KH_AT, KL_AT = 0, 4096, 8192, 10240, 12288, 14336
KS_AT, QS_AT, V_AT = 0, 32768, 16384
S_MV, S_SSQ, S_MAX, S_SC, S_U = 0, 100, 102, 104, 106


def qkv(k):
    nc = k.nc
    tn, tnt = k.at(TN_AT, L), k.at(TNT_AT, L)
    full = [k.at(QF_AT, L), k.at(KF_AT, L)]
    hi = [k.at(a, L // 2).bitcast(F16) for a in (QH_AT, KH_AT)]
    lo = [k.at(a, L // 2).bitcast(F16) for a in (QL_AT, KL_AT)]
    stack = [k.at(a, 2 * L).bitcast(F16).rearrange("p (h n) -> p h n", h=HEADS) for a in (QS_AT, KS_AT)]
    v = k.at(V_AT, L)
    S = k.small
    ssq, mx, sc, u = S[:, S_SSQ:S_SSQ + 2], S[:, S_MAX:S_MAX + 2], S[:, S_SC:S_SC + 2], S[:, S_U:S_U + 1]
    tn_s, tr, tr_ev, mm, ev, vmm, vev = (k.sem(n) for n in ("ln_done", "tr_done", "tnt_ready", "qk_mm", "qk_ready", "v_mm", "v_ready"))
    ss_s, sq_s, split_s, stacked, umm = (k.sem(n) for n in ("squares", "norm_roots", "split_done", "stacked", "bound_mm"))
    NG = NT // 4
    with nc.Block() as block:
        @block.tensor
        def _(pe):
            for i in range(NT):
                pe.wait_ge(tn_s, i + 1)
                last = pe.transpose(k.ps[:, i * 128:(i + 1) * 128], tn[:, i * 128:(i + 1) * 128], k.ident[:, :])
                if i % 4 == 3:
                    last.then_inc(tr, 1)
            for m in range(2):
                for c in range(NCH):
                    if m == 0:
                        pe.wait_ge(tr_ev, max(c + 1, NG if c == 0 else 1))
                    else:
                        pe.wait_ge(ev, c + 1)
                    pe.matmul(k.bank(c), k.wqkv[:, m * C:(m + 1) * C], tnt[:, c * CH:(c + 1) * CH], start=True, stop=True).then_inc(mm, 1)
            for g in range(NG):
                pe.wait_ge(ev, NCH + g + 1)
                for i in range(4 * g, 4 * g + 4):
                    last = pe.matmul(k.ps[:, i * 128:(i + 1) * 128], tnt[:, i * 128:(i + 1) * 128], k.wqkv[:, 2 * C:3 * C], start=True, stop=True)
                last.then_inc(vmm, 1)
            pe.wait_ge(sq_s, 2)
            pe.wait_ge(vev, 1)
            pe.matmul(k.ps[0:1, 0:1], u, k.ones[:, 0:1], start=True, stop=True).then_inc(umm, 1)

        @block.scalar
        def _(act):
            normalize(k, None, act, TN_AT, T_AT, 1e-5)
            for g in range(NG):
                act.wait_ge(tr, g + 1)
                act.activation(tnt[:, g * CH:(g + 1) * CH], k.bank(g), ACT.Copy).then_inc(tr_ev, 1)
            for m in range(2):
                for c in range(NCH):
                    act.wait_ge(mm, m * NCH + c + 1)
                    act.activation(full[m][:, c * CH:(c + 1) * CH], k.bank(c), ACT.Copy).then_inc(ev, 1)
            act.wait_ge(ss_s, 2)
            act.activation(sc, ssq, ACT.Sqrt).then_inc(sq_s, 1)
            for g in range(NG):
                act.wait_ge(vmm, g + 1)
                act.activation(v[:, g * CH:(g + 1) * CH], k.bank(g), ACT.Copy).then_inc(vev, 1)

        @block.vector
        def _(dve):
            normalize(k, dve, None, TN_AT, T_AT, 1e-5)
            step = Chain(dve, k.sem("v_chain"))
            dve.wait_ge(tr, NG)
            for m in range(2):
                dve.wait_ge(ev, (m + 1) * NCH)
                dve.scalar_tensor_tensor(tn, full[m], 1.0, full[m], ALU.mult, ALU.mult, accum_out=ssq[:, m:m + 1]).then_inc(ss_s, 1)
                dve.wait_ge(ss_s, m + 1)
                step(dve.reduce_max(mx[:, m:m + 1], tn, axis=AX.X))
            dve.wait_ge(sq_s, 1)
            step(dve.tensor_scalar(sc, sc, 1e-12, None, ALU.max))
            step(dve.reciprocal(sc, sc))
            step(dve.tensor_tensor(mx, mx, sc, ALU.mult))
            step(dve.tensor_tensor(mx, mx, sc, ALU.mult))
            step(dve.tensor_tensor(u, mx[:, 0:1], mx[:, 1:2], ALU.mult))
            step(dve.tensor_scalar(sc, sc, SPLIT, None, ALU.mult))
            dve.sem_inc(sq_s, 1)
            for m in range(2):
                step(dve.tensor_scalar(hi[m], full[m], sc[:, m:m + 1], None, ALU.mult))
                dve.scalar_tensor_tensor(lo[m], full[m], sc[:, m:m + 1], hi[m], ALU.mult, ALU.subtract).then_inc(split_s, 1)
            dve.wait_ge(umm, 1)
            dve.tensor_scalar(k.flag[0:1, 0:1], k.ps[0:1, 0:1], (SAFE / SCALE) ** 2 / C, None, ALU.is_gt).then_inc(k.sem("flag"), 1)

        @block.sync
        def _(sp):
            n = 0
            for m in range(2):
                sp.wait_ge(split_s, 2 if m else 1)
                for g in range(4):
                    high = (g < 2) if m == 0 else (g % 2 == 0)
                    for h in range(HEADS):
                        sp.dma_start(stack[m][32 * g:32 * g + 32, h, :], (hi if high else lo)[m][32 * h:32 * h + 32, :]).then_inc(stacked, 16)
                        n += 16
            sp.wait_ge(stacked, n)
    k.clear()


def attend(k):
    qs, ks = (k.at(a, 2 * L).bitcast(F16).rearrange("p (h n) -> p h n", h=HEADS) for a in (QS_AT, KS_AT))
    v, ao = k.at(V_AT, L), k.at(TNT_AT, L)
    probs = [k.at(8192 + i * 2 * CH, 2 * CH) for i in range(8)]
    acc = [k.at(TN_AT + i * 2 * CH, 2 * CH) for i in range(2)]
    rl = k.at(TN_AT + 4 * CH, CH)
    NJ, NPAIR = L // 128, 2 * (L // 128)
    s_mm, exp_s, pv_s, acc_s, l_mm, l_s, norm_s = (k.sem(n) for n in (
        "scores_mm", "probs_ready", "pv_mm", "probs_summed", "sums_mm", "sums_inverse", "chunk_normed"))
    O, LS = 6, 7
    group = [p % 3 for p in range(NPAIR - 1)] + [1]
    direct = [j for j in range(NJ) if j % 5 == 4]
    NA = NPAIR - 2 * len(direct)

    def summed(c, p):
        before, p = (0, p + NPAIR) if p < 0 else (NA, p)
        return c * NA + (before + sum(i // 2 not in direct for i in range(p + 1)))

    def tensor(pe):
        def ones_by(c, j, t, start, stop):
            for h in range(HEADS):
                last = pe.matmul(k.ps[32 * h:32 * h + 32, LS * CH:(LS + 1) * CH], k.ones[:, 0:32],
                                 t[h // 2][:, (h % 2) * CH:(h % 2 + 1) * CH], start=start, stop=stop, tile_position=(0, 32 * h))
            return last

        def weigh(c, j):
            pe.wait_ge(exp_s, c * NPAIR + (2 * j + 2 + 3))
            if j == 0:
                pe.wait_ge(norm_s, c + 1)
            if j in direct:
                ones_by(c, j, [probs[(2 * j + a) % 8] for a in range(2)], j == direct[0], False)
            for h in range(HEADS):
                last = pe.matmul(k.ps[32 * h:32 * h + 32, O * CH:(O + 1) * CH], v[:, j * 128 + 32 * h:j * 128 + 32 * h + 32],
                                 probs[(2 * j + h // 2) % 8][:, (h % 2) * CH:(h % 2 + 1) * CH],
                                 start=j == 0, stop=j == NJ - 1, tile_position=(0, 32 * h))
            last.then_inc(pv_s, 1)

        def finish(c):
            pe.wait_ge(acc_s, summed(c, NPAIR - 1))
            ones_by(c, 0, acc, False, True).then_inc(l_mm, 1)

        def body(c, first):
            for j in range(NJ):
                for a in range(2):
                    p = 2 * j + a
                    pe.wait_ge(exp_s, c * NPAIR + (p + (2 if p in (1, NPAIR - 1) else 1)))
                    for e in range(2):
                        h = 2 * a + e
                        last = pe.matmul(k.bank(2 * group[p] + e), ks[:, h, j * 128:(j + 1) * 128],
                                         qs[:, h, cols_of(c)], start=True, stop=True)
                    last.then_inc(s_mm, 1)
                    if p == 1 and not first:
                        weigh(c - 1, NJ - 1)
                    if p == 2 and not first:
                        finish(c - 1)
                if j in (3, 4):
                    weigh(c, 2 * j - 6)
                    weigh(c, 2 * j - 5)
                if j >= 5:
                    weigh(c, j - 1)

        body(0, True)
        with pe.Fori(1, NCH) as c:
            body(c, False)
        weigh(NCH - 1, NJ - 1)
        finish(NCH - 1)

    def scalar(act):
        act.sem_inc(exp_s, 3)
        with act.Fori(0, NCH) as c:
            for p in range(NPAIR):
                act.wait_ge(s_mm, c * NPAIR + (p + 1))
                act.wait_ge(pv_s, c * NJ + (p // 2 + 1))
                act.wait_ge(acc_s, summed(c, p - 8))
                act.activation(probs[p % 8], k.bank(2 * group[p], 2 * CH), ACT.Exp, scale=SCALE / SPLIT ** 2).then_inc(exp_s, 1)

    def vector(dve):
        dve.sem_inc(pv_s, 4)
        dve.sem_inc(acc_s, NA)
        dve.sem_inc(norm_s, 1)
        with dve.Fori(0, NCH) as c:
            for p in range(NPAIR):
                if p // 2 in direct:
                    continue
                dve.wait_ge(exp_s, c * NPAIR + (p + 1 + 3))
                if p < 2:
                    dve.tensor_copy(acc[p], probs[p % 8]).then_inc(acc_s, 1)
                else:
                    dve.wait_ge(acc_s, summed(c, p) - 2)
                    dve.tensor_tensor(acc[p % 2], acc[p % 2], probs[p % 8], ALU.add).then_inc(acc_s, 1)
            dve.wait_ge(l_mm, c + 1)
            dve.reciprocal(rl, k.bank(LS)).then_inc(l_s, 1)
            dve.wait_ge(l_s, c + 1)
            dve.wait_ge(pv_s, c * NJ + (NJ + 4))
            dve.tensor_tensor(ao[:, bass.ds(c * CH, CH)], k.bank(O), rl, ALU.mult).then_inc(norm_s, 1)

    return tensor, scalar, vector


def attend_guarded(k):
    qs, ks = (k.at(a, 2 * L).bitcast(F16).rearrange("p (h n) -> p h n", h=HEADS) for a in (QS_AT, KS_AT))
    v, ao = k.at(V_AT, L), k.at(TNT_AT, L)
    probs = [k.at(8192 + i * 2 * CH, 2 * CH) for i in range(4)]
    mb = k.at(12288, HEADS * CH).rearrange("p (h n) -> p h n", h=HEADS)
    diag, mcol = k.at(14336, 128), k.small[:, 150:151]
    acc = [k.at(TN_AT + i * 2 * CH, 2 * CH) for i in range(2)]
    rl = k.at(TN_AT + 4 * CH, CH)
    NJ, NPAIR, NR = L // 128, 2 * (L // 128), HEADS * CH // 128
    row_mm, max_s, diag_s, spread_mm, mb_s, s_mm, shift_s, exp_s, pv_s, acc_s, l_mm, l_s, norm_s = (k.sem(n) for n in (
        "rows_mm", "max_ready", "diag_ready", "max_spread", "max_saved", "scores_mm", "shifted", "probs_ready", "pv_mm",
        "probs_summed", "sums_mm", "sums_inverse", "chunk_normed"))
    O, LS = 6, 7
    def tensor(pe):
        def weigh(c, j):
            pe.wait_ge(exp_s, c * NPAIR + (2 * j + 2))
            for h in range(HEADS):
                last = pe.matmul(k.ps[32 * h:32 * h + 32, O * CH:(O + 1) * CH], v[:, j * 128 + 32 * h:j * 128 + 32 * h + 32],
                                 probs[(2 * j + h // 2) % 4][:, (h % 2) * CH:(h % 2 + 1) * CH],
                                 start=j == 0, stop=j == NJ - 1, tile_position=(0, 32 * h))
            last.then_inc(pv_s, 1)

        with pe.Fori(0, NCH) as c:
            pe.wait_ge(norm_s, c + 1)
            for r in range(NR):
                h, i = r // 4, r % 4
                pe.wait_ge(mb_s, c * NR + (r + 1))
                for g in range(NCH):
                    last = pe.matmul(k.bank(g), qs[:, h, bass.ds(c * CH + 128 * i, 128)], ks[:, h, g * CH:(g + 1) * CH],
                                     start=True, stop=True)
                last.then_inc(row_mm, 1)
                pe.wait_ge(diag_s, c * NR + (r + 1))
                pe.matmul(k.bank(0, 128), k.ones[:, :], diag, start=True, stop=True).then_inc(spread_mm, 1)
            pe.wait_ge(mb_s, c * NR + (NR + 1))
            for j in range(NJ):
                for a in range(2):
                    p = 2 * j + a
                    pe.wait_ge(shift_s, c * NPAIR + (p + 1 if p >= 3 else 3))
                    for e in range(2):
                        h = 2 * a + e
                        last = pe.matmul(k.bank(2 * (p % 3) + e), ks[:, h, j * 128:(j + 1) * 128], qs[:, h, bass.ds(c * CH, CH)],
                                         start=True, stop=True)
                    last.then_inc(s_mm, 1)
                if j >= 1:
                    weigh(c, j - 1)
            weigh(c, NJ - 1)
            pe.wait_ge(acc_s, c * NPAIR + NPAIR)
            for h in range(HEADS):
                last = pe.matmul(k.ps[32 * h:32 * h + 32, LS * CH:(LS + 1) * CH], k.ones[:, 0:32],
                                 acc[h // 2][:, (h % 2) * CH:(h % 2 + 1) * CH], start=True, stop=True, tile_position=(0, 32 * h))
            last.then_inc(l_mm, 1)

    def scalar(act):
        with act.Fori(0, NCH) as c:
            for p in range(NPAIR):
                act.wait_ge(shift_s, c * NPAIR + (p + 1 + 3))
                act.activation(probs[p % 4], probs[p % 4], ACT.Exp, scale=SCALE / SPLIT ** 2).then_inc(exp_s, 1)

    def vector(dve):
        dve.sem_inc(mb_s, 1)
        dve.sem_inc(shift_s, 3)
        dve.sem_inc(pv_s, 2)
        dve.sem_inc(norm_s, 1)
        with dve.Fori(0, NCH) as c:
            for r in range(NR):
                h, i = r // 4, r % 4
                dve.wait_ge(row_mm, c * NR + (r + 1))
                dve.reduce_max(mcol, k.ps[:, :], axis=AX.X).then_inc(max_s, 1)
                dve.wait_ge(max_s, c * NR + (r + 1))
                dve.tensor_scalar(diag, k.ident[:, :], mcol, None, ALU.mult).then_inc(diag_s, 1)
                dve.wait_ge(spread_mm, c * NR + (r + 1))
                dve.tensor_copy(mb[:, h, 128 * i:128 * i + 128], k.bank(0, 128)).then_inc(mb_s, 1)
            dve.wait_ge(mb_s, c * NR + (NR + 1))

            def add(p):
                dve.wait_ge(exp_s, c * NPAIR + (p + 1))
                if p < 2:
                    dve.tensor_copy(acc[p], probs[p % 4]).then_inc(acc_s, 1)
                else:
                    dve.wait_ge(acc_s, c * NPAIR + (p - 1))
                    dve.tensor_tensor(acc[p % 2], acc[p % 2], probs[p % 4], ALU.add).then_inc(acc_s, 1)

            for p in range(NPAIR):
                a = p % 2
                dve.wait_ge(s_mm, c * NPAIR + (p + 1))
                dve.wait_ge(pv_s, c * NJ + (p // 2 + 1))
                if p >= 4:
                    dve.wait_ge(acc_s, c * NPAIR + (p - 3))
                dve.tensor_tensor(probs[p % 4].rearrange("p (e n) -> p e n", e=2),
                                  k.bank(2 * (p % 3), 2 * CH).rearrange("p (e n) -> p e n", e=2),
                                  mb[:, 2 * a:2 * a + 2, :], ALU.subtract).then_inc(shift_s, 1)
                if p >= 1:
                    add(p - 1)
            add(NPAIR - 1)
            dve.wait_ge(l_mm, c + 1)
            dve.reciprocal(rl, k.bank(LS)).then_inc(l_s, 1)
            dve.wait_ge(l_s, c + 1)
            dve.wait_ge(pv_s, c * NJ + (NJ + 2))
            dve.tensor_tensor(ao[:, bass.ds(c * CH, CH)], k.bank(O), rl, ALU.mult).then_inc(norm_s, 1)
            dve.wait_ge(norm_s, c + 2)

    return tensor, scalar, vector


def attention_out(k):
    nc = k.nc
    t1, ao = k.at(T_AT, L), k.at(TNT_AT, L)
    o_mm, t_s = k.sem("outproj_mm"), k.sem("tokens_ready")
    with nc.Block() as block:
        @block.tensor
        def _(pe):
            for g in range(NT // 4):
                pe.matmul(k.bank(g), k.ones[0:1, :], k.brow[0:1, :, :].rearrange("a q c -> a (q c)"), start=True, stop=False)
                for i in range(4):
                    at = g * CH + 128 * i
                    last = pe.matmul(k.bank(g, 128, 128 * i), ao[:, at:at + 128], k.wout[:, :], start=False, stop=i == 3)
                last.then_inc(o_mm, 1)

        @block.vector
        def _(dve):
            for g in range(NT // 4):
                dve.wait_ge(o_mm, g + 1)
                dve.tensor_tensor(t1[:, g * CH:(g + 1) * CH], t1[:, g * CH:(g + 1) * CH], k.bank(g), ALU.add).then_inc(t_s, 1)
    k.clear()


def attention(k):
    guarded, bounded = attend_guarded(k), attend(k)
    with k.nc.Block() as block:
        @block.tensor
        def _(pe):
            need = pe.value_load(k.flag[0:1, 0:1], min_val=0, max_val=1)
            with pe.If(need == 1):
                guarded[0](pe)
            with pe.Else():
                bounded[0](pe)
            pe.drain()

        @block.scalar
        def _(act):
            need = act.value_load(k.flag[0:1, 0:1], min_val=0, max_val=1)
            with act.If(need == 1):
                guarded[1](act)
            with act.Else():
                bounded[1](act)
            act.drain()

        @block.vector
        def _(dve):
            need = dve.value_load(k.flag[0:1, 0:1], min_val=0, max_val=1)
            with dve.If(need == 1):
                guarded[2](dve)
            with dve.Else():
                bounded[2](dve)
            dve.drain()
    k.clear()
    attention_out(k)


def ffn(k, b):
    nc = k.nc
    t1, tn, tnt, img = k.at(T_AT, L), k.at(TN_AT, L), k.at(0, L), k.at(4096, L)
    E0 = 8192
    names = ("ex", "c1", "oh1", "e2", "oh2", "gate", "tmp")
    small = {n: k.at(E0 + i * 256, NT * NE).rearrange("p (i e) -> p i e", e=NE) for i, n in enumerate(names)}
    gpad = k.at(E0 + 2048, NT * 32).rearrange("p (i e) -> p i e", e=32)
    gt = k.at(E0 + 3072, 1024)
    cols = k.at(E0 + 4096, 256)
    m1, m2, den = (cols[:, i * NT:(i + 1) * NT] for i in range(3))
    prod = [k.at(E0 + 4352 + i * 1024, NE * C).rearrange("p (e c) -> p e c", e=NE) for i in range(4)]
    tn_s, tr, tr_ev, lg, lc, ex_s = (k.sem(n) for n in ("ln_done", "tr_done", "tnt_ready", "logits_mm", "logits_ready", "exp_done"))
    gp, gz, gtm, gte, bmm, bad = (k.sem(n) for n in ("gates_ready", "gates_zero", "gates_tr", "gates_out", "bias_mm", "bias_added"))
    emm, ml, hs, ts, fm, fe, out_s = (k.sem(n) for n in (
        "experts_mm", "weighted", "halved", "tile_added", "final_tr", "final_out", "stored"))
    NG = NT // 4

    def spread(col):
        return col.unsqueeze(2).broadcast_to([128, NT, NE])

    with nc.Block() as block:
        @block.tensor
        def _(pe):
            for i in range(NT):
                pe.wait_ge(tn_s, i + 1)
                last = pe.transpose(k.ps[:, i * 128:(i + 1) * 128], tn[:, i * 128:(i + 1) * 128], k.ident[:, :])
                if i % 4 == 3:
                    last.then_inc(tr, 1)
            pe.wait_ge(tr_ev, NG)
            for i in range(NT):
                last = pe.matmul(k.bank(0, NE, NE * i), tnt[:, i * 128:(i + 1) * 128], k.routw[:, :], start=True, stop=True)
            last.then_inc(lg, 1)
            pe.wait_ge(gp, 1)
            for q in range(NT // 4):
                last = pe.transpose(k.bank(1 + q // 4, 128, 128 * (q % 4)), gpad[:, 4 * q:4 * q + 4, :].rearrange("p i e -> p (i e)"), k.ident[:, :])
            last.then_inc(gtm, 1)
            pe.wait_ge(gte, 1)
            for g in range(NG):
                for i in range(4):
                    last = pe.matmul(k.bank(g, 128, 128 * i), gt[:, g * 128:(g + 1) * 128], k.expb[:, i, :], start=True, stop=True)
                last.then_inc(bmm, 1)
            for i in range(NT):
                if i < 4:
                    pe.wait_ge(bad, NG)
                else:
                    pe.wait_ge(ml, i - 3)
                for hb in range(2):
                    last = pe.matmul(k.bank(2 * (i % 4) + hb), tnt[:, i * 128:(i + 1) * 128],
                                     k.expw[:, hb * 4:hb * 4 + 4, :].rearrange("p e c -> p (e c)"), start=True, stop=True)
                last.then_inc(emm, 1)
            for g in range(NG):
                pe.wait_ge(ml, NT)
                pe.wait_ge(ts, 2 * (4 * g + 4))
                for i in range(4 * g, 4 * g + 4):
                    last = pe.transpose(k.ps[:, i * 128:(i + 1) * 128], t1[:, i * 128:(i + 1) * 128], k.ident[:, :])
                last.then_inc(fm, 1)

        @block.scalar
        def _(act):
            normalize(k, None, act, TN_AT, T_AT, 1e-5)
            for g in range(NG):
                act.wait_ge(tr, g + 1)
                act.activation(tnt[:, g * CH:(g + 1) * CH], k.bank(g), ACT.Copy).then_inc(tr_ev, 1)
            act.wait_ge(lc, 1)
            act.activation(small["ex"], small["tmp"], ACT.Exp).then_inc(ex_s, 1)
            act.wait_ge(gtm, 1)
            act.activation(gt, k.ps[:, CH:3 * CH], ACT.Copy).then_inc(gte, 1)
            for g in range(NG):
                act.wait_ge(fm, g + 1)
                act.activation(patch_order(img, g // PS, g % PS), k.bank(g).rearrange("p (x h w) -> p x h w", x=PS, w=W // PS), ACT.Copy).then_inc(fe, 1)

        @block.gpsimd
        def _(pool):
            pool.memset(gpad, 0.0).then_inc(gz, 1)
            for i in range(NT):
                pool.wait_ge(ml, i + 1)
                t = prod[i % 4]
                pool.tensor_tensor(t[:, 0:4, :], t[:, 0:4, :], t[:, 4:8, :], ALU.add).then_inc(hs, 1)
                pool.wait_ge(hs, 2 * i + 1)
                pool.tensor_tensor(t[:, 0:2, :], t[:, 0:2, :], t[:, 2:4, :], ALU.add).then_inc(hs, 1)

        @block.vector
        def _(dve):
            normalize(k, dve, None, TN_AT, T_AT, 1e-5)
            step = Chain(dve, k.sem("v_chain"))
            ex, c1, oh1, e2, oh2, gate, tmp = (small[n] for n in names)
            dve.wait_ge(lg, 1)
            step(dve.tensor_tensor(tmp, k.bank(0, NT * NE).rearrange("p (i e) -> p i e", e=NE), k.rtb[:, :].unsqueeze(1).broadcast_to([128, NT, NE]), ALU.add))
            step(dve.reduce_max(m1, tmp, axis=AX.X))
            dve.tensor_tensor(tmp, tmp, spread(m1), ALU.subtract).then_inc(lc, 1)
            dve.wait_ge(ex_s, 1)
            order = k.rank8[:, :].unsqueeze(1).broadcast_to([128, NT, NE])

            def first_max(src, top, onehot):
                step(dve.reduce_max(top, src, axis=AX.X))
                step(dve.tensor_tensor(c1, src, spread(top), ALU.is_equal))
                step(dve.tensor_tensor(c1, c1, order, ALU.mult))
                step(dve.reduce_max(den, c1, axis=AX.X))
                step(dve.tensor_tensor(onehot, c1, spread(den), ALU.is_equal))

            first_max(ex, m1, oh1)
            step(dve.scalar_tensor_tensor(e2, oh1, -4.0, ex, ALU.mult, ALU.add))
            first_max(e2, m2, oh2)
            step(dve.tensor_tensor(den, m1, m2, ALU.add))
            step(dve.reciprocal(den, den))
            step(dve.tensor_tensor(gate, oh1, oh2, ALU.add))
            step(dve.tensor_tensor(gate, gate, ex, ALU.mult))
            step(dve.tensor_tensor(gate, gate, spread(den), ALU.mult))
            dve.wait_ge(gz, 1)
            dve.tensor_copy(gpad[:, :, 0:NE], gate).then_inc(gp, 1)
            for g in range(NG):
                dve.wait_ge(bmm, g + 1)
                dve.tensor_tensor(t1[:, g * CH:(g + 1) * CH], t1[:, g * CH:(g + 1) * CH], k.bank(g), ALU.add).then_inc(bad, 1)

            def finish(i):
                dve.wait_ge(hs, 2 * i + 2)
                t = prod[i % 4]
                tile = t1[:, i * 128:(i + 1) * 128]
                dve.tensor_tensor(tile, tile, t[:, 0, :], ALU.add).then_inc(ts, 1)
                dve.wait_ge(ts, 2 * i + 1)
                dve.tensor_tensor(tile, tile, t[:, 1, :], ALU.add).then_inc(ts, 1)

            dve.wait_ge(bad, NG)
            for i in range(NT):
                dve.wait_ge(emm, i + 1)
                if i >= 4:
                    dve.wait_ge(ts, 2 * (i - 3))
                dve.tensor_tensor(prod[i % 4], k.bank(2 * (i % 4), 2 * CH).rearrange("p (e c) -> p e c", e=NE),
                                  gate[:, i, :].unsqueeze(2).broadcast_to([128, NE, C]), ALU.mult).then_inc(ml, 1)
                if i >= 3:
                    finish(i - 3)
            for i in range(NT - 3, NT):
                finish(i)

        @block.sync
        def _(sp):
            sp.wait_ge(fe, NG // 2)
            sp.dma_start(k.out[b, :, 0:L // 2], img[:, 0:L // 2]).then_inc(out_s, 16)
            sp.wait_ge(fe, NG)
            sp.dma_start(k.out[b, :, L // 2:L], img[:, L // 2:L]).then_inc(out_s, 16)
            sp.wait_ge(out_s, 32)
    k.clear()


def program(nc, ins, out):
    with ExitStack() as ctx:
        k = Kernel(nc, ctx, ins, out)
        setup(k)
        with nc.Fori(0, B) as b:
            score(k, b)
            sort_tokens(k)
            project(k)
            scan(k)
            unsort(k, b)
            qkv(k)
            attention(k)
            ffn(k, b)


TRANSPOSED = {
    "in_projT": "L0_conv_in_proj_w", "out_projT": "L0_conv_out_proj_w", "x_projT": "L0_conv_x_proj_w",
    "dt_projT": "L0_conv_dt_proj_w", "ca1T": "L0_conv_ca1_w", "ca2T": "L0_conv_ca2_w",
}


def kernel(**inputs):
    import concourse.bacc as bacc
    from concourse.bass_utils import run_bass_kernel_spmd

    arrays = {n: np.ascontiguousarray(a) for n, a in inputs.items() if n not in TRANSPOSED.values()}
    arrays["x"] = arrays["x"].reshape(B, C, L)
    arrays["pe"] = arrays.pop("L0_conv_pe")
    for name, source in TRANSPOSED.items():
        arrays[name] = np.ascontiguousarray(np.asarray(inputs[source]).T)
    nc = bacc.Bacc("TRN2", target_bir_lowering=False, num_devices=1)
    ins = {n: nc.dram_tensor(n, a.shape, mybir.dt.from_np(a.dtype), kind="ExternalInput").ap() for n, a in arrays.items()}
    out = nc.dram_tensor("out", (B, C, L), F32, kind="ExternalOutput").ap()
    program(nc, ins, out)
    r = run_bass_kernel_spmd(nc, [arrays], core_ids=[0])
    return r.results[0]["out"].reshape(B, C, H, W)
```

```python
import numpy as np
import concourse.bass as bass
from concourse import mybir
from contextlib import ExitStack

F32, BF16, F16, I32 = mybir.dt.float32, mybir.dt.bfloat16, mybir.dt.float16, mybir.dt.int32
ALU, ACT, AX = mybir.AluOpType, mybir.ActivationFunctionType, mybir.AxisListType

B, C, H, W = 4, 128, 64, 64
L = H * W
PS = 4
NP_ = (H // PS) * (W // PS)
TT = NP_ // 128
OFF = PS * PS
NT = TT * OFF
DI, DS, DR, DC = 2 * C, 16, C // 16, 4
HD = DI // 128
CH = 512
NCH = L // CH
PW = W + 2
HEADS, DH = 4, 32
SCALE = 10.0
NE = 8
SPLIT = 4096.0
SAFE = 60.0


ARENA = 44032


class Chain:

    def __init__(self, eng, sem):
        self.eng, self.sem, self.n = eng, sem, 0

    def __call__(self, ins):
        self.n += 1
        ins.then_inc(self.sem, 1)
        self.eng.wait_ge(self.sem, self.n)


class Kernel:

    def __init__(self, nc, ctx, ins, out, batches=B):
        self.nc, self.ctx, self.ins, self.out, self.batches = nc, ctx, ins, out, batches
        self.sems = {}
        self.sem("stored")

        def sb(name, shape, dt=F32):
            return ctx.enter_context(nc.sbuf_tensor(name, shape, dt))

        self.ident = sb("ident", [128, 128])
        self.group = sb("group", [128, 32, 4])
        self.wz = sb("wz", [128, DI])
        self.wx = sb("wx", [128, DI])
        self.taps = sb("taps", [128, HD, DC])
        self.xpw = sb("xpw", [128, HD, 128])
        self.dtw = sb("dtw", [128, DI])
        self.sel = sb("sel", [128, 32, 128], BF16)
        self.pick = sb("pick", [128, 2, HEADS, 128], F16)
        self.outw = sb("outw", [128, HD, C])
        self.wqkv = sb("wqkv", [128, 3 * C])
        self.wout = sb("wout", [128, C])
        self.expw = sb("expw", [128, NE, C])
        self.expb = sb("expb", [128, 4, C])
        self.routw = sb("routw", [128, 32])
        self.dmat = sb("dmat", [128, HD, 128])
        self.iota = sb("iota", [128, NP_], BF16)
        self.lower = sb("lower", [128, TT, NP_], BF16)
        self.rowmask = sb("rowmask", [128, NCH, 32], BF16)
        self.hwin = sb("hwin", [128, 33])
        self.owin = sb("owin", [128, 33])
        self.ca1 = sb("ca1", [128, C // 4])
        self.ca2 = sb("ca2", [C // 4, C])
        self.ones = sb("ones", [128, 128])
        self.cols = sb("cols", [128, 64])
        self.convw = sb("convw", [128, 2, 9])
        self.amat = sb("amat", [128, HD, DS])
        self.rtb = sb("rtb", [128, NE])
        self.rank8 = sb("rank8", [128, NE])
        self.perm = sb("perm", [128, TT, NP_])
        self.permt = sb("permt", [128, TT, NP_])
        self.hlast = sb("hlast", [128, DS, HD, 1])
        self.small = sb("small", [128, 160])
        self.flag = sb("flag", [1, 1], I32)
        self.R = sb("arena", [128, ARENA])
        self.ps = ctx.enter_context(nc.psum_tensor("ps", [128, 8 * CH], F32))

    def sem(self, name):
        if name not in self.sems:
            self.sems[name] = self.ctx.enter_context(self.nc.semaphore(name))
        return self.sems[name]

    def clear(self, but=0):
        nums = sorted(s.num for s in self.sems.values())
        self.nc.all_engine_barrier(sems_to_clear=range(nums[but], nums[-1] + 1))

    def load_x(self, sp, b, done):
        for i in range(4):
            sp.dma_start(self.at(X_AT + i * L // 4, L // 4), self.ins["x"][b, :, i * L // 4:(i + 1) * L // 4]).then_inc(done, 16)
        sp.wait_ge(done, 64)

    def bank(self, n, cols=CH, at=0):
        return self.ps[:, n * CH + at:n * CH + at + cols]

    def at(self, off, n):
        return self.R[:, off:off + n]


C_B1, C_B2, C_G, C_NB, C_HB, C_CB, C_DTB, C_D, C_ONE, C_BO = 0, 1, 2, 3, 4, 5, 7, 9, 11, 12


def patch_order(image, t, y):
    rows = H // TT
    v = image[:, t * rows * W:(t + 1) * rows * W].rearrange("p (h y w x) -> p y x h w", y=PS, w=W // PS, x=PS)
    return v[:, y]


def patch_tiles(tiles, t, y):
    n = PS * 128
    at = (t * PS + y) * n
    return tiles[:, at:at + n].rearrange("p (x h w) -> p x h w", x=PS, w=W // PS)


def setup(k):
    nc, w = k.nc, k.ins
    loaded, zeroed, built = k.sem("weights_loaded"), k.sem("zeroed"), k.sem("masks_built")
    pieces = []

    def col(name, at):
        return (k.cols[:, at:at + 1], w[name].rearrange("(p a) -> p a", a=1))

    pieces += [col("L0_conv_conv1_b", C_B1), col("L0_conv_conv2_b", C_B2), col("L0_conv_norm_g", C_G), col("L0_conv_norm_b", C_NB), col("L1_attn_b_out", C_BO)]
    for n, at in (("L0_conv_conv1d_b", C_CB), ("L0_conv_dt_proj_b", C_DTB), ("L0_conv_D", C_D)):
        for h in range(HD):
            pieces.append((k.cols[:, at + h:at + h + 1], w[n][h * 128:(h + 1) * 128].rearrange("(p a) -> p a", a=1)))
    pieces.append((k.cols[:, C_HB:C_HB + 1], w["L0_conv_head_b"].partition_broadcast(128)))
    pieces.append((k.convw[:, 0, :], w["L0_conv_conv1_w"].rearrange("c a y x -> c (a y x)")))
    pieces.append((k.convw[:, 1, :], w["L0_conv_conv2_w"].rearrange("c a y x -> c (a y x)")))
    pieces.append((k.wx[:, :], w["in_projT"][:, 0:DI]))
    pieces.append((k.wz[:, :], w["in_projT"][:, DI:2 * DI]))
    pieces.append((k.taps[:, :, :], w["L0_conv_conv1d_w"].rearrange("(h p) k -> p h k", h=HD)))
    pieces.append((k.outw[:, :, :], w["out_projT"].rearrange("(h p) c -> p h c", h=HD)))
    pieces.append((k.wqkv[:, :], w["L1_attn_W_qkv"]))
    pieces.append((k.wout[:, :], w["L1_attn_W_out"]))
    pieces.append((k.rtb[:, :], w["L1_ffn_router_b"].partition_broadcast(128)))
    pieces.append((k.expw[:, :, :], w["L1_ffn_expert_w"].rearrange("e d c -> d e c")))
    pieces.append((k.ca1[:, :], w["ca1T"]))
    pieces.append((k.ca2[:, :], w["ca2T"]))
    pieces.append((k.amat[:, :, :], w["L0_conv_A_log"].rearrange("(h p) s -> p h s", h=HD)))
    late = [(k.hwin[:, 1:2], w["L0_conv_head_w"].rearrange("a c -> c a"))]
    for g in range(3):
        for h in range(HD):
            late.append((k.xpw[:, h, 32 * g:32 * g + 32], w["x_projT"][h * 128:(h + 1) * 128, DR:DR + 2 * DS]))
    for h in range(HD):
        late.append((k.xpw[:, h, 96:96 + DR], w["x_projT"][h * 128:(h + 1) * 128, 0:DR]))
    late.append((k.dtw[96:96 + DR, :], w["dt_projT"]))
    late.append((k.routw[:, 0:NE], w["L1_ffn_router_w"]))
    for q in range(4):
        late.append((k.expb[32 * q:32 * q + NE, q, :], w["L1_ffn_expert_b"]))
    total = 16 * (len(pieces) + len(late))

    with nc.Block() as block:
        @block.sync
        def _(sp):
            sp.sem_inc(k.sem("stored"), 32)
            for dst, src in pieces:
                sp.dma_start(dst, src, allow_slow_non_contiguous=True).then_inc(loaded, 16)
            sp.wait_ge(zeroed, 6)
            for dst, src in late:
                sp.dma_start(dst, src, allow_slow_non_contiguous=True).then_inc(loaded, 16)
            k.load_x(sp, 0, k.sem("x_in"))

        @block.gpsimd
        def _(pool):
            step = Chain(pool, built)
            step(pool.memset(k.ident[:, :], 0.0))
            step(pool.affine_select(out=k.ident[:, :], in_=k.ident[:, :], compare_op=ALU.not_equal, fill=1.0,
                                    base=0, pattern=[[-1, 128]], channel_multiplier=1))
            step(pool.memset(k.group[:, :, :], 0.25))
            step(pool.affine_select(out=k.group[:, :, :], in_=k.group[:, :, :], compare_op=ALU.is_ge, fill=0.0,
                                    base=0, pattern=[[-4, 32], [0, 4]], channel_multiplier=1))
            step(pool.affine_select(out=k.group[:, :, :], in_=k.group[:, :, :], compare_op=ALU.is_ge, fill=0.0,
                                    base=3, pattern=[[4, 32], [0, 4]], channel_multiplier=-1))
            step(pool.memset(k.sel[:, :, :], 0.0))
            for g in range(3):
                v = k.sel[32 * g:32 * g + 32, :, :]
                step(pool.affine_select(out=v, in_=v, compare_op=ALU.not_equal, fill=1.0,
                                        base=0, pattern=[[-1, 32], [0, 128]], channel_multiplier=1))
            step(pool.memset(k.pick[:, :, :, :], 0.0))
            for w in range(2):
                v = k.pick[:, w, :, 64 * w:64 * w + 64].rearrange("p h (g r) -> p h g r", g=2)
                step(pool.affine_select(out=v, in_=v, compare_op=ALU.not_equal, fill=1.0,
                                        base=0, pattern=[[-32, HEADS], [0, 2], [-1, 32]], channel_multiplier=1))
            step(pool.iota(k.iota[:, :], [[1, NP_]], base=0, channel_multiplier=0, allow_small_or_imprecise_dtypes=True))
            step(pool.iota(k.rank8[:, :], [[-1, NE]], base=NE, channel_multiplier=0, allow_small_or_imprecise_dtypes=True))
            step(pool.memset(k.lower[:, :, :], 1.0))
            step(pool.affine_select(out=k.lower[:, :, :], in_=k.lower[:, :, :], compare_op=ALU.is_gt, fill=0.0,
                                    base=0, pattern=[[128, TT], [-1, NP_]], channel_multiplier=1))
            step(pool.memset(k.rowmask[:, :, :], 0.0))
            v = k.rowmask[:, :, :].rearrange("p (b a) q -> p b a q", a=2)
            step(pool.affine_select(out=v, in_=v, compare_op=ALU.not_equal, fill=1.0,
                                    base=0, pattern=[[-32, NCH // 2], [-1, 2], [0, 32]], channel_multiplier=1))
            step(pool.memset(k.owin[:, :], 0.0))
            step(pool.memset(k.owin[:, 1:2], 1.0))
            step(pool.memset(k.ones[:, :], 1.0))
            step(pool.memset(k.cols[:, C_ONE:C_ONE + 1], 1.0))

        @block.vector
        def _(dve):
            for t in (k.hwin[:, :], k.xpw[:, :, :], k.dtw[:, :], k.expb[:, :, :], k.small[:, :], k.routw[:, :]):
                dve.memset(t, 0.0).then_inc(zeroed, 1)

        @block.scalar
        def _(act):
            step = Chain(act, k.sem("a_made"))
            act.wait_ge(loaded, total)
            step(act.activation(k.amat[:, :, :], k.amat[:, :, :], ACT.Exp))
            step(act.mul(k.amat[:, :, :], k.amat[:, :, :], -1.0))
            act.wait_ge(built, 2)
            for h in range(HD):
                step(act.mul(k.dmat[:, h, :], k.ident[:, :], k.cols[:, C_D + h:C_D + h + 1]))
    k.clear(but=1)


X_AT, PAD1_AT, PAD2_AT, FEAT_AT, SQ_AT, XT_AT, PE_AT, X1_AT, XP_AT, DIAG_AT = 39936, 4096, 8704, 13312, 17408, 21504, 25600, 29696, 33800, 37896


def score_and_sort(k, b):
    nc = k.nc
    x = k.at(X_AT, L)
    pad = [k.at(o, PW * PW).rearrange("p (h w) -> p h w", w=PW) for o in (PAD1_AT, PAD2_AT)]
    inner = [p[:, 1:H + 1, 1:W + 1] for p in pad]
    feat, sq, xp = k.at(FEAT_AT, L), k.at(SQ_AT, L), k.at(XP_AT, L)
    NG, PT, RG = 4, 4, H // 4
    S = k.small
    stats = S[:, 0:48].rearrange("p (n s) -> p n s", s=6)
    mv, g2, gm, rstd, t0, t1 = S[:, 48:50], S[:, 50:52], S[:, 52:53], S[:, 53:54], S[:, 54:55], S[:, 55:56]
    csum, ctot, hid, ca = S[:, 56:56 + NG], S[:, 64:65], S[0:C // 4, 65:66], S[:, 66:67]
    colv, rank = S[:, 68:70], S[:, 70:72]
    diag = k.at(DIAG_AT, 2 * PT * 128).rearrange("p (i t n) -> p i t n", i=2, t=PT)
    work = k.at(X1_AT, 4096)
    rows = [work[:, i * CH:(i + 1) * CH] for i in range(6)]
    bd = work[:, 3072:3072 + NP_].rearrange("p (n q) -> p n q", q=32)
    smb, junk = work[:, 3328:3328 + NP_], work[:, 3584:3584 + NP_]
    pe_in, stored = k.sem("pe_in"), k.sem("stored")
    border, gn_in, gn_sum, gn_var, gn_std, xn = (k.sem(n) for n in ("borders_zero", "gn_in", "gn_sum", "gn_var", "gn_std", "xn_ready"))
    conv, taps_s = k.sem("conv_mm"), k.sem("taps_added")
    gelu = [k.sem("gelu1_done"), k.sem("gelu2_done")]
    csm, hmm, hre, amm, ca_s, sums, sq_s = (k.sem(n) for n in ("csum_ready", "hid_mm", "hid_relu", "att_mm", "att_ready", "channel_sums", "squares"))
    head, sigs, pv, bd_s, bc, pm, pt = (k.sem(n) for n in ("head_mm", "sigmoids", "pv_ready", "scores_spread", "scores_bcast", "perm_ready", "permt_mm"))
    vch, diag_s = k.sem("v_chain"), k.sem("diag_ready")

    xt, pe_t = k.at(XT_AT, L), k.at(PE_AT, L)
    x1v = k.at(X1_AT, L).rearrange("p (s o) -> p o s", o=OFF)
    tr, xt_s, xtr, std, nrm, pmm = (k.sem(n) for n in ("tr_done", "tokens_stats", "var_ready", "std_ready", "norm_done", "perm_mm"))
    st = k.at(SQ_AT, NT * 6).rearrange("p (n s) -> p n s", s=6)
    tmv = k.at(SQ_AT + 192, NT * 2).rearrange("p (n s) -> p n s", s=2)
    rs = k.at(SQ_AT + 256, NT)
    token_bank = [4, 5, 0, 1, 2, 3, 4, 5]

    def tap(i, g, j):
        return pad[i][:, RG * g + j // 3:RG * g + j // 3 + RG, j % 3:j % 3 + W]

    def pair(i, g):
        return (NG * i + g) % 3

    def group(t, g):
        return t[:, g * RG * W:(g + 1) * RG * W].rearrange("p (h w) -> p h w", w=W)

    with nc.Block() as block:
        @block.sync
        def _(sp):
            pe_v = k.ins["pe"].rearrange("(t h y w x) c -> t y h w (x c)", t=TT, y=PS, w=W // PS, x=PS)
            dst = k.at(PE_AT, L).rearrange("p (t y n) -> p t y n", t=TT, y=PS)
            for t in range(TT):
                for y in range(PS):
                    for h in range(8):
                        sp.dma_start(dst[16 * h:16 * h + 16, t, y, :], pe_v[t, y, h]).then_inc(pe_in, 16)
            sp.wait_ge(pe_in, 16 * TT * PS * 8)

        @block.gpsimd
        def _(pool):
            for p in pad:
                pool.memset(p[:, 0:PW:PW - 1, :], 0.0).then_inc(border, 1)
                pool.memset(p[:, 1:H + 1, 0:PW:PW - 1], 0.0).then_inc(border, 1)
            pool.wait_ge(xn, 1)
            for t in range(TT):
                for y in range(PS):
                    pool.tensor_scalar(patch_tiles(xp, t, y), patch_order(x, t, y), gm, rstd, ALU.subtract, ALU.mult)\
                        .then_inc(k.sem("patches_ready"), 1)

        @block.vector
        def _(dve):
            step = Chain(dve, vch)
            for n in range(2):
                for t in range(PT):
                    dve.tensor_scalar(diag[:, n, t, :], k.ident[:, :], k.convw[:, n, t:t + 1], None, ALU.mult).then_inc(diag_s, 1)
            for n in range(NCH):
                step(dve.bn_stats(stats[:, n, :], x[:, n * CH:(n + 1) * CH]))
            step(dve.bn_aggr(mv, stats))
            step(dve.tensor_copy(g2[:, 0:1], mv[:, 0:1]))
            dve.scalar_tensor_tensor(g2[:, 1:2], mv[:, 0:1], mv[:, 0:1], mv[:, 1:2], ALU.mult, ALU.add).then_inc(gn_in, 1)
            dve.wait_ge(gn_sum, 1)
            step(dve.tensor_copy(gm, k.bank(0, 1)))
            step(dve.tensor_tensor(t0, gm, gm, ALU.mult))
            step(dve.tensor_tensor(t0, k.bank(0, 1, 1), t0, ALU.subtract))
            dve.tensor_scalar(t0, t0, 1e-5, None, ALU.add).then_inc(gn_var, 1)
            dve.wait_ge(gn_std, 1)
            step(dve.reciprocal(rstd, rstd))
            step(dve.tensor_tensor(t1, rstd, rstd, ALU.mult))
            step(dve.tensor_tensor(t1, t1, t0, ALU.mult))
            step(dve.tensor_scalar(t1, t1, -0.5, 1.5, ALU.mult, ALU.add))
            step(dve.tensor_tensor(rstd, rstd, t1, ALU.mult))
            dve.wait_ge(border, 4)
            dve.tensor_scalar(inner[0], x.rearrange("p (h w) -> p h w", w=W), gm, rstd, ALU.subtract, ALU.mult).then_inc(xn, 1)
            def taps(i, g):
                dve.wait_ge(conv, NG * i + g + 1)
                for j in range(PT, 9):
                    if j > PT:
                        dve.wait_ge(taps_s, (NG * i + g) * (9 - PT) + (j - PT))
                    ins = dve.scalar_tensor_tensor(group(feat, g), tap(i, g, j), k.convw[:, i, j:j + 1],
                                                   group(k.ps, pair(i, g)) if j == PT else group(feat, g), ALU.mult, ALU.add)
                    ins.then_inc(taps_s, 1)

            for g in range(NG):
                taps(0, g)
            dve.wait_ge(stored, 32)
            dve.wait_ge(sums, 2)
            step(dve.tensor_copy(rows[0], k.bank(6)))
            step(dve.scalar_tensor_tensor(rows[1], rows[0], -1.0 / C, rows[0], ALU.mult, ALU.mult))
            dve.tensor_tensor(rows[1], k.bank(7), rows[1], ALU.add).then_inc(pv, 1)
            taps(1, 0)
            dve.wait_ge(gelu[0], NG)
            step(dve.reduce_sum(ctot, csum, axis=AX.X))
            dve.tensor_scalar(ctot, ctot, 1.0 / L, None, ALU.mult).then_inc(csm, 1)
            taps(1, 1)
            dve.wait_ge(hmm, 1)
            dve.tensor_scalar(hid, k.bank(6, 1)[0:C // 4, :], 0.0, None, ALU.max).then_inc(hre, 1)
            taps(1, 2)
            taps(1, 3)
            dve.wait_ge(pe_in, 16 * TT * PS * 8)
            for g in range(NT // 4):
                dve.wait_ge(tr, g + 1)
                dve.tensor_tensor(xt[:, g * CH:(g + 1) * CH], k.bank(token_bank[g]), pe_t[:, g * CH:(g + 1) * CH], ALU.add)\
                    .then_inc(k.sem("tokens_embedded"), 1)
                dve.wait_ge(k.sem("tokens_embedded"), g + 1)
                for i in range(4 * g, 4 * g + 4):
                    dve.bn_stats(st[:, i, :], xt[:, i * 128:(i + 1) * 128]).then_inc(xt_s, 1)
            dve.wait_ge(xt_s, NT)
            for i in range(NT):
                dve.bn_aggr(tmv[:, i, :], st[:, i, :]).then_inc(xt_s, 1)
            dve.wait_ge(xt_s, 2 * NT)
            dve.tensor_scalar(rs, tmv[:, :, 1], 1e-5, None, ALU.add).then_inc(xtr, 1)
            dve.wait_ge(sigs, 2)
            step(dve.tensor_scalar(rows[3], rows[3], 0.3, None, ALU.mult))
            step(dve.scalar_tensor_tensor(rows[4], rows[2], 0.7, rows[3], ALU.mult, ALU.add))
            step(dve.reduce_sum(rows[5][:, 0:128], rows[4].rearrange("p (n x) -> p n x", x=PS), axis=AX.X))
            step(dve.reduce_sum(rows[0][:, 0:32].rearrange("p (h w) -> p h w", h=2),
                                rows[5][:, 0:128].rearrange("p (h y w) -> p h w y", h=2, y=PS), axis=AX.X))
            dve.scalar_tensor_tensor(bd, rows[0][:, 0:32].unsqueeze(1).broadcast_to([128, NCH, 32]), 1.0 / OFF,
                                     k.rowmask[:, :, :], ALU.mult, ALU.mult).then_inc(bd_s, 1)
            dve.wait_ge(std, 1)
            step(dve.reciprocal(rs, rs))
            for i in range(NT):
                dve.tensor_scalar(xt[:, i * 128:(i + 1) * 128], xt[:, i * 128:(i + 1) * 128], tmv[:, i, 0:1], rs[:, i:i + 1],
                                  ALU.subtract, ALU.mult).then_inc(nrm, 1)
            dve.wait_ge(bc, 1)
            step(dve.tensor_copy(smb, k.bank(3, NP_)))
            for t in range(TT):
                step(dve.scalar_tensor_tensor(junk[:, 0:128], smb[:, 128 * t:128 * t + 128], 1.0, k.ident[:, :],
                                              ALU.mult, ALU.mult, accum_out=colv[:, t:t + 1]))
                step(dve.scalar_tensor_tensor(junk, smb, colv[:, t:t + 1], k.lower[:, t, :], ALU.is_equal, ALU.mult))
                step(dve.scalar_tensor_tensor(junk, smb, colv[:, t:t + 1], junk, ALU.is_gt, ALU.add,
                                              accum_out=rank[:, t:t + 1]))
                dve.tensor_scalar(k.perm[:, t, :], k.iota[:, :], rank[:, t:t + 1], None, ALU.is_equal).then_inc(pm, 1)
            dve.wait_ge(pt, 1)
            dve.tensor_copy(k.permt[:, :, :].rearrange("p a b -> p (a b)"), k.bank(7)).then_inc(k.sem("permt_ready"), 1)

        @block.scalar
        def _(act):
            act.wait_ge(gn_var, 1)
            act.activation(rstd, t0, ACT.Sqrt).then_inc(gn_std, 1)
            act.wait_ge(xn, 1)
            act.activation(sq.rearrange("p (h w) -> p h w", w=W), inner[0], ACT.Square).then_inc(sq_s, 1)
            act.wait_ge(border, 4)
            for g in range(NG):
                act.wait_ge(taps_s, (g + 1) * (9 - PT))
                act.activation(pad[1][:, 1 + RG * g:1 + RG * g + RG, 1:W + 1], group(feat, g), ACT.Gelu,
                               bias=k.cols[:, C_B1:C_B1 + 1], accum_out=csum[:, g:g + 1]).then_inc(gelu[0], 1)
            act.wait_ge(amm, 1)
            act.activation(ca, k.bank(7, 1), ACT.Sigmoid).then_inc(ca_s, 1)
            act.wait_ge(ca_s, 1)
            for g in range(NG):
                act.wait_ge(taps_s, (NG + g + 1) * (9 - PT))
                act.activation(group(feat, g), group(feat, g), ACT.Gelu, scale=ca, bias=k.cols[:, C_B2:C_B2 + 1]).then_inc(gelu[1], 1)
            act.wait_ge(head, 1)
            act.wait_ge(stored, 32)
            act.activation(rows[2], k.bank(6), ACT.Sigmoid, bias=k.cols[:, C_HB:C_HB + 1]).then_inc(sigs, 1)
            act.wait_ge(pv, 1)
            act.activation(rows[3], rows[1], ACT.Sigmoid, scale=10.0 / (C - 1)).then_inc(sigs, 1)
            act.wait_ge(xtr, 1)
            act.activation(rs, rs, ACT.Sqrt).then_inc(std, 1)
            for g in range(OFF // 2):
                act.wait_ge(pmm, g + 1)
                act.activation(x1v[:, 2 * g:2 * g + 2, :], k.bank(g).rearrange("p (o s) -> p o s", o=2), ACT.Identity,
                               bias=k.cols[:, C_NB:C_NB + 1], scale=k.cols[:, C_G:C_G + 1]).then_inc(k.sem("x1_ready"), 1)

        @block.tensor
        def _(pe):
            pe.wait_ge(gn_in, 1)
            pe.matmul(k.bank(0, 2), k.group[:, :, :].rearrange("p a b -> p (a b)"), g2, start=True, stop=True).then_inc(gn_sum, 1)
            pe.wait_ge(diag_s, 2 * PT)
            pe.wait_ge(xn, 1)

            def taps(i, g):
                job = NG * i + g
                if i == 1:
                    pe.wait_ge(gelu[0], min(g + 2, NG))
                if job >= 3:
                    pe.wait_ge(taps_s, (job - 3) * (9 - PT) + 1)
                for n in range(2):
                    for j in range(PT):
                        last = pe.matmul(k.bank(pair(i, g) * 2 + n).rearrange("p (h w) -> p h w", w=W), diag[:, i, j, :],
                                         tap(i, g, j)[:, n * RG // 2:(n + 1) * RG // 2, :], start=j == 0, stop=j == PT - 1)
                last.then_inc(conv, 1)

            def over_channels(bank, window, rhs):
                for a in range(2):
                    for b in range(NCH // 2):
                        last = pe.matmul(bank[32 * b:32 * b + 32, :], window[:, 1 - a:33 - a], rhs(2 * b + a),
                                         start=a == 0, stop=a == 1, tile_position=(0, 32 * b))
                return last

            for g in range(NG):
                taps(0, g)
            over_channels(k.bank(6), k.owin, lambda n: pad[0][:, 1 + n * RG // 2:1 + (n + 1) * RG // 2, 1:W + 1]).then_inc(sums, 1)
            pe.wait_ge(sq_s, 1)
            over_channels(k.bank(7), k.owin, lambda n: sq[:, n * CH:(n + 1) * CH]).then_inc(sums, 1)
            taps(1, 0)
            taps(1, 1)
            pe.wait_ge(csm, 1)
            pe.wait_ge(pv, 1)
            pe.matmul(k.bank(6, 1)[0:C // 4, :], k.ca1[:, :], ctot, start=True, stop=True).then_inc(hmm, 1)
            taps(1, 2)
            pe.wait_ge(hre, 1)
            pe.matmul(k.bank(7, 1), k.ca2[:, :], hid, start=True, stop=True).then_inc(amm, 1)
            taps(1, 3)

            def token_tiles(g):
                if g < 6:
                    pe.wait_ge(taps_s, (2 * NG - 3 + g // 2) * (9 - PT) + 1)
                else:
                    pe.wait_ge(k.sem("tokens_embedded"), g - 5)
                pe.wait_ge(k.sem("patches_ready"), g + 1)
                for i in range(4):
                    at = g * CH + 128 * i
                    last = pe.transpose(k.bank(token_bank[g], 128, 128 * i), xp[:, at:at + 128], k.ident[:, :])
                last.then_inc(tr, 1)

            for g in range(6):
                token_tiles(g)
            pe.wait_ge(gelu[1], NG)
            over_channels(k.bank(6), k.hwin, lambda n: feat[:, n * CH:(n + 1) * CH]).then_inc(head, 1)
            token_tiles(6)
            token_tiles(7)
            pe.wait_ge(bd_s, 1)
            pe.matmul(k.bank(3, NP_), k.ones[:, :], bd.rearrange("p n q -> p (n q)"), start=True, stop=True).then_inc(bc, 1)
            for t in range(TT):
                pe.wait_ge(pm, t + 1)
                for u in range(TT):
                    last = pe.transpose(k.bank(7, 128, NP_ * u + 128 * t), k.perm[:, t, 128 * u:128 * u + 128], k.ident[:, :])
            last.then_inc(pt, 1)
            pe.wait_ge(nrm, NT)
            for o in range(0, OFF, 2):
                if o == OFF - 2:
                    pe.wait_ge(k.sem("permt_ready"), 1)
                for oo in (o, o + 1):
                    for t in range(TT):
                        last = pe.matmul(k.bank(o // 2, NP_, (oo % 2) * NP_), xt[:, (t * OFF + oo) * 128:(t * OFF + oo + 1) * 128],
                                         k.perm[:, t, :], start=t == 0, stop=t == TT - 1)
                last.then_inc(pmm, 1)
    k.clear()


XC_AT, SZ_AT, DBC_AT, XI_AT = 0, 8192, 16384, 20480


def project(k):
    nc = k.nc
    x1 = k.at(X1_AT, L)
    xc = k.at(XC_AT, HD * L).rearrange("p (h n) -> p h n", h=HD)
    sz = k.at(SZ_AT, HD * L).rearrange("p (h n) -> p h n", h=HD)
    dbc = k.at(DBC_AT, L)
    xi = k.at(XI_AT, HD * (DC - 1 + L)).rearrange("p (h n) -> p h n", h=HD)
    xi_mm, z_mm, xp_mm, xi_ev, z_ev, xp_ev, tap_s, xc_s = (k.sem(n) for n in (
        "xi_mm", "z_mm", "xproj_mm", "xi_ready", "z_ready", "dbc_ready", "taps_added", "xc_ready"))

    with nc.Block() as block:
        @block.tensor
        def _(pe):
            def xproj(c):
                pe.wait_ge(xc_s, c * HD + HD)
                pe.wait_ge(xp_ev, c + 1)
                for h in range(HD):
                    last = pe.matmul(k.bank(4), k.xpw[:, h, :], xc[:, h, cols_of(c)], start=h == 0, stop=h == HD - 1)
                last.then_inc(xp_mm, 1)

            def inproj(c):
                for h in range(HD):
                    pe.wait_ge(xi_ev, c * HD + (h + 1))
                    pe.matmul(k.bank(h), k.wx[:, h * 128:(h + 1) * 128], x1[:, cols_of(c)], start=True, stop=True).then_inc(xi_mm, 1)
                for h in range(HD):
                    pe.wait_ge(z_ev, c * HD + (h + 1))
                    pe.matmul(k.bank(2 + h), k.wz[:, h * 128:(h + 1) * 128], x1[:, cols_of(c)], start=True, stop=True).then_inc(z_mm, 1)

            inproj(0)
            with pe.Fori(1, NCH) as c:
                inproj(c)
                xproj(c - 1)
            xproj(NCH - 1)

        @block.scalar
        def _(act):
            def keep_xi(c):
                for h in range(HD):
                    act.wait_ge(xi_mm, c * HD + (h + 1))
                    act.activation(xi[:, h, cols_of(c, CH, DC - 1)], k.bank(h), ACT.Copy).then_inc(xi_ev, 1)

            def silu_x(c):
                for h in range(HD):
                    act.wait_ge(tap_s, c * (HD * DC) + (HD * (DC - 1) + h + 1))
                    act.activation(xc[:, h, cols_of(c)], xc[:, h, cols_of(c)], ACT.Silu,
                                   bias=k.cols[:, C_CB + h:C_CB + h + 1]).then_inc(xc_s, 1)

            def silu_z(c):
                for h in range(HD):
                    act.wait_ge(z_mm, c * HD + (h + 1))
                    act.activation(sz[:, h, cols_of(c)], k.bank(2 + h), ACT.Silu).then_inc(z_ev, 1)

            def keep_dbc(c):
                act.wait_ge(xp_mm, c + 1)
                act.activation(dbc[:, cols_of(c)], k.bank(4), ACT.Copy).then_inc(xp_ev, 1)

            for s, n in ((xi_ev, HD), (z_ev, HD), (xp_ev, 1)):
                act.sem_inc(s, n)
            keep_xi(0)
            silu_z(0)
            with act.Fori(1, NCH) as c:
                keep_xi(c)
                silu_x(c - 1)
                silu_z(c)
                keep_dbc(c - 1)
            silu_x(NCH - 1)
            keep_dbc(NCH - 1)

        @block.vector
        def _(dve):
            dve.memset(xi[:, :, 0:DC - 1], 0.0).then_inc(k.sem("xi_pad"), 1)
            dve.wait_ge(k.sem("xi_pad"), 1)
            with dve.Fori(0, NCH) as c:
                dve.wait_ge(xi_ev, c * HD + (2 * HD))
                for t in range(DC):
                    for h in range(HD):
                        src, w, out = xi[:, h, cols_of(c, CH, t)], k.taps[:, h, t:t + 1], xc[:, h, cols_of(c)]
                        if t == 0:
                            dve.tensor_scalar(out, src, w, None, ALU.mult).then_inc(tap_s, 1)
                        else:
                            dve.wait_ge(tap_s, c * (HD * DC) + (HD * (t - 1) + h + 1))
                            dve.scalar_tensor_tensor(out, src, w, out, ALU.mult, ALU.add).then_inc(tap_s, 1)
    k.clear()


def cols_of(c, n=CH, at=0):
    return slice(c * n + at, (c + 1) * n + at) if isinstance(c, int) else bass.ds(c * n + at, n)


def scan(k):
    nc = k.nc
    xc = k.at(XC_AT, HD * L).rearrange("p (h n) -> p h n", h=HD)
    sz = k.at(SZ_AT, HD * L).rearrange("p (h n) -> p h n", h=HD)
    dbc = k.at(DBC_AT, L)
    at = [DBC_AT + L]

    def ring(n, cols=HD * CH):
        out = [k.at(at[0] + i * cols, cols) for i in range(n)]
        at[0] += n * cols
        return out

    def halves(t):
        return t.rearrange("p (h n) -> p h n", h=HD)

    dt, u = ring(2), ring(2)
    (ab,), (onep,), (rx,) = ring(1), ring(1), ring(1)
    rest = onep[:, 0:CH]
    pieces = [t.bitcast(BF16) for t in ring(2, CH // 2)]
    da, dbx, hb, g, cs = ring(4), ring(2), ring(4), ring(4), ring(3, CH)
    assert at[0] <= ARENA
    dt_mm, ab_s, e_s, w_s, q_s, ln_s, rx_s, dt_s, hi_s, mid_s, r_s, pc_s = (k.sem(n) for n in (
        "dt_mm", "dt_abs", "dt_exp", "dt_onep", "dt_rest", "dt_ln", "dt_relu", "dt_ready", "high_ready", "middle_ready",
        "remainder", "pieces_ready"))
    b_mm, c_mm, y_mm, da_s, dbx_s, sc_s, hl_s, hp_s, hv_s, cs_s, fin_s = (k.sem(n) for n in (
        "b_mm", "c_mm", "y_mm", "da_ready", "dbx_ready", "scan_done", "hlast_saved", "hc_gpsimd", "hc_vector", "c_copied",
        "chunk_done"))

    def pooled(s):
        return s % 4 != 3

    NP = sum(pooled(s) for s in range(DS))
    NV = DS - NP

    def count(kind, c, s):
        n = NP if kind else NV
        if s < 0:
            return c * n + sum(pooled(i) == kind for i in range(s + DS + 1))
        return c * n + (n + sum(pooled(i) == kind for i in range(s + 1)))

    def chunks(prepare, body, eng):
        prepare(0, 0)
        for q in range(2):
            body(q, q, True)
        with eng.Fori(1, NCH // 2 - 1) as cc:
            for q in range(2):
                body(cc * 2 + q, q, True)
        body(NCH - 2, 0, True)
        body(NCH - 1, 1, False)

    def first(c):
        return isinstance(c, int) and c == 0

    with nc.Block() as block:
        @block.tensor
        def _(pe):
            def prepare(c, q):
                if not first(c):
                    pe.wait_ge(rx_s, c * 2)
                for h in range(HD):
                    last = pe.matmul(k.bank(h), k.dtw[:, h * 128:(h + 1) * 128], dbc[:, cols_of(c)], start=True, stop=True)
                last.then_inc(dt_mm, 1)

            def total(c, s):
                pe.wait_ge(hp_s if pooled(s) else hv_s, count(pooled(s), c, s))
                if s == 0:
                    pe.wait_ge(fin_s, c * 1 + 1)
                    for h in range(HD):
                        pe.matmul(k.bank(6 + h), k.dmat[:, h, :], xc[:, h, cols_of(c)], start=True, stop=False)
                for h in range(HD):
                    last = pe.matmul(k.bank(6 + h), k.ident[:, :], halves(g[s % 4])[:, h, :], start=False, stop=s == DS - 1)
                last.then_inc(y_mm, 1)

            def body(c, q, more):
                pe.wait_ge(pc_s, c * 1 + 1)
                for s in range(DS):
                    n = c * DS + s
                    pe.wait_ge(dbx_s, n + 1)
                    pe.matmul(k.bank(2 + s % 2), k.sel[:, s, :], pieces[q], start=True, stop=True).then_inc(b_mm, 1)
                    kind = pooled((s - 2) % DS)
                    pe.wait_ge(cs_s if kind else hv_s, count(kind, c, s - 2))
                    pe.matmul(k.bank(4 + s % 2), k.sel[:, DS + s, :], pieces[q], start=True, stop=True).then_inc(c_mm, 1)
                    if s >= 4:
                        total(c, s - 4)
                    elif not first(c):
                        total(c - 1, s - 4 + DS)
                    if more and s == 0:
                        prepare(c + 1, 1 - q)
            chunks(prepare, body, pe)
            for s in range(DS - 4, DS):
                total(NCH - 1, s)

        @block.scalar
        def _(act):
            def abs_exp(c):
                act.wait_ge(dt_mm, c * 1 + 1)
                for h in range(HD):
                    act.activation(halves(ab)[:, h, :], k.bank(h), ACT.Abs, bias=k.cols[:, C_DTB + h:C_DTB + h + 1]).then_inc(ab_s, 1)
                for h in range(HD):
                    act.activation(halves(rx)[:, h, :], k.bank(h), ACT.Relu, bias=k.cols[:, C_DTB + h:C_DTB + h + 1]).then_inc(rx_s, 1)
                act.wait_ge(ab_s, c * 2 + 2)
                act.activation(ab, ab, ACT.Exp, scale=-1.0).then_inc(e_s, 1)

            def one_plus(c):
                act.wait_ge(e_s, c * 1 + 1)
                act.wait_ge(pc_s, c * 1 + 1)
                act.activation(onep, ab, ACT.Identity, bias=k.cols[:, C_ONE:C_ONE + 1]).then_inc(w_s, 1)

            def log(c):
                act.wait_ge(q_s, c * 1 + 1)
                act.activation(onep, onep, ACT.Ln).then_inc(ln_s, 1)

            def high(c, q):
                act.activation(pieces[q][0:96, :], dbc[0:96, cols_of(c)], ACT.Copy).then_inc(hi_s, 1)

            def middle(c, q):
                act.wait_ge(r_s, c * 1 + 1)
                act.activation(pieces[q][0:64, :], rest[0:64, :], ACT.Copy).then_inc(mid_s, 1)

            def body(c, q, more):
                act.wait_ge(dt_s, c * 2 + 1)
                for s in range(DS):
                    act.wait_ge(sc_s, c * (2 * DS) + (2 * s + 2))
                    for h in range(HD):
                        act.activation(halves(da[s % 4])[:, h, :], halves(dt[q])[:, h, :], ACT.Exp,
                                       scale=k.amat[:, h, s:s + 1]).then_inc(da_s, 1)
                    if pooled(s):
                        act.wait_ge(c_mm, c * DS + (s + 1))
                        act.wait_ge(hp_s, count(True, c, s - 4))
                        act.activation(cs[s % 4], k.bank(4 + s % 2), ACT.Copy).then_inc(cs_s, 1)
                    if more and s == 0:
                        high(c + 1, 1 - q)
                    if more and s == 2:
                        abs_exp(c + 1)
                    if more and s == 3:
                        middle(c + 1, 1 - q)
                    if more and s == 7:
                        one_plus(c + 1)
                    if more and s == 10:
                        log(c + 1)
            chunks(lambda c, q: (abs_exp(c), high(c, q), middle(c, q), one_plus(c), log(c)), body, act)

        @block.gpsimd
        def _(pool):
            def wait(sem, value):
                pool.wait_ge(sem, value)
                pool.sem_inc(k.sem("pool_waits_met"), 1)

            def remainder(c, q):
                wait(hi_s, c * 1 + 1)
                pool.tensor_tensor(rest[0:64, :], dbc[0:64, cols_of(c)], pieces[q][0:64, :], ALU.subtract).then_inc(r_s, 1)

            def low(c, q):
                wait(mid_s, c * 1 + 1)
                pool.tensor_tensor(pieces[q][0:32, :], rest[0:32, :], pieces[q][0:32, :], ALU.subtract).then_inc(pc_s, 1)

            def softplus(c, q, part):
                if part == 0:
                    wait(ln_s, c * 1 + 1)
                    pool.tensor_tensor(onep, onep, ab, ALU.subtract).then_inc(k.sem("log1p"), 1)
                if part == 1:
                    wait(k.sem("log1p"), c * 1 + 1)
                    wait(rx_s, c * 2 + 2)
                    pool.tensor_tensor(dt[q], onep, rx, ALU.add).then_inc(dt_s, 1)
                if part == 2:
                    wait(dt_s, c * 2 + 1)
                    pool.tensor_tensor(halves(u[q]), halves(dt[q]), xc[:, :, cols_of(c)], ALU.mult).then_inc(dt_s, 1)

            def body(c, q, more):
                for s in range(DS):
                    wait(sc_s, c * (2 * DS) + (2 * s + 2 + 8))
                    pool.tensor_copy(k.hlast[:, s, :, :], halves(hb[s % 4])[:, :, CH - 1:CH]).then_inc(hl_s, 1)
                    if pooled(s):
                        wait(cs_s, count(True, c, s))
                        wait(y_mm, c * DS + (s + 1))
                        pool.tensor_tensor(halves(g[s % 4]), halves(hb[s % 4]), cs[s % 4].unsqueeze(1).broadcast_to([128, HD, CH]),
                                           ALU.mult).then_inc(hp_s, 1)
                    if more and s == 0:
                        remainder(c + 1, 1 - q)
                    if more and s == 5:
                        low(c + 1, 1 - q)
                    if more and s in (10, 11, 13):
                        softplus(c + 1, 1 - q, (10, 11, 13).index(s))

            def prepare(c, q):
                for p in pieces:
                    pool.memset(p[96:128, :], 0.0).then_inc(k.sem("p_zero"), 1)
                pool.wait_ge(k.sem("p_zero"), 2)
                pool.memset(k.hlast[:, :, :, :], 0.0).then_inc(k.sem("h_zero"), 1)
                pool.wait_ge(k.sem("h_zero"), 1)
                pool.sem_inc(hl_s, DS)
                pool.sem_inc(hp_s, NP)
                remainder(c, q)
                low(c, q)
                for part in range(3):
                    softplus(c, q, part)
            chunks(prepare, body, pool)

        @block.vector
        def _(dve):
            def rounding(c):
                dve.wait_ge(w_s, c * 1 + 1)
                dve.scalar_tensor_tensor(ab, onep, 1.0, ab, ALU.subtract, ALU.subtract).then_inc(q_s, 1)

            def inject(c, q, s):
                if s == 0:
                    dve.wait_ge(dt_s, c * 2 + 2)
                dve.wait_ge(b_mm, c * DS + (s + 1))
                dve.tensor_tensor(halves(dbx[s % 2]), halves(u[q]), k.bank(2 + s % 2).unsqueeze(1).broadcast_to([128, HD, CH]),
                                  ALU.mult).then_inc(dbx_s, 1)

            def finish(c):
                dve.wait_ge(y_mm, c * DS + (DS + 4))
                dve.tensor_tensor(sz[:, :, cols_of(c)], k.bank(6, 2 * CH).rearrange("p (h n) -> p h n", h=HD), sz[:, :, cols_of(c)],
                                  ALU.mult).then_inc(fin_s, 1)

            def body(c, q, more):
                inject(c, q, 0)
                for s in range(DS):
                    dve.wait_ge(hl_s, c * DS + (s - 3 + DS))
                    kind = pooled((s - 4) % DS)
                    dve.wait_ge(hp_s if kind else hv_s, count(kind, c, s - 4))
                    dve.wait_ge(dbx_s, c * DS + (s + 1 + 2))
                    for h in range(HD):
                        dve.wait_ge(da_s, c * (2 * DS) + (2 * s + h + 1))
                        dve.tensor_tensor_scan(halves(hb[s % 4])[:, h, :], halves(da[s % 4])[:, h, :], halves(dbx[s % 2])[:, h, :],
                                               k.hlast[:, s, h, :], ALU.mult, ALU.add).then_inc(sc_s, 1)
                        if h == 0 and s < DS - 1:
                            if s >= 1:
                                dve.wait_ge(sc_s, c * (2 * DS) + (2 * s + 8))
                            inject(c, q, s + 1)
                    if not pooled(s):
                        dve.wait_ge(c_mm, c * DS + (s + 1))
                        dve.wait_ge(y_mm, c * DS + (s + 1))
                        dve.wait_ge(sc_s, c * (2 * DS) + (2 * s + 2 + 8))
                        dve.tensor_tensor(halves(g[s % 4]), halves(hb[s % 4]), k.bank(4 + s % 2).unsqueeze(1).broadcast_to([128, HD, CH]),
                                          ALU.mult).then_inc(hv_s, 1)
                    if more and s == 8:
                        rounding(c + 1)
                    if s == 2 and not first(c):
                        finish(c - 1)

            dve.sem_inc(dbx_s, 2)
            dve.sem_inc(hv_s, NV)
            dve.sem_inc(cs_s, NP)
            dve.sem_inc(sc_s, 8)
            dve.sem_inc(fin_s, 1)
            dve.sem_inc(y_mm, 4)
            chunks(lambda c, q: rounding(c), body, dve)
            finish(NCH - 1)
    k.clear()


T_AT = 20480


def unsort(k, b):
    nc = k.nc
    y = k.at(SZ_AT, HD * L).rearrange("p (h n) -> p h n", h=HD)
    om, x, xp, t1 = k.at(DBC_AT, L), k.at(0, L), k.at(4096, L), k.at(T_AT, L)
    x_in, xp_s, o_mm, o_ev, t_mm = (k.sem(n) for n in ("x_in", "patches_ready", "outproj_mm", "outproj_read", "unsort_mm"))
    t_ev = k.sem("tokens_ready")
    with nc.Block() as block:
        @block.sync
        def _(sp):
            for i in range(4):
                sp.dma_start(x[:, i * 1024:(i + 1) * 1024], k.ins["x"][b, :, i * 1024:(i + 1) * 1024]).then_inc(x_in, 16)

        @block.gpsimd
        def _(pool):
            pool.wait_ge(x_in, 64)
            for t in range(TT):
                for r in range(PS):
                    pool.tensor_copy(patch_tiles(xp, t, r), patch_order(x, t, r)).then_inc(xp_s, 1)

        @block.tensor
        def _(pe):
            for i in range(NT):
                u, o = i // OFF, i % OFF
                for h in range(HD):
                    first = u * 128 * OFF + o
                    last = pe.matmul(k.ps[:, i * 128:(i + 1) * 128], y[:, h, first:first + 127 * OFF + 1:OFF], k.outw[:, h, :],
                                     start=h == 0, stop=h == HD - 1)
                if i % 4 == 3:
                    last.then_inc(o_mm, 1)
            pe.wait_ge(o_ev, NT // 4)
            for g in range(NT // 4):
                t, o4 = g // 4, g % 4
                for u in range(TT):
                    pe.matmul(k.bank(g), k.permt[:, u, t * 128:(t + 1) * 128], om[:, u * OFF * 128 + o4 * CH:u * OFF * 128 + (o4 + 1) * CH],
                              start=u == 0, stop=False)
                pe.wait_ge(xp_s, g + 1)
                for j in range(4):
                    last = pe.matmul(k.bank(g, 128, 128 * j), xp[:, g * CH + 128 * j:g * CH + 128 * j + 128], k.ident[:, :],
                                     start=False, stop=j == 3)
                last.then_inc(t_mm, 1)

        @block.scalar
        def _(act):
            for g in range(0, NT // 4):
                act.wait_ge(o_mm, g + 1)
                act.activation(om[:, g * CH:(g + 1) * CH], k.bank(g), ACT.Copy).then_inc(o_ev, 1)

        @block.vector
        def _(dve):
            for g in range(NT // 4):
                dve.wait_ge(t_mm, g + 1)
                dve.tensor_copy(t1[:, g * CH:(g + 1) * CH], k.bank(g)).then_inc(t_ev, 1)
                dve.wait_ge(t_ev, g + 1)
                tile_stats(k, dve, g, TN_AT, T_AT)
    k.clear()


def tile_stats(k, dve, g, tn_at, x_at):
    x = k.at(x_at, L)
    st = k.at(tn_at, NT * 6).rearrange("p (n s) -> p n s", s=6)
    for i in range(4 * g, 4 * g + 4):
        dve.bn_stats(st[:, i, :], x[:, i * 128:(i + 1) * 128]).then_inc(k.sem("ln_stats"), 1)


def normalize(k, dve, act, tn_at, x_at, eps):
    x, tn = k.at(x_at, L), k.at(tn_at, L)
    S = k.small
    st = k.at(tn_at, NT * 6).rearrange("p (n s) -> p n s", s=6)
    mv = S[:, 0:NT * 2].rearrange("p (n s) -> p n s", s=2)
    rs = S[:, 64:64 + NT]
    var_s, std_s, st_s, tn_s = k.sem("ln_var"), k.sem("ln_std"), k.sem("ln_stats"), k.sem("ln_done")
    if act is not None:
        act.wait_ge(var_s, 1)
        act.activation(rs, rs, ACT.Sqrt).then_inc(std_s, 1)
        return
    for i in range(NT):
        dve.bn_aggr(mv[:, i, :], st[:, i, :]).then_inc(st_s, 1)
    dve.wait_ge(st_s, NT)
    dve.tensor_scalar(rs, mv[:, :, 1], eps, None, ALU.add).then_inc(var_s, 1)
    dve.wait_ge(std_s, 1)
    dve.reciprocal(rs, rs).then_inc(st_s, 1)
    dve.wait_ge(st_s, NT + 1)
    for i in range(NT):
        dve.tensor_scalar(tn[:, i * 128:(i + 1) * 128], x[:, i * 128:(i + 1) * 128], mv[:, i, 0:1], rs[:, i:i + 1],
                          ALU.subtract, ALU.mult).then_inc(tn_s, 1)


TN_AT, TNT_AT = 24576, 28672
QF_AT, KF_AT, KH_AT, KL_AT, QH_AT, QL_AT = 0, 4096, 8192, 10240, 40960, 24576
QS_AT, KS_AT, V_AT, SUM_AT, RL_AT = 0, 32768, 16384, 26624, 43008
S_MV, S_SSQ, S_MAX, S_SC, S_U, S_PART = 0, 100, 102, 104, 106, 112


def stack_heads(k, sp, to, high_at, low_at, high_groups, a, b, done):
    hi, lo = (k.at(at, L // 2).bitcast(F16) for at in (high_at, low_at))
    stack = k.at(to, 2 * L).bitcast(F16).rearrange("p (h n) -> p h n", h=HEADS)
    for g in range(4):
        src = hi if g in high_groups else lo
        for h in range(HEADS):
            sp.dma_start(stack[32 * g:32 * g + 32, h, a:b], src[32 * h:32 * h + 32, a:b]).then_inc(done, 16)


def qkv(k):
    nc = k.nc
    K_, Q_ = 0, 1
    tn, tnt = k.at(TN_AT, L), k.at(TNT_AT, L)
    full = [k.at(a, L) for a in (KF_AT, QF_AT)]
    square = [tn, k.at(12288, L)]
    hi = [k.at(a, L // 2).bitcast(F16) for a in (KH_AT, QH_AT)]
    lo = [k.at(a, L // 2).bitcast(F16) for a in (KL_AT, QL_AT)]
    v = k.at(V_AT, L)
    qstack = k.at(QS_AT, 2 * L).bitcast(F16).rearrange("p (h n) -> p h n", h=HEADS)
    q0_mm = k.sem("q0_mm")
    S = k.small
    ssq, mx, sc, u = (S[:, a:a + n] for a, n in ((S_SSQ, 2), (S_MAX, 2), (S_SC, 2), (S_U, 1)))
    part = S[:, S_PART:S_PART + 4 * NCH].rearrange("p (w m c) -> p w m c", w=2, m=2)
    tn_s, tr, tr_ev, mm, kept, sq_s, vmm, vev = (k.sem(n) for n in (
        "ln_done", "tr_done", "tnt_ready", "qk_mm", "qk_ready", "squares", "v_mm", "v_ready"))
    ss_s, root_s, split_s, stacked, umm = (k.sem(n) for n in ("norms_squared", "norm_roots", "split_done", "stacked", "bound_mm"))
    NG = NT // 4
    with nc.Block() as block:
        @block.tensor
        def _(pe):
            for i in range(NT):
                pe.wait_ge(tn_s, i + 1)
                last = pe.transpose(k.ps[:, i * 128:(i + 1) * 128], tn[:, i * 128:(i + 1) * 128], k.ident[:, :])
                if i % 4 == 3:
                    last.then_inc(tr, 1)
            for m in (K_, Q_):
                at = (1 - m) * C
                for c in range(NCH):
                    if m == K_:
                        pe.wait_ge(tr_ev, NG)
                    else:
                        pe.wait_ge(sq_s, c + 1)
                    pe.matmul(k.bank(c), k.wqkv[:, at:at + C], tnt[:, c * CH:(c + 1) * CH], start=True, stop=True).then_inc(mm, 1)
            for g in range(NG):
                pe.wait_ge(sq_s, NCH + g + 1)
                for i in range(4 * g, 4 * g + 4):
                    last = pe.matmul(k.ps[:, i * 128:(i + 1) * 128], tnt[:, i * 128:(i + 1) * 128], k.wqkv[:, 2 * C:3 * C], start=True, stop=True)
                last.then_inc(vmm, 1)
            pe.wait_ge(split_s, 2)
            for h in range(HEADS):
                pe.wait_ge(vev, h + 1)
                for w, src in enumerate((hi[Q_], lo[Q_])):
                    last = pe.matmul(k.bank(h), k.pick[:, w, h, :], src[:, 0:CH], start=w == 0, stop=w == 1)
                last.then_inc(q0_mm, 1)
            pe.wait_ge(root_s, 3)
            pe.wait_ge(vev, 5)
            pe.matmul(k.bank(4, 1)[0:1, :], u, k.ones[:, 0:1], start=True, stop=True).then_inc(umm, 1)

        @block.scalar
        def _(act):
            def root(m):
                act.wait_ge(ss_s, m + 1)
                act.activation(sc[:, m:m + 1], ssq[:, m:m + 1], ACT.Sqrt).then_inc(root_s, 1)

            normalize(k, None, act, TN_AT, T_AT, 1e-5)
            for g in range(NG):
                act.wait_ge(tr, g + 1)
                act.activation(tnt[:, g * CH:(g + 1) * CH], k.bank(g), ACT.Copy).then_inc(tr_ev, 1)
            for m in (K_, Q_):
                for c in range(NCH):
                    act.wait_ge(mm, m * NCH + c + 1)
                    act.activation(full[m][:, c * CH:(c + 1) * CH], k.bank(c), ACT.Copy).then_inc(kept, 1)
                    act.activation(square[m][:, c * CH:(c + 1) * CH], k.bank(c), ACT.Square,
                                   accum_out=part[:, 0, m, c:c + 1]).then_inc(sq_s, 1)
                    if m == Q_ and c == 2:
                        root(K_)
            root(Q_)
            for g in range(NG):
                act.wait_ge(vmm, g + 1)
                act.activation(v[:, g * CH:(g + 1) * CH], k.bank(g), ACT.Copy).then_inc(vev, 1)
            act.wait_ge(split_s, 3)
            for h in range(HEADS):
                act.wait_ge(q0_mm, h + 1)
                act.activation(qstack[:, h, 0:CH], k.bank(h), ACT.Copy).then_inc(k.sem("q0_stacked"), 1)

        @block.vector
        def _(dve):
            normalize(k, dve, None, TN_AT, T_AT, 1e-5)
            step = Chain(dve, k.sem("v_chain"))

            def split(m, a, b):
                step(dve.tensor_scalar(hi[m][:, a:b], full[m][:, a:b], sc[:, m:m + 1], None, ALU.mult))
                dve.scalar_tensor_tensor(lo[m][:, a:b], full[m][:, a:b], sc[:, m:m + 1], hi[m][:, a:b], ALU.mult, ALU.subtract)\
                    .then_inc(split_s, 1)

            for m in (K_, Q_):
                for c in range(NCH):
                    dve.wait_ge(sq_s, m * NCH + c + 1)
                    dve.reduce_max(part[:, 1, m, c:c + 1], square[m][:, c * CH:(c + 1) * CH], axis=AX.X).then_inc(k.sem("maxima"), 1)
                dve.wait_ge(k.sem("maxima"), (m + 1) * NCH)
                dve.reduce_sum(ssq[:, m:m + 1], part[:, 0, m, :], axis=AX.X).then_inc(ss_s, 1)
                step(dve.reduce_max(mx[:, m:m + 1], part[:, 1, m, :], axis=AX.X))
                s, x = sc[:, m:m + 1], mx[:, m:m + 1]
                dve.wait_ge(root_s, m + 1)
                step(dve.tensor_scalar(s, s, 1e-12, None, ALU.max))
                step(dve.reciprocal(s, s))
                step(dve.scalar_tensor_tensor(x, x, s, s, ALU.mult, ALU.mult))
                step(dve.tensor_scalar(s, s, SPLIT, None, ALU.mult))
                dve.wait_ge(kept, (m + 1) * NCH)
                if m == K_:
                    split(m, 0, L)
                else:
                    split(m, 0, CH)
                    split(m, CH, L)
            dve.tensor_tensor(u, mx[:, 0:1], mx[:, 1:2], ALU.mult).then_inc(root_s, 1)
            dve.wait_ge(umm, 1)
            dve.tensor_scalar(k.flag[0:1, 0:1], k.bank(4, 1)[0:1, :], (SAFE / SCALE) ** 2 / C, None, ALU.is_gt).then_inc(k.sem("flag"), 1)

        @block.sync
        def _(sp):
            sp.wait_ge(split_s, 1)
            stack_heads(k, sp, KS_AT, KH_AT, KL_AT, (0, 2), 0, L, stacked)
            sp.wait_ge(stacked, 4 * HEADS * 16)
    k.clear()


def attend(k):
    qs, ks = (k.at(a, 2 * L).bitcast(F16).rearrange("p (h n) -> p h n", h=HEADS) for a in (QS_AT, KS_AT))
    v, ao = k.at(V_AT, L), k.at(TNT_AT, L)
    probs = [k.at(8192 + i * 2 * CH, 2 * CH) for i in range(8)]
    acc = [k.at(SUM_AT + i * 2 * CH, 2 * CH) for i in range(2)]
    rl = k.at(RL_AT, CH)
    NJ, NPAIR = L // 128, 2 * (L // 128)
    s_mm, exp_s, pv_s, acc_s, l_mm, l_s, norm_s = (k.sem(n) for n in (
        "scores_mm", "probs_ready", "pv_mm", "probs_summed", "sums_mm", "sums_inverse", "chunk_normed"))
    O, LS = 6, 7
    group = [p % 3 for p in range(NPAIR - 1)] + [1]
    direct = [j for j in range(NJ) if j % 6 == 5]
    NA = NPAIR - 2 * len(direct)

    def summed(c, p):
        before, p = (0, p + NPAIR) if p < 0 else (NA, p)
        return c * NA + (before + sum(i // 2 not in direct for i in range(p + 1)))

    def tensor(pe):
        def ones_by(c, j, t, start, stop):
            for h in range(HEADS):
                last = pe.matmul(k.ps[32 * h:32 * h + 32, LS * CH:(LS + 1) * CH], k.ones[:, 0:32],
                                 t[h // 2][:, (h % 2) * CH:(h % 2 + 1) * CH], start=start, stop=stop, tile_position=(0, 32 * h))
            return last

        def weigh(c, j):
            pe.wait_ge(exp_s, c * NPAIR + (2 * j + 2 + 3))
            if j == 0:
                pe.wait_ge(norm_s, c + 1)
            if j in direct:
                ones_by(c, j, [probs[(2 * j + a) % 8] for a in range(2)], j == direct[0], False)
            for h in range(HEADS):
                last = pe.matmul(k.ps[32 * h:32 * h + 32, O * CH:(O + 1) * CH], v[:, j * 128 + 32 * h:j * 128 + 32 * h + 32],
                                 probs[(2 * j + h // 2) % 8][:, (h % 2) * CH:(h % 2 + 1) * CH],
                                 start=j == 0, stop=j == NJ - 1, tile_position=(0, 32 * h))
            last.then_inc(pv_s, 1)

        def finish(c):
            pe.wait_ge(acc_s, summed(c, NPAIR - 1))
            ones_by(c, 0, acc, False, True).then_inc(l_mm, 1)

        def body(c, first):
            for j in range(NJ):
                for a in range(2):
                    p = 2 * j + a
                    pe.wait_ge(exp_s, c * NPAIR + (p + (2 if p in (1, NPAIR - 1) else 1)))
                    for e in range(2):
                        h = 2 * a + e
                        last = pe.matmul(k.bank(2 * group[p] + e), ks[:, h, j * 128:(j + 1) * 128],
                                         qs[:, h, cols_of(c)], start=True, stop=True)
                    last.then_inc(s_mm, 1)
                    if p == 1 and not first:
                        weigh(c - 1, NJ - 1)
                    if p == 2 and not first:
                        finish(c - 1)
                if j in (3, 4):
                    weigh(c, 2 * j - 6)
                    weigh(c, 2 * j - 5)
                if j >= 5:
                    weigh(c, j - 1)

        body(0, True)
        pe.wait_ge(k.sem("q_rest"), 4 * HEADS * 16)
        with pe.Fori(1, NCH) as c:
            body(c, False)
        weigh(NCH - 1, NJ - 1)
        finish(NCH - 1)

    def scalar(act):
        act.sem_inc(exp_s, 3)
        with act.Fori(0, NCH) as c:
            for p in range(NPAIR):
                act.wait_ge(s_mm, c * NPAIR + (p + 1))
                act.wait_ge(pv_s, c * NJ + (p // 2 + 1))
                act.wait_ge(acc_s, summed(c, p - 8))
                act.activation(probs[p % 8], k.bank(2 * group[p], 2 * CH), ACT.Exp, scale=SCALE / SPLIT ** 2).then_inc(exp_s, 1)

    def vector(dve):
        dve.sem_inc(pv_s, 4)
        dve.sem_inc(acc_s, NA)
        dve.sem_inc(norm_s, 1)
        with dve.Fori(0, NCH) as c:
            for p in range(NPAIR):
                if p // 2 in direct:
                    continue
                dve.wait_ge(exp_s, c * NPAIR + (p + 1 + 3))
                if p < 2:
                    dve.tensor_copy(acc[p % 2], probs[p % 8]).then_inc(acc_s, 1)
                else:
                    dve.wait_ge(acc_s, summed(c, p) - 2)
                    dve.tensor_tensor(acc[p % 2], acc[p % 2], probs[p % 8], ALU.add).then_inc(acc_s, 1)
            dve.wait_ge(l_mm, c + 1)
            dve.reciprocal(rl, k.bank(LS)).then_inc(l_s, 1)
            dve.wait_ge(l_s, c + 1)
            dve.wait_ge(pv_s, c * NJ + (NJ + 4))
            dve.tensor_tensor(ao[:, bass.ds(c * CH, CH)], k.bank(O), rl, ALU.mult).then_inc(norm_s, 1)

    return tensor, scalar, vector


def attend_guarded(k):
    qs, ks = (k.at(a, 2 * L).bitcast(F16).rearrange("p (h n) -> p h n", h=HEADS) for a in (QS_AT, KS_AT))
    v, ao = k.at(V_AT, L), k.at(TNT_AT, L)
    probs = [k.at(8192 + i * 2 * CH, 2 * CH) for i in range(4)]
    mb = k.at(12288, HEADS * CH).rearrange("p (h n) -> p h n", h=HEADS)
    diag, mcol = k.at(14336, 128), k.small[:, 150:151]
    acc = [k.at(SUM_AT + i * 2 * CH, 2 * CH) for i in range(2)]
    rl = k.at(RL_AT, CH)
    NJ, NPAIR, NR = L // 128, 2 * (L // 128), HEADS * CH // 128
    row_mm, max_s, diag_s, spread_mm, mb_s, s_mm, shift_s, exp_s, pv_s, acc_s, l_mm, l_s, norm_s = (k.sem(n) for n in (
        "rows_mm", "max_ready", "diag_ready", "max_spread", "max_saved", "scores_mm", "shifted", "probs_ready", "pv_mm",
        "probs_summed", "sums_mm", "sums_inverse", "chunk_normed"))
    O, LS = 6, 7
    def tensor(pe):
        def weigh(c, j):
            pe.wait_ge(exp_s, c * NPAIR + (2 * j + 2))
            for h in range(HEADS):
                last = pe.matmul(k.ps[32 * h:32 * h + 32, O * CH:(O + 1) * CH], v[:, j * 128 + 32 * h:j * 128 + 32 * h + 32],
                                 probs[(2 * j + h // 2) % 4][:, (h % 2) * CH:(h % 2 + 1) * CH],
                                 start=j == 0, stop=j == NJ - 1, tile_position=(0, 32 * h))
            last.then_inc(pv_s, 1)

        pe.wait_ge(k.sem("q_rest"), 4 * HEADS * 16)
        with pe.Fori(0, NCH) as c:
            pe.wait_ge(norm_s, c + 1)
            for r in range(NR):
                h, i = r // 4, r % 4
                pe.wait_ge(mb_s, c * NR + (r + 1))
                for g in range(NCH):
                    last = pe.matmul(k.bank(g), qs[:, h, bass.ds(c * CH + 128 * i, 128)], ks[:, h, g * CH:(g + 1) * CH],
                                     start=True, stop=True)
                last.then_inc(row_mm, 1)
                pe.wait_ge(diag_s, c * NR + (r + 1))
                pe.matmul(k.bank(0, 128), k.ones[:, :], diag, start=True, stop=True).then_inc(spread_mm, 1)
            pe.wait_ge(mb_s, c * NR + (NR + 1))
            for j in range(NJ):
                for a in range(2):
                    p = 2 * j + a
                    pe.wait_ge(shift_s, c * NPAIR + (p + 1 if p >= 3 else 3))
                    for e in range(2):
                        h = 2 * a + e
                        last = pe.matmul(k.bank(2 * (p % 3) + e), ks[:, h, j * 128:(j + 1) * 128], qs[:, h, bass.ds(c * CH, CH)],
                                         start=True, stop=True)
                    last.then_inc(s_mm, 1)
                if j >= 1:
                    weigh(c, j - 1)
            weigh(c, NJ - 1)
            pe.wait_ge(acc_s, c * NPAIR + NPAIR)
            for h in range(HEADS):
                last = pe.matmul(k.ps[32 * h:32 * h + 32, LS * CH:(LS + 1) * CH], k.ones[:, 0:32],
                                 acc[h // 2][:, (h % 2) * CH:(h % 2 + 1) * CH], start=True, stop=True, tile_position=(0, 32 * h))
            last.then_inc(l_mm, 1)

    def scalar(act):
        with act.Fori(0, NCH) as c:
            for p in range(NPAIR):
                act.wait_ge(shift_s, c * NPAIR + (p + 1 + 3))
                act.activation(probs[p % 4], probs[p % 4], ACT.Exp, scale=SCALE / SPLIT ** 2).then_inc(exp_s, 1)

    def vector(dve):
        dve.sem_inc(mb_s, 1)
        dve.sem_inc(shift_s, 3)
        dve.sem_inc(pv_s, 2)
        dve.sem_inc(norm_s, 1)
        with dve.Fori(0, NCH) as c:
            for r in range(NR):
                h, i = r // 4, r % 4
                dve.wait_ge(row_mm, c * NR + (r + 1))
                dve.reduce_max(mcol, k.ps[:, :], axis=AX.X).then_inc(max_s, 1)
                dve.wait_ge(max_s, c * NR + (r + 1))
                dve.tensor_scalar(diag, k.ident[:, :], mcol, None, ALU.mult).then_inc(diag_s, 1)
                dve.wait_ge(spread_mm, c * NR + (r + 1))
                dve.tensor_copy(mb[:, h, 128 * i:128 * i + 128], k.bank(0, 128)).then_inc(mb_s, 1)
            dve.wait_ge(mb_s, c * NR + (NR + 1))

            def add(p):
                dve.wait_ge(exp_s, c * NPAIR + (p + 1))
                if p < 2:
                    dve.tensor_copy(acc[p], probs[p % 4]).then_inc(acc_s, 1)
                else:
                    dve.wait_ge(acc_s, c * NPAIR + (p - 1))
                    dve.tensor_tensor(acc[p % 2], acc[p % 2], probs[p % 4], ALU.add).then_inc(acc_s, 1)

            for p in range(NPAIR):
                a = p % 2
                dve.wait_ge(s_mm, c * NPAIR + (p + 1))
                dve.wait_ge(pv_s, c * NJ + (p // 2 + 1))
                if p >= 4:
                    dve.wait_ge(acc_s, c * NPAIR + (p - 3))
                dve.tensor_tensor(probs[p % 4].rearrange("p (e n) -> p e n", e=2),
                                  k.bank(2 * (p % 3), 2 * CH).rearrange("p (e n) -> p e n", e=2),
                                  mb[:, 2 * a:2 * a + 2, :], ALU.subtract).then_inc(shift_s, 1)
                if p >= 1:
                    add(p - 1)
            add(NPAIR - 1)
            dve.wait_ge(l_mm, c + 1)
            dve.reciprocal(rl, k.bank(LS)).then_inc(l_s, 1)
            dve.wait_ge(l_s, c + 1)
            dve.wait_ge(pv_s, c * NJ + (NJ + 2))
            dve.tensor_tensor(ao[:, bass.ds(c * CH, CH)], k.bank(O), rl, ALU.mult).then_inc(norm_s, 1)
            dve.wait_ge(norm_s, c + 2)

    return tensor, scalar, vector


def attention_out(k):
    nc = k.nc
    t1, ao, ot = k.at(T_AT, L), k.at(TNT_AT, L), k.at(0, L)
    o_mm, o_ev, t_mm, t_s = k.sem("outproj_mm"), k.sem("outproj_ready"), k.sem("tokens_tr"), k.sem("tokens_ready")
    with nc.Block() as block:
        @block.tensor
        def _(pe):
            for c in range(NCH):
                pe.matmul(k.bank(c), k.wout[:, :], ao[:, cols_of(c)], start=True, stop=True).then_inc(o_mm, 1)
            for g in range(NT // 4):
                pe.wait_ge(o_ev, g + 1)
                for i in range(4):
                    at = g * CH + 128 * i
                    last = pe.transpose(k.bank(g, 128, 128 * i), ot[:, at:at + 128], k.ident[:, :])
                last.then_inc(t_mm, 1)

        @block.scalar
        def _(act):
            for c in range(NCH):
                act.wait_ge(o_mm, c + 1)
                act.activation(ot[:, cols_of(c)], k.bank(c), ACT.Identity, bias=k.cols[:, C_BO:C_BO + 1]).then_inc(o_ev, 1)

        @block.vector
        def _(dve):
            for g in range(NT // 4):
                dve.wait_ge(t_mm, g + 1)
                dve.tensor_tensor(t1[:, g * CH:(g + 1) * CH], t1[:, g * CH:(g + 1) * CH], k.bank(g), ALU.add).then_inc(t_s, 1)
                dve.wait_ge(t_s, g + 1)
                tile_stats(k, dve, g, TN_AT, T_AT)
    k.clear()


def attention(k):
    guarded, bounded = attend_guarded(k), attend(k)
    with k.nc.Block() as block:
        @block.sync
        def _(sp):
            stack_heads(k, sp, QS_AT, QH_AT, QL_AT, (0, 1), CH, L, k.sem("q_rest"))
            sp.wait_ge(k.sem("q_rest"), 4 * HEADS * 16)

        @block.tensor
        def _(pe):
            need = pe.value_load(k.flag[0:1, 0:1], min_val=0, max_val=1)
            with pe.If(need == 1):
                guarded[0](pe)
            with pe.Else():
                bounded[0](pe)
            pe.drain()

        @block.scalar
        def _(act):
            need = act.value_load(k.flag[0:1, 0:1], min_val=0, max_val=1)
            with act.If(need == 1):
                guarded[1](act)
            with act.Else():
                bounded[1](act)
            act.drain()

        @block.vector
        def _(dve):
            need = dve.value_load(k.flag[0:1, 0:1], min_val=0, max_val=1)
            with dve.If(need == 1):
                guarded[2](dve)
            with dve.Else():
                bounded[2](dve)
            dve.drain()
    k.clear()
    attention_out(k)


def ffn(k, b):
    nc = k.nc
    t1, tn, tnt, img = k.at(T_AT, L), k.at(TN_AT, L), k.at(0, L), k.at(X1_AT, L)
    E0 = 8192
    names = ("ex", "c1", "oh1", "e2", "oh2", "gate", "tmp")
    small = {n: k.at(E0 + i * 256, NT * NE).rearrange("p (i e) -> p i e", e=NE) for i, n in enumerate(names)}
    gpad = k.at(E0 + 2048, NT * 32).rearrange("p (i e) -> p i e", e=32)
    gt = k.at(E0 + 3072, 1024)
    lt = k.at(E0 + 8448, 2 * CH)
    cols = k.at(E0 + 4096, 256)
    m1, m2, den = (cols[:, i * NT:(i + 1) * NT] for i in range(3))
    prod = [k.at(E0 + 4352 + i * 1024, NE * C).rearrange("p (e c) -> p e c", e=NE) for i in range(4)]
    tn_s, tr, tr_ev, lg, lc, ex_s = (k.sem(n) for n in ("ln_done", "tr_done", "tnt_ready", "logits_mm", "logits_ready", "exp_done"))
    gp, gz, gtm, gte, bmm, bad = (k.sem(n) for n in ("gates_ready", "gates_zero", "gates_tr", "gates_out", "bias_mm", "bias_added"))
    emm, ml, hs, ts, fm, fe, out_s = (k.sem(n) for n in (
        "experts_mm", "weighted", "halved", "tile_added", "final_tr", "final_out", "stored"))
    NG = NT // 4

    def spread(col):
        return col.unsqueeze(2).broadcast_to([128, NT, NE])

    with nc.Block() as block:
        @block.tensor
        def _(pe):
            for i in range(NT):
                pe.wait_ge(tn_s, i + 1)
                last = pe.transpose(k.ps[:, i * 128:(i + 1) * 128], tn[:, i * 128:(i + 1) * 128], k.ident[:, :])
                if i % 4 == 3:
                    last.then_inc(tr, 1)
            for a in range(2):
                pe.wait_ge(tr_ev, 4 * a + 4)
                for q in range(4):
                    last = pe.matmul(k.bank(a)[32 * q:32 * q + 32, :], k.routw[:, :], tnt[:, cols_of(4 * a + q)],
                                     start=True, stop=True, tile_position=(0, 32 * q))
                last.then_inc(k.sem("logits_t"), 1)
            for a in range(2):
                pe.wait_ge(k.sem("logits_kept"), a + 1)
                for i in range(4):
                    last = pe.transpose(k.bank(2 + a, 128, 128 * i), lt[:, a * CH + 128 * i:a * CH + 128 * i + 128], k.ident[:, :])
            last.then_inc(lg, 1)
            pe.wait_ge(gp, 1)
            for q in range(NT // 4):
                last = pe.transpose(k.bank(1 + q // 4, 128, 128 * (q % 4)), gpad[:, 4 * q:4 * q + 4, :].rearrange("p i e -> p (i e)"), k.ident[:, :])
            last.then_inc(gtm, 1)
            pe.wait_ge(gte, 1)
            for g in range(NG):
                for i in range(4):
                    last = pe.matmul(k.bank(g, 128, 128 * i), gt[:, g * 128:(g + 1) * 128], k.expb[:, i, :], start=True, stop=True)
                last.then_inc(bmm, 1)
            for i in range(NT):
                if i < 4:
                    pe.wait_ge(bad, NG)
                else:
                    pe.wait_ge(ml, i - 3)
                for hb in range(2):
                    last = pe.matmul(k.bank(2 * (i % 4) + hb), tnt[:, i * 128:(i + 1) * 128],
                                     k.expw[:, hb * 4:hb * 4 + 4, :].rearrange("p e c -> p (e c)"), start=True, stop=True)
                last.then_inc(emm, 1)
            for g in range(NG):
                pe.wait_ge(ml, NT)
                pe.wait_ge(ts, 2 * (4 * g + 4))
                for i in range(4 * g, 4 * g + 4):
                    last = pe.transpose(k.ps[:, i * 128:(i + 1) * 128], t1[:, i * 128:(i + 1) * 128], k.ident[:, :])
                last.then_inc(fm, 1)

        @block.scalar
        def _(act):
            normalize(k, None, act, TN_AT, T_AT, 1e-5)
            for g in range(NG):
                act.wait_ge(tr, g + 1)
                act.activation(tnt[:, g * CH:(g + 1) * CH], k.bank(g), ACT.Copy).then_inc(tr_ev, 1)
            for a in range(2):
                act.wait_ge(k.sem("logits_t"), a + 1)
                act.activation(lt[:, a * CH:(a + 1) * CH], k.bank(a), ACT.Copy).then_inc(k.sem("logits_kept"), 1)
            act.wait_ge(lc, 1)
            act.activation(small["ex"], small["tmp"], ACT.Exp).then_inc(ex_s, 1)
            act.wait_ge(gtm, 1)
            act.activation(gt, k.ps[:, CH:3 * CH], ACT.Copy).then_inc(gte, 1)
            for g in range(NG):
                act.wait_ge(fm, g + 1)
                act.activation(patch_order(img, g // PS, g % PS), k.bank(g).rearrange("p (x h w) -> p x h w", x=PS, w=W // PS), ACT.Copy).then_inc(fe, 1)

        @block.gpsimd
        def _(pool):
            pool.memset(gpad, 0.0).then_inc(gz, 1)
            for i in range(NT):
                pool.wait_ge(ml, i + 1)
                t = prod[i % 4]
                pool.tensor_tensor(t[:, 0:4, :], t[:, 0:4, :], t[:, 4:8, :], ALU.add).then_inc(hs, 1)
                pool.wait_ge(hs, 2 * i + 1)
                pool.tensor_tensor(t[:, 0:2, :], t[:, 0:2, :], t[:, 2:4, :], ALU.add).then_inc(hs, 1)

        @block.vector
        def _(dve):
            normalize(k, dve, None, TN_AT, T_AT, 1e-5)
            step = Chain(dve, k.sem("v_chain"))
            ex, c1, oh1, e2, oh2, gate, tmp = (small[n] for n in names)
            dve.wait_ge(lg, 1)
            for a in range(2):
                src = k.bank(2 + a).rearrange("p (j q e) -> p q j e", j=4, q=4)[:, :, :, 0:NE]
                dst = tmp[:, 16 * a:16 * a + 16, :].rearrange("p (q j) e -> p q j e", q=4)
                step(dve.tensor_copy(dst, src))
            step(dve.tensor_tensor(tmp, tmp, k.rtb[:, :].unsqueeze(1).broadcast_to([128, NT, NE]), ALU.add))
            step(dve.reduce_max(m1, tmp, axis=AX.X))
            dve.tensor_tensor(tmp, tmp, spread(m1), ALU.subtract).then_inc(lc, 1)
            dve.wait_ge(ex_s, 1)
            order = k.rank8[:, :].unsqueeze(1).broadcast_to([128, NT, NE])

            def first_max(src, top, onehot):
                step(dve.reduce_max(top, src, axis=AX.X))
                step(dve.tensor_tensor(c1, src, spread(top), ALU.is_equal))
                step(dve.tensor_tensor(c1, c1, order, ALU.mult))
                step(dve.reduce_max(den, c1, axis=AX.X))
                step(dve.tensor_tensor(onehot, c1, spread(den), ALU.is_equal))

            first_max(ex, m1, oh1)
            step(dve.scalar_tensor_tensor(e2, oh1, -4.0, ex, ALU.mult, ALU.add))
            first_max(e2, m2, oh2)
            step(dve.tensor_tensor(den, m1, m2, ALU.add))
            step(dve.reciprocal(den, den))
            step(dve.tensor_tensor(gate, oh1, oh2, ALU.add))
            step(dve.tensor_tensor(gate, gate, ex, ALU.mult))
            step(dve.tensor_tensor(gate, gate, spread(den), ALU.mult))
            dve.wait_ge(gz, 1)
            dve.tensor_copy(gpad[:, :, 0:NE], gate).then_inc(gp, 1)
            for g in range(NG):
                dve.wait_ge(bmm, g + 1)
                dve.tensor_tensor(t1[:, g * CH:(g + 1) * CH], t1[:, g * CH:(g + 1) * CH], k.bank(g), ALU.add).then_inc(bad, 1)

            def finish(i):
                dve.wait_ge(hs, 2 * i + 2)
                t = prod[i % 4]
                tile = t1[:, i * 128:(i + 1) * 128]
                dve.tensor_tensor(tile, tile, t[:, 0, :], ALU.add).then_inc(ts, 1)
                dve.wait_ge(ts, 2 * i + 1)
                dve.tensor_tensor(tile, tile, t[:, 1, :], ALU.add).then_inc(ts, 1)

            dve.wait_ge(bad, NG)
            for i in range(NT):
                dve.wait_ge(emm, i + 1)
                if i >= 4:
                    dve.wait_ge(ts, 2 * (i - 3))
                dve.tensor_tensor(prod[i % 4], k.bank(2 * (i % 4), 2 * CH).rearrange("p (e c) -> p e c", e=NE),
                                  gate[:, i, :].unsqueeze(2).broadcast_to([128, NE, C]), ALU.mult).then_inc(ml, 1)
                if i >= 3:
                    finish(i - 3)
            for i in range(NT - 3, NT):
                finish(i)

        @block.sync
        def _(sp):
            with sp.If(b < B - 1):
                k.load_x(sp, (b + 1) % B, k.sem("x_in"))
            sp.wait_ge(fe, NG // 2)
            sp.dma_start(k.out[b, :, 0:L // 2], img[:, 0:L // 2]).then_inc(out_s, 16)
            sp.wait_ge(fe, NG)
            sp.dma_start(k.out[b, :, L // 2:L], img[:, L // 2:L]).then_inc(out_s, 16)
    k.clear(but=1)


def program(nc, ins, out):
    with ExitStack() as ctx:
        k = Kernel(nc, ctx, ins, out)
        setup(k)
        with nc.Fori(0, B) as b:
            score_and_sort(k, b)
            project(k)
            scan(k)
            unsort(k, b)
            qkv(k)
            attention(k)
            ffn(k, b)
        with nc.Block() as block:
            @block.sync
            def _(sp):
                sp.wait_ge(k.sem("stored"), 32)


TRANSPOSED = {
    "in_projT": "L0_conv_in_proj_w", "out_projT": "L0_conv_out_proj_w", "x_projT": "L0_conv_x_proj_w",
    "dt_projT": "L0_conv_dt_proj_w", "ca1T": "L0_conv_ca1_w", "ca2T": "L0_conv_ca2_w",
}


def kernel(**inputs):
    import concourse.bacc as bacc
    from concourse.bass_utils import run_bass_kernel_spmd

    arrays = {n: np.ascontiguousarray(a) for n, a in inputs.items() if n not in TRANSPOSED.values()}
    arrays["x"] = arrays["x"].reshape(B, C, L)
    arrays["pe"] = arrays.pop("L0_conv_pe")
    for name, source in TRANSPOSED.items():
        arrays[name] = np.ascontiguousarray(np.asarray(inputs[source]).T)
    nc = bacc.Bacc("TRN2", target_bir_lowering=False, num_devices=1)
    ins = {n: nc.dram_tensor(n, a.shape, mybir.dt.from_np(a.dtype), kind="ExternalInput").ap() for n, a in arrays.items()}
    out = nc.dram_tensor("out", (B, C, L), F32, kind="ExternalOutput").ap()
    program(nc, ins, out)
    r = run_bass_kernel_spmd(nc, [arrays], core_ids=[0])
    return r.results[0]["out"].reshape(B, C, H, W)
```
